# Optimizing a Trainium2 kernel written in Bass

```python
import numpy as np
import jax
import jax.numpy as jnp

def _softmax(x, axis=-1):
    return jax.nn.softmax(x, axis=axis)

def _gelu(x):
    return jax.nn.gelu(x, approximate=True)

def _silu(x):
    return jax.nn.silu(x)

def _sigmoid(x):
    return jax.nn.sigmoid(x)

def _layernorm(x, axis=-1, eps=1e-05):
    m = jnp.mean(x, axis=axis, keepdims=True)
    v = jnp.var(x, axis=axis, keepdims=True)
    return (x - m) / jnp.sqrt(v + eps)

def _scatter_add(tgt, idx, src, axis=0):
    return tgt.at[idx].add(src)

def _segment_sum(src, seg, n):
    return jax.ops.segment_sum(src, seg, n)
kernel_name = 'mk_adaln_d2_jaxref_r4_7f5164'

def setup_inputs(seed: int=0):
    np.random.seed(seed)
    _w = jnp.asarray

    def _L0_attn_setup():
        import jax, jax.numpy as jnp
        import numpy as np
        DIM = 256
        HIDDEN = 512
        QK_DIM = 512
        LN_EPS = 1e-05
        key = jax.random.key(seed)
        ks = jax.random.split(key, 10)
        B, N = (4, 1024)
        s = 0.02
        return {'x': jax.random.normal(ks[0], (B, N, DIM), dtype=jnp.float32), 'ln_g': jnp.ones((DIM,), jnp.float32), 'ln_b': jnp.zeros((DIM,), jnp.float32), 'W_hidden': jax.random.normal(ks[1], (DIM, HIDDEN * 2), jnp.float32) * s, 'b_hidden': jnp.zeros((HIDDEN * 2,), jnp.float32), 'W_qk': jax.random.normal(ks[2], (DIM, QK_DIM), jnp.float32) * s, 'b_qk': jnp.zeros((QK_DIM,), jnp.float32), 'os_gamma': jax.random.normal(ks[3], (2, QK_DIM), jnp.float32) * s, 'os_beta': jnp.zeros((2, QK_DIM), jnp.float32), 'W_out': jax.random.normal(ks[4], (HIDDEN, DIM), jnp.float32) * s, 'b_out': jnp.zeros((DIM,), jnp.float32)}
    _L0_attn_in = _L0_attn_setup()

    def _L0_ffn_setup():
        import jax, jax.numpy as jnp
        import numpy as np
        D_MODEL = 256
        H_SHARED = 512
        H_ROUTED = 256
        N_EXPERTS = 8
        TOP_K = 2
        key = jax.random.key(seed)
        ks = jax.random.split(key, 8)
        B, T = (2, 512)
        sc_d = 1.0 / np.sqrt(D_MODEL)
        sc_hs = 1.0 / np.sqrt(H_SHARED)
        sc_hr = 1.0 / np.sqrt(H_ROUTED)
        return {'x': jax.random.normal(ks[0], (B, T, D_MODEL), dtype=jnp.float32), 'router_w': jax.random.normal(ks[1], (N_EXPERTS, D_MODEL), dtype=jnp.float32) * sc_d, 'router_bias': jnp.zeros((N_EXPERTS,), dtype=jnp.float32), 'sw1': jax.random.normal(ks[2], (D_MODEL, H_SHARED), dtype=jnp.float32) * sc_d, 'sw3': jax.random.normal(ks[3], (D_MODEL, H_SHARED), dtype=jnp.float32) * sc_d, 'sw2': jax.random.normal(ks[4], (H_SHARED, D_MODEL), dtype=jnp.float32) * sc_hs, 'ew1': jax.random.normal(ks[5], (N_EXPERTS, D_MODEL, H_ROUTED), dtype=jnp.float32) * sc_d, 'ew2': jax.random.normal(ks[6], (N_EXPERTS, H_ROUTED, D_MODEL), dtype=jnp.float32) * sc_hr}
    _L0_ffn_in = _L0_ffn_setup()
    _L0_c = _w((lambda *s: np.random.randn(*s).astype(np.float32) * 0.05)(8, 256))
    _L0_wmod = _w((lambda *s: np.random.randn(*s).astype(np.float32) * 0.05)(256, 6 * 256) * 256 ** (-0.5))

    def _L1_attn_setup():
        import jax, jax.numpy as jnp
        import numpy as np
        B, S, H = (1, 512, 256)
        INTER, K, DST, DTR = (512, 4, 16, 64)

        def _ssm(dA, dBu, C):
            xs = (jnp.moveaxis(dA, 1, 0), jnp.moveaxis(dBu, 1, 0), jnp.moveaxis(C, 1, 0))
            state0 = jnp.zeros(dA.shape[:1] + dA.shape[2:], dA.dtype)

            def step(state, inp):
                Ai, dBui, Ci = inp
                state = Ai * state + dBui
                y = jnp.einsum('bhd,bd->bh', state, Ci)
                return (state, y)
            _, ys = jax.lax.scan(step, state0, xs)
            return jnp.moveaxis(ys, 0, 1)
        key = jax.random.key(seed)
        ks = jax.random.split(key, 10)
        sc = 0.02
        return {'x': jax.random.normal(ks[0], (B, S, H), jnp.float32), 'W_in': jax.random.normal(ks[1], (H, 2 * INTER), jnp.float32) * sc, 'conv_w': jax.random.normal(ks[2], (K, 1, INTER), jnp.float32) * sc, 'conv_b': jax.random.normal(ks[3], (INTER,), jnp.float32) * sc, 'W_x': jax.random.normal(ks[4], (INTER, DTR + 2 * DST), jnp.float32) * sc, 'W_dt': jax.random.normal(ks[5], (DTR, INTER), jnp.float32) * sc, 'b_dt': jax.random.normal(ks[6], (INTER,), jnp.float32) * sc, 'A_log': jax.random.normal(ks[7], (INTER, DST), jnp.float32) * sc, 'D': jax.random.normal(ks[8], (INTER,), jnp.float32) * sc, 'W_out': jax.random.normal(ks[9], (INTER, H), jnp.float32) * sc}
    _L1_attn_in = _L1_attn_setup()

    def _L1_ffn_setup():
        import jax, jax.numpy as jnp
        import numpy as np
        D_IN, D_HID = (256, 1024)

        def _ternary(key, shape):
            return jax.random.randint(key, shape, -1, 2).astype(jnp.float32)

        def _tlin(x, w, s):
            return jnp.einsum('bsi,oi->bso', x, w) * s
        key = jax.random.key(seed)
        ks = jax.random.split(key, 12)
        inv = lambda fan: 1.0 / np.sqrt(fan).astype(np.float32)
        return {'x': jax.random.normal(ks[0], (4, 512, D_IN), dtype=jnp.float32), 'w1_w': _ternary(ks[1], (D_HID, D_IN)), 'w1_s': jax.random.uniform(ks[2], (D_HID,), dtype=jnp.float32) * inv(D_IN), 'w2_w': _ternary(ks[3], (D_HID, D_IN)), 'w2_s': jax.random.uniform(ks[4], (D_HID,), dtype=jnp.float32) * inv(D_IN), 'h1_w': _ternary(ks[5], (D_HID, D_HID)), 'h1_s': jax.random.uniform(ks[6], (D_HID,), dtype=jnp.float32) * inv(D_HID), 'h2_w': _ternary(ks[7], (D_HID, D_HID)), 'h2_s': jax.random.uniform(ks[8], (D_HID,), dtype=jnp.float32) * inv(D_HID), 'w3_w': _ternary(ks[9], (D_IN, D_HID)), 'w3_s': jax.random.uniform(ks[10], (D_IN,), dtype=jnp.float32) * inv(D_HID)}
    _L1_ffn_in = _L1_ffn_setup()
    _L1_c = _w((lambda *s: np.random.randn(*s).astype(np.float32) * 0.05)(8, 256))
    _L1_wmod = _w((lambda *s: np.random.randn(*s).astype(np.float32) * 0.05)(256, 6 * 256) * 256 ** (-0.5))
    _d = {'L0_attn_x': _L0_attn_in['x'], 'L0_attn_ln_g': _L0_attn_in['ln_g'], 'L0_attn_ln_b': _L0_attn_in['ln_b'], 'L0_attn_W_hidden': _L0_attn_in['W_hidden'], 'L0_attn_b_hidden': _L0_attn_in['b_hidden'], 'L0_attn_W_qk': _L0_attn_in['W_qk'], 'L0_attn_b_qk': _L0_attn_in['b_qk'], 'L0_attn_os_gamma': _L0_attn_in['os_gamma'], 'L0_attn_os_beta': _L0_attn_in['os_beta'], 'L0_attn_W_out': _L0_attn_in['W_out'], 'L0_attn_b_out': _L0_attn_in['b_out'], 'L0_ffn_router_w': _L0_ffn_in['router_w'], 'L0_ffn_router_bias': _L0_ffn_in['router_bias'], 'L0_ffn_sw1': _L0_ffn_in['sw1'], 'L0_ffn_sw3': _L0_ffn_in['sw3'], 'L0_ffn_sw2': _L0_ffn_in['sw2'], 'L0_ffn_ew1': _L0_ffn_in['ew1'], 'L0_ffn_ew2': _L0_ffn_in['ew2'], 'L0_c': _L0_c, 'L0_wmod': _L0_wmod, 'L1_attn_W_in': _L1_attn_in['W_in'], 'L1_attn_conv_w': _L1_attn_in['conv_w'], 'L1_attn_conv_b': _L1_attn_in['conv_b'], 'L1_attn_W_x': _L1_attn_in['W_x'], 'L1_attn_W_dt': _L1_attn_in['W_dt'], 'L1_attn_b_dt': _L1_attn_in['b_dt'], 'L1_attn_A_log': _L1_attn_in['A_log'], 'L1_attn_D': _L1_attn_in['D'], 'L1_attn_W_out': _L1_attn_in['W_out'], 'L1_ffn_w1_w': _L1_ffn_in['w1_w'], 'L1_ffn_w1_s': _L1_ffn_in['w1_s'], 'L1_ffn_w2_w': _L1_ffn_in['w2_w'], 'L1_ffn_w2_s': _L1_ffn_in['w2_s'], 'L1_ffn_h1_w': _L1_ffn_in['h1_w'], 'L1_ffn_h1_s': _L1_ffn_in['h1_s'], 'L1_ffn_h2_w': _L1_ffn_in['h2_w'], 'L1_ffn_h2_s': _L1_ffn_in['h2_s'], 'L1_ffn_w3_w': _L1_ffn_in['w3_w'], 'L1_ffn_w3_s': _L1_ffn_in['w3_s'], 'L1_c': _L1_c, 'L1_wmod': _L1_wmod}
    _x0 = _d['L0_attn_x']
    _d['L0_attn_x'] = jax.random.normal(jax.random.fold_in(jax.random.key(seed), 1), (8, 512, 256), dtype=_x0.dtype)
    del _x0
    return _d

def reference(L0_attn_x, L0_attn_ln_g, L0_attn_ln_b, L0_attn_W_hidden, L0_attn_b_hidden, L0_attn_W_qk, L0_attn_b_qk, L0_attn_os_gamma, L0_attn_os_beta, L0_attn_W_out, L0_attn_b_out, L0_ffn_router_w, L0_ffn_router_bias, L0_ffn_sw1, L0_ffn_sw3, L0_ffn_sw2, L0_ffn_ew1, L0_ffn_ew2, L0_c, L0_wmod, L1_attn_W_in, L1_attn_conv_w, L1_attn_conv_b, L1_attn_W_x, L1_attn_W_dt, L1_attn_b_dt, L1_attn_A_log, L1_attn_D, L1_attn_W_out, L1_ffn_w1_w, L1_ffn_w1_s, L1_ffn_w2_w, L1_ffn_w2_s, L1_ffn_h1_w, L1_ffn_h1_s, L1_ffn_h2_w, L1_ffn_h2_s, L1_ffn_w3_w, L1_ffn_w3_s, L1_c, L1_wmod):

    def _L0_attn_ref(x, ln_g, ln_b, W_hidden, b_hidden, W_qk, b_qk, os_gamma, os_beta, W_out, b_out):
        import jax, jax.numpy as jnp
        import numpy as np
        DIM = 256
        HIDDEN = 512
        QK_DIM = 512
        LN_EPS = 1e-05
        seq_len = x.shape[-2]
        mu = jnp.mean(x, axis=-1, keepdims=True)
        var = jnp.mean(jnp.square(x - mu), axis=-1, keepdims=True)
        normed = (x - mu) * jax.lax.rsqrt(var + LN_EPS) * ln_g + ln_b
        h = jax.nn.silu(normed @ W_hidden + b_hidden)
        v, gate = (h[..., :HIDDEN], h[..., HIDDEN:])
        qk = jax.nn.silu(normed @ W_qk + b_qk)
        q = qk * os_gamma[0] + os_beta[0]
        k = qk * os_gamma[1] + os_beta[1]
        sim = jnp.einsum('bid,biD->bdD', q, k) / seq_len
        attn = jax.nn.softmax(sim, axis=-1)
        out = v * jnp.sum(attn, axis=-1)[:, None, :]
        out = out * gate
        out = out @ W_out + b_out
        return out + x

    def _L0_ffn_ref(x, router_w, router_bias, sw1, sw3, sw2, ew1, ew2):
        import jax, jax.numpy as jnp
        import numpy as np
        D_MODEL = 256
        H_SHARED = 512
        H_ROUTED = 256
        N_EXPERTS = 8
        TOP_K = 2
        B, T, C = x.shape
        xf = x.reshape(-1, C)
        shared_out = jax.nn.silu(xf @ sw1) * (xf @ sw3) @ sw2
        s = jax.nn.sigmoid((xf @ router_w.T).astype(jnp.float32))
        sel_scores = s + router_bias.astype(jnp.float32)
        _, topk_idx = jax.lax.top_k(sel_scores, TOP_K)
        s_sel = jnp.take_along_axis(s, topk_idx, axis=1)
        denom = s_sel.sum(axis=1, keepdims=True)
        gates = jnp.where(denom > 1e-09, s_sel / (denom + 1e-09), 1.0 / TOP_K).astype(x.dtype)
        one_hot = jax.nn.one_hot(topk_idx, N_EXPERTS, dtype=x.dtype)
        comb = jnp.einsum('nke,nk->ne', one_hot, gates)
        h = jax.nn.gelu(jnp.einsum('nd,edh->neh', xf, ew1), approximate=False)
        y = jnp.einsum('neh,ehd->ned', h, ew2)
        routed_out = jnp.einsum('ned,ne->nd', y, comb)
        return (shared_out + routed_out).reshape(B, T, C)

    def _L1_attn_ref(x, W_in, conv_w, conv_b, W_x, W_dt, b_dt, A_log, D, W_out):
        import jax, jax.numpy as jnp
        import numpy as np
        B, S, H = (1, 512, 256)
        INTER, K, DST, DTR = (512, 4, 16, 64)

        def _ssm(dA, dBu, C):
            xs = (jnp.moveaxis(dA, 1, 0), jnp.moveaxis(dBu, 1, 0), jnp.moveaxis(C, 1, 0))
            state0 = jnp.zeros(dA.shape[:1] + dA.shape[2:], dA.dtype)

            def step(state, inp):
                Ai, dBui, Ci = inp
                state = Ai * state + dBui
                y = jnp.einsum('bhd,bd->bh', state, Ci)
                return (state, y)
            _, ys = jax.lax.scan(step, state0, xs)
            return jnp.moveaxis(ys, 0, 1)
        proj = x @ W_in
        raw, gate = jnp.split(proj, 2, axis=-1)
        conv = jax.lax.conv_general_dilated(raw, conv_w, window_strides=(1,), padding=[(K - 1, 0)], dimension_numbers=('NWC', 'WIO', 'NWC'), feature_group_count=INTER)
        h = jax.nn.silu(conv + conv_b)
        ssm_p = h @ W_x
        ts, Bmat, C = jnp.split(ssm_p, [DTR, DTR + DST], axis=-1)
        dt = jax.nn.softplus(ts @ W_dt + b_dt)
        A = -jnp.exp(A_log)
        dA = jnp.exp(dt[..., None] * A)
        dBu = dt[..., None] * Bmat[:, :, None, :] * h[..., None]
        y = _ssm(dA, dBu, C)
        y = y + h * D
        y = y * jax.nn.silu(gate)
        return y @ W_out

    def _L1_ffn_ref(x, w1_w, w1_s, w2_w, w2_s, h1_w, h1_s, h2_w, h2_s, w3_w, w3_s):
        import jax, jax.numpy as jnp
        import numpy as np
        D_IN, D_HID = (256, 1024)

        def _ternary(key, shape):
            return jax.random.randint(key, shape, -1, 2).astype(jnp.float32)

        def _tlin(x, w, s):
            return jnp.einsum('bsi,oi->bso', x, w) * s
        h = jax.nn.silu(_tlin(x, w1_w, w1_s)) * _tlin(x, w2_w, w2_s)
        h = jax.nn.gelu(_tlin(h, h1_w, h1_s), approximate=False)
        h = jax.nn.gelu(_tlin(h, h2_w, h2_s), approximate=False)
        return _tlin(h, w3_w, w3_s)
    x = L0_attn_x
    mod = (_silu(L0_c) @ L0_wmod).reshape(L0_c.shape[0], 6, 1, -1)
    sa, ca, ga, sb, cb, gb = (mod[:, 0], mod[:, 1], mod[:, 2], mod[:, 3], mod[:, 4], mod[:, 5])
    ga = (2 * (ga >= 0) - 1) * jnp.maximum(jnp.abs(ga), 0.25)
    gb = (2 * (gb >= 0) - 1) * jnp.maximum(jnp.abs(gb), 0.25)
    h = _layernorm(x, axis=-1) * (1 + ca) + sa
    x = x + ga * _L0_attn_ref(h, L0_attn_ln_g, L0_attn_ln_b, L0_attn_W_hidden, L0_attn_b_hidden, L0_attn_W_qk, L0_attn_b_qk, L0_attn_os_gamma, L0_attn_os_beta, L0_attn_W_out, L0_attn_b_out)
    h = _layernorm(x, axis=-1) * (1 + cb) + sb
    x = x + gb * _L0_ffn_ref(h, L0_ffn_router_w, L0_ffn_router_bias, L0_ffn_sw1, L0_ffn_sw3, L0_ffn_sw2, L0_ffn_ew1, L0_ffn_ew2)
    mod = (_silu(L1_c) @ L1_wmod).reshape(L1_c.shape[0], 6, 1, -1)
    sa, ca, ga, sb, cb, gb = (mod[:, 0], mod[:, 1], mod[:, 2], mod[:, 3], mod[:, 4], mod[:, 5])
    ga = (2 * (ga >= 0) - 1) * jnp.maximum(jnp.abs(ga), 0.25)
    gb = (2 * (gb >= 0) - 1) * jnp.maximum(jnp.abs(gb), 0.25)
    h = _layernorm(x, axis=-1) * (1 + ca) + sa
    x = x + ga * _L1_attn_ref(h, L1_attn_W_in, L1_attn_conv_w, L1_attn_conv_b, L1_attn_W_x, L1_attn_W_dt, L1_attn_b_dt, L1_attn_A_log, L1_attn_D, L1_attn_W_out)
    h = _layernorm(x, axis=-1) * (1 + cb) + sb
    x = x + gb * _L1_ffn_ref(h, L1_ffn_w1_w, L1_ffn_w1_s, L1_ffn_w2_w, L1_ffn_w2_s, L1_ffn_h1_w, L1_ffn_h1_s, L1_ffn_h2_w, L1_ffn_h2_s, L1_ffn_w3_w, L1_ffn_w3_s)
    return x

_drawn_inputs = setup_inputs


def setup_inputs(seed=0):
    import zlib

    import numpy as np

    out = dict(_drawn_inputs(seed))
    spreads = {'L0_attn_ln_g': (1.0, 0.2),
     'L0_attn_ln_b': (0.0, 0.1),
     'L0_attn_b_hidden': (0.0, 0.1),
     'L0_attn_b_qk': (0.0, 0.1),
     'L0_attn_os_beta': (0.0, 0.1),
     'L0_attn_b_out': (0.0, 0.1),
     'L0_ffn_router_bias': (0.0, 0.1)}
    factors = {}
    for name, (base, spread) in spreads.items():
        noise = np.random.default_rng([zlib.crc32(name.encode()), seed]).standard_normal(out[name].shape)
        drawn = base * np.exp(spread * noise) if base else spread * noise
        out[name] = jnp.asarray(drawn.astype(out[name].dtype))
    for name, factor in factors.items():
        out[name] = (out[name] * factor).astype(out[name].dtype)
    return out
```

```python
from contextlib import ExitStack

import concourse.bass as bass
from concourse import mybir

F32 = mybir.dt.float32
F32R = mybir.dt.float32r
U32 = mybir.dt.uint32
ALU = mybir.AluOpType
ACT = mybir.ActivationFunctionType
AX = mybir.AxisListType

P = 128


class Lane:

    def __init__(self, nc, name, engine, sem):
        self.nc, self.name, self.e, self.sem = nc, name, engine, sem
        self.restart()

    def restart(self):
        self.count, self.seen = 0, {}

    def done(self, instruction):
        instruction.then_inc(self.sem, 1)
        self.count += 1
        return (self.sem, self.count)

    def wait(self, *events):
        for event in events:
            if event is None:
                continue
            sem, value = event
            if self.seen.get(sem.name, 0) < value:
                self.e.wait_ge(sem, value)
                self.seen[sem.name] = value


class Load:

    def __init__(self, sem):
        self.sem = sem
        self.restart()

    def restart(self):
        self.count = 0

    def start(self, lane, out, in_):
        lane.e.dma_start(out, in_).then_inc(self.sem, 16)
        self.count += 16
        return (self.sem, self.count)


class Bank:

    def __init__(self, tensor):
        self.t, self.free = tensor, None


class Ring:
    def __init__(self, banks):
        self.banks, self.at = banks, 0

    def take(self):
        bank = self.banks[self.at % len(self.banks)]
        self.at += 1
        return bank


def adaln_kernel(nc, ins, out):
    B, S, D = ins["L0_attn_x"].shape
    TT = S // P
    KD = D // P
    HID = ins["L0_attn_W_hidden"].shape[1] // 2
    KH = HID // P
    HS = ins["L0_ffn_sw1"].shape[1]
    KS = HS // P
    E, _, HR = ins["L0_ffn_ew1"].shape
    KR = HR // P
    INTER = ins["L1_attn_W_in"].shape[1] // 2
    KI = INTER // P
    NST = ins["L1_attn_A_log"].shape[1]
    DTR = ins["L1_attn_W_dt"].shape[0]
    KC = ins["L1_attn_conv_w"].shape[1]
    DH = ins["w1_T"].shape[1]
    KF = DH // P
    EPS = 1e-5
    NMOD = 6
    SA, CA, GA, SB_, CB, GB = range(NMOD)

    mod_dram = nc.dram_tensor("mod_rows", (2, B, NMOD * D), F32, kind="Internal").ap()
    x_mid = nc.dram_tensor("x_after_layer0", (B, S, D), F32, kind="Internal").ap()
    x_ssm = nc.dram_tensor("x_after_ssm", (B, S, D), F32, kind="Internal").ap()

    def token_tiles(dram):
        return dram.rearrange("b (t p) d -> b p t d", p=P)

    x_in_v, x_mid_v, x_ssm_v, out_v = map(token_tiles, (ins["L0_attn_x"], x_mid, x_ssm, out))

    with ExitStack() as top:
        sem = lambda name: top.enter_context(nc.semaphore(name))
        PE = Lane(nc, "pe", nc.tensor, sem("pe_done"))
        ACTE = Lane(nc, "act", nc.scalar, sem("act_done"))
        DVE = Lane(nc, "dve", nc.vector, sem("dve_done"))
        POOL = Lane(nc, "pool", nc.gpsimd, sem("pool_done"))
        SP = Lane(nc, "sp", nc.sync, sem("sp_done"))
        lanes = (PE, ACTE, DVE, POOL, SP)
        loads = [Load(sem(f"load{i}")) for i in range(24)]
        stores = Load(sem("stores"))
        sems = [lane.sem for lane in lanes] + [q.sem for q in loads] + [stores.sem]
        next_load = [0]

        def load(out_, in_, lane=None):
            q = loads[next_load[0] % len(loads)]
            next_load[0] += 1
            return q.start(lane or SP, out_, in_)

        def join():
            SP.wait((stores.sem, stores.count)) if stores.count else None
            for q in loads:
                if q.count:
                    SP.wait((q.sem, q.count))
            nc.all_engine_barrier()
            for s in sems:
                nc.sync.sem_clear(s)
            nc.all_engine_barrier()
            for lane in lanes:
                lane.restart()
            for q in loads + [stores]:
                q.restart()
            next_load[0] = 0
            for bank in banks:
                bank.free = None

        banks = [Bank(top.enter_context(nc.psum_tensor(f"bank{i}", [P, 512], F32))) for i in range(4)]
        wide = [Bank(top.enter_context(nc.psum_tensor(f"wide{i}", [P, 1024], F32))) for i in range(2)]
        banks_all = banks + wide
        banks, narrow = banks_all, banks[:4]
        ring = Ring(narrow)

        def sb_in(stack):
            return lambda name, shape, dt=F32: stack.enter_context(nc.sbuf_tensor(name, shape, dt))

        keep = sb_in(top)

        ident = keep("ident", [P, P])
        minus_half = keep("minus_half", [P, TT])
        mod_col = [keep(f"mod_col{l}", [P, NMOD * KD, B]) for l in range(2)]
        cur_col = keep("cur_col", [P, NMOD * KD])
        stat6 = keep("stat6", [P, TT, 6])
        stat = keep("stat", [P, TT, 2])
        veps = keep("veps", [P, TT])
        rstd = keep("rstd", [P, TT])

        def col(which, k):
            return cur_col[:, which * KD + k:which * KD + k + 1]

        def layernorm(x, xhat, x_ready, xhat_free=None):
            DVE.wait(x_ready)
            for t in range(TT):
                s6 = DVE.done(nc.vector.bn_stats(stat6[:, t, :], x[:, t, :]))
            DVE.wait(s6)
            for t in range(TT):
                s2 = DVE.done(nc.vector.bn_aggr(stat[:, t, :], stat6[:, t, :]))
            DVE.wait(s2)
            v = DVE.done(nc.vector.tensor_scalar(veps[:, :], stat[:, :, 1], EPS, None, ALU.add))
            POOL.wait(v)
            r = POOL.done(nc.gpsimd.tensor_tensor(rstd[:, :], veps[:, :], minus_half[:, :], ALU.pow))
            DVE.wait(r, xhat_free)
            for t in range(TT):
                done = DVE.done(nc.vector.tensor_scalar(xhat[:, t, :], x[:, t, :], stat[:, t, 0:1],
                                                        rstd[:, t:t + 1], ALU.subtract, ALU.mult))
            return done

        def transposed(src, k, src_ready):
            bank = ring.take()
            PE.wait(src_ready, bank.free)
            for t in range(TT):
                ins_ = nc.tensor.transpose(bank.t[:, t * P:(t + 1) * P], src[:, t, k * P:(k + 1) * P],
                                           ident[:, :])
            return bank, PE.done(ins_)

        def split(full, hi, lo, ready, free=None, lo_lane=None):
            DVE.wait(ready, free)
            h = DVE.done(nc.vector.tensor_copy(hi, full))
            lane = lo_lane or DVE
            lane.wait(ready, h, free)
            l = lane.done(lane.e.tensor_tensor(lo, full, hi.bitcast(F32), ALU.subtract))
            return (h, l)

        def modulated_T(src, src_ready, scale, bias, full, hi, lo, free=None):
            parts = []
            for k in range(KD):
                bank, turned = transposed(src, k, src_ready)
                ACTE.wait(turned, free)
                m = ACTE.done(nc.scalar.activation(full[:, k, :], bank.t[:, :], ACT.Identity,
                                                   bias=bias(k), scale=scale(k)))
                bank.free = m
                parts.append((m,) + split(full[:, k, :], hi[:, k, :], lo[:, k, :], m, free))
            return parts

        def product3(out_, lhs, rhs, nk, ready, first=True, last=True, skip=False):
            for k in range(nk):
                PE.wait(*ready(k))
                (lh, ll), (rh, rl) = lhs(k), rhs(k)
                for n, (a, b) in enumerate(((lh, rh), (lh, rl), (ll, rh))):
                    i = nc.tensor.matmul(out_, a, b, start=(first and k == 0 and n == 0),
                                         stop=(last and k == nk - 1 and n == 2), skip_group_check=skip)
            return i

        def weights_split(stage_buf, name, hi, lo, src, width, before):
            step = stage_buf.shape[2]
            done = None
            for n, c in enumerate(range(0, width, step)):
                w = min(step, width - c)
                slot = stage_buf[:, n % 2, 0:w]
                SP.wait(before[n % 2])
                got = load(slot, src[:, c:c + w])
                h, l = split(slot, hi[:, c:c + w], lo[:, c:c + w], got)
                before[n % 2] = l
                done = l
            return done

        def row(vector):
            return vector.partition_broadcast(P)

        z = POOL.done(nc.gpsimd.memset(ident[:, :], 0.0))
        POOL.wait(z)
        ident_ready = POOL.done(nc.gpsimd.affine_select(
            out=ident[:, :], in_=ident[:, :], compare_op=ALU.not_equal, fill=1.0, base=0,
            pattern=[[-1, P]], channel_multiplier=1))
        POOL.done(nc.gpsimd.memset(minus_half[:, :], -0.5))

        with ExitStack() as stack:
            sb = sb_in(stack)
            c_tok = sb("c_tok", [B, 2, D])
            c_act = sb("c_act", [B, 2, D])
            cT = sb("cT", [P, 2, KD, B])
            wmod = sb("wmod", [P, 2, KD, NMOD * D])
            rows = sb("rows", [B, 2, NMOD * D])
            sgn = sb("sgn", [B, 2, D])
            mag = sb("mag", [B, 2, D])
            got = []
            for l in range(2):
                got.append(load(c_tok[:, l, :], ins[f"L{l}_c"]))
                got.append(load(wmod[:, l, :, :], ins[f"L{l}_wmod"].rearrange("(k p) n -> p k n", p=P)))
            ACTE.wait(*got)
            silu_c = ACTE.done(nc.scalar.activation(c_act[:, :, :], c_tok[:, :, :], ACT.Silu))
            PE.wait(ident_ready, silu_c)
            b0 = ring.take()
            for l in range(2):
                for k in range(KD):
                    at = (l * KD + k) * B
                    i = nc.tensor.transpose(b0.t[:, at:at + B], c_act[:, l, k * P:(k + 1) * P], ident[0:B, 0:B])
            turned = PE.done(i)
            DVE.wait(turned)
            cT_ready = DVE.done(nc.vector.tensor_copy(
                cT[:, :, :, :], b0.t[:, 0:2 * KD * B].rearrange("p (l k b) -> p l k b", l=2, k=KD)))
            b0.free = cT_ready
            PE.wait(cT_ready, *got)
            row_parts = []
            for l in range(2):
                for c in range(0, NMOD * D, 512):
                    bank = ring.take()
                    PE.wait(bank.free)
                    for k in range(KD):
                        i = nc.tensor.matmul(bank.t[0:B, :], cT[:, l, k, :], wmod[:, l, k, c:c + 512],
                                             start=(k == 0), stop=(k == KD - 1))
                    made = PE.done(i)
                    DVE.wait(made)
                    copied = DVE.done(nc.vector.tensor_copy(rows[:, l, c:c + 512], bank.t[0:B, :]))
                    bank.free = copied
            DVE.wait(copied)
            for l in range(2):
                for which in (CA, CB):
                    r = rows[:, l, which * D:(which + 1) * D]
                    last = DVE.done(nc.vector.tensor_scalar(r, r, 1.0, None, ALU.add))
            for which in (GA, GB):
                r = rows[:, :, which * D:(which + 1) * D]
                DVE.wait(last)
                a = DVE.done(nc.vector.tensor_scalar(sgn[:, :, :], r, 0.0, 2.0, ALU.is_ge, ALU.mult))
                b = DVE.done(nc.vector.tensor_scalar(mag[:, :, :], r, -1.0, None, ALU.mult))
                DVE.wait(b)
                c = DVE.done(nc.vector.tensor_tensor(mag[:, :, :], mag[:, :, :], r, ALU.max))
                DVE.wait(c)
                d = DVE.done(nc.vector.tensor_scalar(mag[:, :, :], mag[:, :, :], 0.25, None, ALU.max))
                e = DVE.done(nc.vector.tensor_scalar(sgn[:, :, :], sgn[:, :, :], -1.0, None, ALU.add))
                DVE.wait(d, e)
                last = DVE.done(nc.vector.tensor_tensor(r, sgn[:, :, :], mag[:, :, :], ALU.mult))
            PE.wait(last)
            for l in range(2):
                bank = ring.take()
                PE.wait(bank.free)
                for j in range(NMOD * KD):
                    i = nc.tensor.transpose(bank.t[:, j * B:(j + 1) * B], rows[:, l, j * P:(j + 1) * P],
                                            ident[0:B, 0:B])
                turned = PE.done(i)
                DVE.wait(turned)
                bank.free = DVE.done(nc.vector.tensor_copy(
                    mod_col[l][:, :, :], bank.t[:, 0:NMOD * KD * B].rearrange("p (j b) -> p j b", b=B)))
            SP.wait(last)
            for l in range(2):
                stores.start(SP, mod_dram[l], rows[:, l, :])
            join()

        with ExitStack() as stack:
            sb = sb_in(stack)
            w_hid = [sb(f"w_hid{h}", [P, KD * 2 * HID], F32R) for h in "HL"]
            w_qk = [sb(f"w_qk{h}", [P, KD * HID], F32R) for h in "HL"]
            w_s1 = [sb(f"w_s1{h}", [P, KD * HS], F32R) for h in "HL"]
            w_s3 = [sb(f"w_s3{h}", [P, KD * HS], F32R) for h in "HL"]
            w_e1 = [sb(f"w_e1{h}", [P, E * KD * HR], F32R) for h in "HL"]
            w_o = sb("w_o", [P, KH, D])
            w_s2 = sb("w_s2", [P, KS, D])
            w_e2 = sb("w_e2", [P, E, KR, D])
            w_router = sb("w_router", [P, KD, E])
            lnc = sb("lnc", [P, 2, KD])
            b_hid = sb("b_hid", [P, 2 * KH])
            osr = sb("osr", [P, 2, 2, HID])
            bqk_row = sb("bqk_row", [P, HID])
            bout_row = sb("bout_row", [P, D])
            rbias_row = sb("rbias_row", [P, E])
            iota_e = sb("iota_e", [P, E])
            with ExitStack() as st2:
                stage_buf = sb_in(st2)("stage1", [P, 2, 2048])
                before = [None, None]
                kt = lambda w: w.rearrange("(k p) n -> p k n", p=P)
                for name, parts in (("L0_attn_W_hidden", w_hid), ("L0_attn_W_qk", w_qk),
                                    ("L0_ffn_sw1", w_s1), ("L0_ffn_sw3", w_s3)):
                    src = kt(ins[name])
                    n = src.shape[2]
                    for k in range(KD):
                        weights_split(stage_buf, name, parts[0][:, k * n:(k + 1) * n],
                                      parts[1][:, k * n:(k + 1) * n], src[:, k, :], n, before)
                for e in range(E):
                    src = kt(ins["L0_ffn_ew1"][e])
                    for k in range(KD):
                        at = (e * KD + k) * HR
                        weights_split(stage_buf, "ew1", w_e1[0][:, at:at + HR], w_e1[1][:, at:at + HR],
                                      src[:, k, :], HR, before)
                load(w_o[:, :, :], kt(ins["L0_attn_W_out"]))
                load(w_s2[:, :, :], kt(ins["L0_ffn_sw2"]))
                for e in range(E):
                    load(w_e2[:, e, :, :], kt(ins["L0_ffn_ew2"][e]))
                load(w_router[:, :, :], ins["router_T"].rearrange("(k p) e -> p k e", p=P))
                load(lnc[:, 0, :], ins["L0_attn_ln_g"])
                load(lnc[:, 1, :], ins["L0_attn_ln_b"])
                load(b_hid[:, :], ins["L0_attn_b_hidden"])
                for which in range(2):
                    load(osr[:, which, 0, :], row(ins["L0_attn_os_gamma"][which]))
                    load(osr[:, which, 1, :], row(ins["L0_attn_os_beta"][which]))
                load(bqk_row[:, :], row(ins["L0_attn_b_qk"]))
                load(bout_row[:, :], row(ins["L0_attn_b_out"]))
                load(rbias_row[:, :], row(ins["L0_ffn_router_bias"]))
                POOL.done(nc.gpsimd.iota(iota_e[:, :], pattern=[[1, E]], base=0, channel_multiplier=0,
                                         allow_small_or_imprecise_dtypes=True))
                join()

            xres = sb("xres", [P, TT, D])
            h_tok = sb("h_tok", [P, TT, D])
            xhat = sb("xhat", [P, TT, D])
            nT = sb("nT", [P, KD, S])
            nTH = sb("nTH", [P, KD, S], F32R)
            nTL = sb("nTL", [P, KD, S], F32R)
            q_tok = sb("q_tok", [P, TT, HID])
            k_tok = sb("k_tok", [P, TT, HID])
            v_T = q_tok
            g_T = k_tok
            qk_tmp = sb("qk_tmp", [P, 2, HID])
            smax = sb("smax", [P, KH])
            esum = sb("esum", [P, KH])
            rsum = sb("rsum", [P, KH])
            attn_sum = sb("attn_sum", [P, KH])
            rows0 = sb("rows0", [P, NMOD, D])
            s1_act = sb("s1_act", [P, 2, S])
            s_act = sb("s_act", [P, KS, S])
            e_act = sb("e_act", [P, 2 * KR, S])
            rt = sb("rt", [P, 12, TT, E])
            rt_idx = sb("rt_idx", [P, TT, 8], U32)
            rt_small = sb("rt_small", [P, 4, TT])

            def wk(parts, n, k, c, w=P):
                return parts[0][:, k * n + c:k * n + c + w], parts[1][:, k * n + c:k * n + c + w]

            def layer0(b):
                x_got = load(xres[:, :, :], x_in_v[b])
                rows_got = load(rows0[:, :, :], mod_dram[0, b].rearrange("(j d) -> j d", j=NMOD).partition_broadcast(P))
                cols = DVE.done(nc.vector.tensor_copy(cur_col[:, :], mod_col[0][:, :, b]))
                rb = lambda which: rows0[:, which:which + 1, :].broadcast_to([P, TT, D])
                n1 = layernorm(xres, xhat, x_got)
                DVE.wait(n1, rows_got)
                m1 = DVE.done(nc.vector.tensor_tensor(h_tok[:, :, :], xhat[:, :, :], rb(CA), ALU.mult))
                DVE.wait(m1)
                h_ready = DVE.done(nc.vector.tensor_tensor(h_tok[:, :, :], h_tok[:, :, :], rb(SA_ := SA), ALU.add))
                n2 = layernorm(h_tok, xhat, h_ready, m1)
                parts = modulated_T(xhat, n2, lambda k: lnc[:, 0, k:k + 1], lambda k: lnc[:, 1, k:k + 1],
                                    nT, nTH, nTL)
                nparts = lambda k: parts[k]
                prev = [None, None]
                for t in range(TT):
                    bank = ring.take()
                    PE.wait(bank.free)
                    made = PE.done(product3(
                        bank.t[:, :], lambda k: (nTH[:, k, t * P:(t + 1) * P], nTL[:, k, t * P:(t + 1) * P]),
                        lambda k: wk(w_qk, HID, k, 0, HID), KD, nparts))
                    tmp = qk_tmp[:, t % 2, :]
                    DVE.wait(made, prev[t % 2])
                    biased = DVE.done(nc.vector.tensor_tensor(tmp, bank.t[:, :], bqk_row[:, :], ALU.add))
                    bank.free = biased
                    ACTE.wait(biased)
                    act = ACTE.done(nc.scalar.activation(tmp, tmp, ACT.Silu))
                    DVE.wait(act)
                    qm = DVE.done(nc.vector.tensor_tensor(q_tok[:, t, :], tmp, osr[:, 0, 0, :], ALU.mult))
                    km = DVE.done(nc.vector.tensor_tensor(k_tok[:, t, :], tmp, osr[:, 1, 0, :], ALU.mult))
                    DVE.wait(km)
                    qa = DVE.done(nc.vector.tensor_tensor(q_tok[:, t, :], q_tok[:, t, :], osr[:, 0, 1, :], ALU.add))
                    ka = DVE.done(nc.vector.tensor_tensor(k_tok[:, t, :], k_tok[:, t, :], osr[:, 1, 1, :], ALU.add))
                    prev[t % 2] = km
                PE.wait(ka)
                for d in range(KH):
                    bank = ring.take()
                    PE.wait(bank.free)
                    for t in range(TT):
                        i = nc.tensor.matmul(bank.t[:, :], q_tok[:, t, d * P:(d + 1) * P], k_tok[:, t, :],
                                             start=(t == 0), stop=(t == TT - 1))
                    made = PE.done(i)
                    DVE.wait(made)
                    mx = DVE.done(nc.vector.tensor_reduce(smax[:, d:d + 1], bank.t[:, :], AX.X, ALU.max))
                    DVE.wait(mx)
                    neg = DVE.done(nc.vector.tensor_scalar(smax[:, d:d + 1], smax[:, d:d + 1], -1.0 / S, None, ALU.mult))
                    ACTE.wait(neg, made)
                    ex = ACTE.done(nc.scalar.activation(s_act[:, d % KS, :], bank.t[:, :], ACT.Exp, bias=smax[:, d:d + 1],
                                                        scale=1.0 / S, accum_out=esum[:, d:d + 1]))
                    bank.free = ex
                sim_done = made
                DVE.wait(ex)
                rc = DVE.done(nc.vector.reciprocal(rsum[:, :], esum[:, :]))
                DVE.wait(rc)
                asum = DVE.done(nc.vector.tensor_tensor(attn_sum[:, :], esum[:, :], rsum[:, :], ALU.mult))
                gated = []
                ACTE.wait(sim_done)
                for d in range(KH):
                    evs = []
                    for half, dst in ((0, v_T), (1, g_T)):
                        bank = ring.take()
                        PE.wait(bank.free)
                        made = PE.done(product3(
                            bank.t[:, :], lambda k: wk(w_hid, 2 * HID, k, half * HID + d * P),
                            lambda k: (nTH[:, k, :], nTL[:, k, :]), KD, nparts))
                        ACTE.wait(made)
                        j = half * KH + d
                        ev = ACTE.done(nc.scalar.activation(dst[:, d, :], bank.t[:, :], ACT.Silu, bias=b_hid[:, j:j + 1]))
                        bank.free = ev
                        evs.append(ev)
                    DVE.wait(asum, *evs)
                    gated.append(DVE.done(nc.vector.scalar_tensor_tensor(
                        out=v_T[:, d, :], in0=v_T[:, d, :], scalar=attn_sum[:, d:d + 1], in1=g_T[:, d, :],
                        op0=ALU.mult, op1=ALU.mult)))
                DVE.wait(h_ready)
                i1 = DVE.done(nc.vector.tensor_tensor(h_tok[:, :, :], h_tok[:, :, :],
                                                      bout_row[:, None, :].broadcast_to([P, TT, D]), ALU.add))
                acc = wide[0]
                PE.wait(acc.free)
                for t in range(TT):
                    for k in range(KH):
                        PE.wait(gated[k])
                        i = nc.tensor.matmul(acc.t[:, t * D:(t + 1) * D], v_T[:, k, t * P:(t + 1) * P], w_o[:, k, :],
                                             start=(k == 0), stop=(k == KH - 1))
                made = PE.done(i)
                accv = acc.t[:, :].rearrange("p (t d) -> p t d", t=TT)
                DVE.wait(made, i1)
                i2 = DVE.done(nc.vector.tensor_tensor(h_tok[:, :, :], h_tok[:, :, :], accv, ALU.add))
                acc.free = i2
                DVE.wait(i2)
                i3 = DVE.done(nc.vector.tensor_tensor(h_tok[:, :, :], h_tok[:, :, :], rb(GA), ALU.mult))
                DVE.wait(i3)
                x1 = DVE.done(nc.vector.tensor_tensor(xres[:, :, :], xres[:, :, :], h_tok[:, :, :], ALU.add))
                n3 = layernorm(xres, xhat, x1)
                DVE.wait(cols)
                ACTE.wait(cols, made)
                parts2 = modulated_T(xhat, n3, lambda k: col(CB, k), lambda k: col(SB_, k), nT, nTH, nTL, made)
                rb_ = ring.take()
                PE.wait(rb_.free, parts2[0][0], parts2[1][0])
                for t in range(TT):
                    for k in range(KD):
                        i = nc.tensor.matmul(rb_.t[:, t * E:(t + 1) * E], nT[:, k, t * P:(t + 1) * P], w_router[:, k, :],
                                             start=(k == 0), stop=(k == KD - 1))
                made = PE.done(i)
                ACTE.wait(made)
                sg, sel, e8, oh1, oh2, msk, scored, comb, tmpr = (rt[:, j, :, :] for j in range(9))
                sig = ACTE.done(nc.scalar.activation(sg, rb_.t[:, 0:TT * E].rearrange("p (t e) -> p t e", t=TT), ACT.Sigmoid))
                rb_.free = sig
                DVE.wait(sig)
                a = DVE.done(nc.vector.tensor_tensor(sel, sg, rbias_row[:, None, :].broadcast_to([P, TT, E]), ALU.add))
                DVE.wait(a)
                for t in range(TT):
                    a = DVE.done(nc.vector.max(rt[:, 2, t, :], rt[:, 1, t, :]))
                DVE.wait(a)
                for t in range(TT):
                    a = DVE.done(nc.vector.max_index(rt_idx[:, t, :], rt[:, 2, t, :], rt[:, 1, t, :]))
                DVE.wait(a)
                a = DVE.done(nc.vector.tensor_copy(tmpr, rt_idx[:, :, :]))
                DVE.wait(a)
                iob = iota_e[:, None, :].broadcast_to([P, TT, E])
                a1 = DVE.done(nc.vector.tensor_tensor(oh1, rt[:, 8, :, 0:1].broadcast_to([P, TT, E]), iob, ALU.is_equal))
                a2 = DVE.done(nc.vector.tensor_tensor(oh2, rt[:, 8, :, 1:2].broadcast_to([P, TT, E]), iob, ALU.is_equal))
                DVE.wait(a2)
                a = DVE.done(nc.vector.tensor_tensor(msk, oh1, oh2, ALU.add))
                DVE.wait(a)
                a = DVE.done(nc.vector.tensor_tensor(scored, msk, sg, ALU.mult))
                DVE.wait(a)
                den, ok, rden, half_ = (rt_small[:, j, :] for j in range(4))
                a = DVE.done(nc.vector.tensor_reduce(den, scored, AX.X, ALU.add))
                DVE.wait(a)
                a1 = DVE.done(nc.vector.tensor_scalar(ok, den, 1e-9, None, ALU.is_gt))
                a2 = DVE.done(nc.vector.tensor_scalar(half_, den, 1e-9, 0.5, ALU.is_le, ALU.mult))
                a3 = DVE.done(nc.vector.tensor_scalar(den, den, 1e-9, None, ALU.add))
                DVE.wait(a3)
                a = DVE.done(nc.vector.reciprocal(rden, den))
                DVE.wait(a)
                a = DVE.done(nc.vector.tensor_tensor(rden, rden, ok, ALU.mult))
                DVE.wait(a)
                bc = lambda j: rt_small[:, j, :, None].broadcast_to([P, TT, E])
                a1 = DVE.done(nc.vector.tensor_tensor(scored, scored, bc(2), ALU.mult))
                a2 = DVE.done(nc.vector.tensor_tensor(msk, msk, bc(3), ALU.mult))
                DVE.wait(a2)
                comb_ready = DVE.done(nc.vector.tensor_tensor(comb, scored, msk, ALU.add))
                f2 = lambda k: parts2[k]
                s_parts = []
                prev = [None, None]
                for m in range(KS):
                    b1, b3 = ring.take(), None
                    PE.wait(b1.free)
                    m1_ = PE.done(product3(b1.t[:, :], lambda k: wk(w_s1, HS, k, m * P),
                                           lambda k: (nTH[:, k, :], nTL[:, k, :]), KD, f2))
                    ACTE.wait(m1_, prev[m % 2])
                    a1 = ACTE.done(nc.scalar.activation(s1_act[:, m % 2, :], b1.t[:, :], ACT.Silu))
                    b1.free = a1
                    b3 = ring.take()
                    PE.wait(b3.free)
                    m3_ = PE.done(product3(b3.t[:, :], lambda k: wk(w_s3, HS, k, m * P),
                                           lambda k: (nTH[:, k, :], nTL[:, k, :]), KD, f2))
                    DVE.wait(m3_, a1, ex)
                    a3 = DVE.done(nc.vector.tensor_tensor(s_act[:, m, :], b3.t[:, :], s1_act[:, m % 2, :], ALU.mult))
                    b3.free = a3
                    prev[m % 2] = a3
                    s_parts.append(a3)
                slot_free = [None] * 2
                combined = [comb_ready] * TT
                eparts = {}

                def expert_up(e):
                    evs = []
                    for m in range(KR):
                        bank = ring.take()
                        PE.wait(bank.free)
                        md = PE.done(product3(bank.t[:, :], lambda k: wk(w_e1, HR, e * KD + k, m * P),
                                              lambda k: (nTH[:, k, :], nTL[:, k, :]), KD, f2))
                        ACTE.wait(md, slot_free[e % 2])
                        ev = ACTE.done(nc.scalar.activation(e_act[:, (e % 2) * KR + m, :], bank.t[:, :], ACT.Gelu))
                        bank.free = ev
                        evs.append(ev)
                    eparts[e] = evs

                expert_up(0)
                acc = wide[1]
                PE.wait(acc.free)
                for t in range(TT):
                    for k in range(KS):
                        PE.wait(s_parts[k])
                        i = nc.tensor.matmul(acc.t[:, t * D:(t + 1) * D], s_act[:, k, t * P:(t + 1) * P], w_s2[:, k, :],
                                             start=(k == 0), stop=(k == KS - 1))
                made = PE.done(i)
                DVE.wait(made, i3)
                shared = DVE.done(nc.vector.tensor_copy(h_tok[:, :, :], acc.t[:, :].rearrange("p (t d) -> p t d", t=TT)))
                acc.free = shared
                combined = [shared] * TT
                for e in range(E):
                    if e + 1 < E:
                        expert_up(e + 1)
                    acc = wide[e % 2]
                    PE.wait(acc.free, *eparts[e])
                    for t in range(TT):
                        for k in range(KR):
                            i = nc.tensor.matmul(acc.t[:, t * D:(t + 1) * D], e_act[:, (e % 2) * KR + k, t * P:(t + 1) * P],
                                                 w_e2[:, e, k, :], start=(k == 0), stop=(k == KR - 1))
                    made = PE.done(i)
                    slot_free[e % 2] = made
                    DVE.wait(made, comb_ready)
                    for t in range(TT):
                        DVE.wait(combined[t])
                        combined[t] = DVE.done(nc.vector.scalar_tensor_tensor(
                            out=h_tok[:, t, :], in0=acc.t[:, t * D:(t + 1) * D], scalar=rt[:, 7, t, e:e + 1],
                            in1=h_tok[:, t, :], op0=ALU.mult, op1=ALU.add))
                    acc.free = combined[TT - 1]
                DVE.wait(combined[TT - 1])
                a = DVE.done(nc.vector.tensor_tensor(h_tok[:, :, :], h_tok[:, :, :], rb(GB), ALU.mult))
                DVE.wait(a)
                x2 = DVE.done(nc.vector.tensor_tensor(xres[:, :, :], xres[:, :, :], h_tok[:, :, :], ALU.add))
                SP.wait(x2)
                stores.start(SP, x_mid_v[b], xres[:, :, :])

            with nc.Fori(0, B) as b:
                layer0(b)
                join()

        with ExitStack() as stack:
            sb = sb_in(stack)
            w_in = [sb(f"w_in{h}", [P, KD * 2 * INTER], F32R) for h in "HL"]
            w_x = sb("w_x", [P, KI, DTR])
            w_bc = sb("w_bc", [P, KI, 2, 2 * NST])
            w_dt = sb("w_dt", [DTR, INTER])
            w_out = sb("w_out", [P, KI, D])
            conv_w = sb("conv_w", [P, KC, KI])
            conv_b = sb("conv_b", [P, KI])
            b_dt = sb("b_dt", [P, KI])
            d_skip = sb("d_skip", [P, KI])
            a_neg = sb("a_neg", [P, KI, NST])
            pick = sb("pick", [4 * NST, 2 * NST, P], F32R)
            pick_f = sb("pick_f", [4 * NST, 2 * NST])
            with ExitStack() as st2:
                stage_buf = sb_in(st2)("stage2", [P, 2, 1024])
                before = [None, None]
                src = kt(ins["L1_attn_W_in"])
                for k in range(KD):
                    n = 2 * INTER
                    weights_split(stage_buf, "w_in", w_in[0][:, k * n:(k + 1) * n], w_in[1][:, k * n:(k + 1) * n],
                                  src[:, k, :], n, before)
                wx = kt(ins["L1_attn_W_x"])
                load(w_x[:, :, :], wx[:, :, 0:DTR])
                for twice in range(2):
                    load(w_bc[:, :, twice, :], wx[:, :, DTR:DTR + 2 * NST])
                load(w_dt[:, :], ins["L1_attn_W_dt"])
                load(w_out[:, :, :], kt(ins["L1_attn_W_out"]))
                load(conv_w[:, :, :], ins["L1_attn_conv_w"])
                load(conv_b[:, :], ins["L1_attn_conv_b"])
                load(b_dt[:, :], ins["L1_attn_b_dt"])
                load(d_skip[:, :], ins["L1_attn_D"])
                al = load(a_neg[:, :, :], ins["L1_attn_A_log"].rearrange("(k p) n -> p k n", p=P))
                ACTE.wait(al)
                ex = ACTE.done(nc.scalar.activation(a_neg[:, :, :], a_neg[:, :, :], ACT.Exp))
                DVE.wait(ex)
                DVE.done(nc.vector.tensor_scalar(a_neg[:, :, :], a_neg[:, :, :], -1.0, None, ALU.mult))
                zz = POOL.done(nc.gpsimd.memset(pick_f[:, :], 0.0))
                for shift in (0, 2 * NST):
                    POOL.wait(zz)
                    zz = POOL.done(nc.gpsimd.affine_select(
                        out=pick_f[:, :], in_=pick_f[:, :], compare_op=ALU.not_equal, fill=1.0, base=-shift,
                        pattern=[[-1, 2 * NST]], channel_multiplier=1))
                DVE.wait(zz)
                DVE.done(nc.vector.tensor_copy(pick[:, :, :], pick_f[:, :, None].broadcast_to([4 * NST, 2 * NST, P])))
                join()

            xres = sb("xres2", [P, TT, D])
            xhat = sb("xhat2", [P, TT, D])
            hT = sb("hT2", [P, KD, S])
            hTH = sb("hTH2", [P, KD, S], F32R)
            hTL = sb("hTL2", [P, KD, S], F32R)
            rows1 = sb("rows1", [P, NMOD, D])
            PAD = KC - 1
            raw = sb("raw", [P, KI, PAD + S])
            cv = sb("cv", [P, 2, S])
            hcv = sb("hcv", [P, KI, S])
            gate = sb("gate", [P, KI, S])
            ts = sb("ts", [DTR, S])
            bc_full = sb("bc_full", [4 * NST, S])
            bc_parts = sb("bc_parts", [4 * NST, S], F32R)
            sp_t = sb("sp_t", [P, 2, 2, S])
            dt = sb("dt", [P, KI, S])
            u = sb("u", [P, KI, S])
            y = sb("y", [P, KI, S])
            HC = KI // 2
            bcb = sb("bcb", [P, 2, 2, S])
            dA = sb("dA", [P, 2, HC, S])
            st = sb("st", [P, 3, HC, S])
            fills = [POOL.done(nc.gpsimd.memset(raw[:, :, 0:PAD], 0.0)),
                     POOL.done(nc.gpsimd.memset(dA[:, :, :, 0:1], 0.0))]
            join()

            def ssm(b):
                x_got = load(xres[:, :, :], x_mid_v[b])
                rows_got = load(rows1[:, :, :], mod_dram[1, b].rearrange("(j d) -> j d", j=NMOD).partition_broadcast(P))
                cols = DVE.done(nc.vector.tensor_copy(cur_col[:, :], mod_col[1][:, :, b]))
                n1 = layernorm(xres, xhat, x_got)
                ACTE.wait(cols)
                parts = modulated_T(xhat, n1, lambda k: col(CA, k), lambda k: col(SA, k), hT, hTH, hTL)
                hp = lambda k: parts[k]
                conv_done, cv_free = [], [None, None]
                for c in range(KI):
                    bank = ring.take()
                    PE.wait(bank.free)
                    md = PE.done(product3(bank.t[:, :], lambda k: wk2(w_in, 2 * INTER, k, c * P),
                                          lambda k: (hTH[:, k, :], hTL[:, k, :]), KD, hp))
                    ACTE.wait(md)
                    rw = ACTE.done(nc.scalar.activation(raw[:, c, PAD:], bank.t[:, :], ACT.Copy))
                    bank.free = rw
                    DVE.wait(rw, cv_free[c % 2])
                    o = cv[:, c % 2, :]
                    a = DVE.done(nc.vector.tensor_scalar(o, raw[:, c, 0:S], conv_w[:, 0, c:c + 1], None, ALU.mult))
                    for tap in range(1, KC):
                        DVE.wait(a)
                        a = DVE.done(nc.vector.scalar_tensor_tensor(
                            out=o, in0=raw[:, c, tap:tap + S], scalar=conv_w[:, tap, c:c + 1], in1=o,
                            op0=ALU.mult, op1=ALU.add))
                    ACTE.wait(a)
                    hv = ACTE.done(nc.scalar.activation(hcv[:, c, :], o, ACT.Silu, bias=conv_b[:, c:c + 1]))
                    cv_free[c % 2] = hv
                    conv_done.append(hv)
                for c in range(KI):
                    bank = ring.take()
                    PE.wait(bank.free)
                    md = PE.done(product3(bank.t[:, :], lambda k: wk2(w_in, 2 * INTER, k, INTER + c * P),
                                          lambda k: (hTH[:, k, :], hTL[:, k, :]), KD, hp))
                    ACTE.wait(md)
                    gate_ready = ACTE.done(nc.scalar.activation(gate[:, c, :], bank.t[:, :], ACT.Silu))
                    bank.free = gate_ready
                bank = ring.take()
                PE.wait(bank.free)
                for k in range(KI):
                    PE.wait(conv_done[k])
                    i = nc.tensor.matmul(bank.t[0:DTR, :], w_x[:, k, :], hcv[:, k, :], start=(k == 0), stop=(k == KI - 1))
                md = PE.done(i)
                bank2 = ring.take()
                PE.wait(bank2.free)
                for k in range(KI):
                    i = nc.tensor.matmul(bank2.t[0:4 * NST, :], w_bc[:, k, :, :].rearrange("p a n -> p (a n)"),
                                         hcv[:, k, :], start=(k == 0), stop=(k == KI - 1))
                md2 = PE.done(i)
                DVE.wait(md)
                ts_ready = DVE.done(nc.vector.tensor_copy(ts[:, :], bank.t[0:DTR, :]))
                bank.free = ts_ready
                DVE.wait(md2)
                f = DVE.done(nc.vector.tensor_copy(bc_full[:, :], bank2.t[0:4 * NST, :]))
                bank2.free = f
                DVE.wait(f)
                p1 = DVE.done(nc.vector.tensor_copy(bc_parts[:, :], bc_full[:, :]))
                DVE.wait(p1)
                low = slice(2 * NST, 4 * NST)
                bc_ready = DVE.done(nc.vector.tensor_tensor(bc_parts[low, :], bc_full[low, :],
                                                            bc_parts[low, :].bitcast(F32), ALU.subtract))
                sp_free = [None, None]
                u_ready = []
                for c in range(KI):
                    bank = ring.take()
                    PE.wait(bank.free, ts_ready)
                    md = PE.done(nc.tensor.matmul(bank.t[:, :], w_dt[:, c * P:(c + 1) * P], ts[:, :], start=True, stop=True))
                    ab, mx = sp_t[:, c % 2, 0, :], sp_t[:, c % 2, 1, :]
                    ACTE.wait(md, sp_free[c % 2])
                    s1 = ACTE.done(nc.scalar.activation(ab, bank.t[:, :], ACT.Abs, bias=b_dt[:, c:c + 1]))
                    DVE.wait(s1, sp_free[c % 2])
                    s2 = DVE.done(nc.vector.tensor_scalar(mx, bank.t[:, :], b_dt[:, c:c + 1], 0.0, ALU.add, ALU.max))
                    bank.free = s2
                    ACTE.wait(s1)
                    s3 = ACTE.done(nc.scalar.activation(ab, ab, ACT.Exp, scale=-1.0))
                    ACTE.wait(s3)
                    s4 = ACTE.done(nc.scalar.activation(ab, ab, ACT.Ln, bias=1.0))
                    DVE.wait(s4, s2)
                    s5 = DVE.done(nc.vector.tensor_tensor(dt[:, c, :], ab, mx, ALU.add))
                    sp_free[c % 2] = s5
                    DVE.wait(s5)
                    u_ready.append(DVE.done(nc.vector.tensor_tensor(u[:, c, :], dt[:, c, :], hcv[:, c, :], ALU.mult)))
                DVE.wait(conv_done[-1])
                for c in range(KI):
                    y_ready = DVE.done(nc.vector.tensor_scalar(y[:, c, :], hcv[:, c, :], d_skip[:, c:c + 1], None, ALU.mult))
                b_free, c_free = [None, None], [None, None]
                dA_free, st_free = [None, None], [None, None, None]
                y_acc = [y_ready, y_ready]
                step = 0
                for n in range(NST):
                    bc_ev = []
                    for which, free in ((0, b_free), (1, c_free)):
                        bank = ring.take()
                        PE.wait(bank.free, bc_ready)
                        md = PE.done(nc.tensor.matmul(bank.t[:, :], pick[:, which * NST + n, :], bc_parts[:, :],
                                                      start=True, stop=True))
                        ACTE.wait(md, free[n % 2])
                        ev = ACTE.done(nc.scalar.activation(bcb[:, n % 2, which, :], bank.t[:, :], ACT.Copy))
                        bank.free = ev
                        bc_ev.append(ev)
                    for half in range(KI // HC):
                        dslot, sslot = step % 2, step % 3
                        ACTE.wait(dA_free[dslot], u_ready[-1])
                        for j in range(HC):
                            c = half * HC + j
                            ex = ACTE.done(nc.scalar.activation(dA[:, dslot, j, 1:], dt[:, c, 1:], ACT.Exp,
                                                                scale=a_neg[:, c, n:n + 1]))
                        sv = st[:, sslot, :, :]
                        flat = lambda a: a.rearrange("p j s -> p (j s)")
                        spread = lambda which: bcb[:, n % 2, which:which + 1, :].broadcast_to([P, HC, S])
                        DVE.wait(bc_ev[0], bc_ev[1], st_free[sslot], u_ready[-1])
                        bu = DVE.done(nc.vector.tensor_tensor(sv, u[:, half * HC:(half + 1) * HC, :], spread(0), ALU.mult))
                        b_free[n % 2] = bu
                        DVE.wait(bu, ex)
                        sc = DVE.done(nc.vector.tensor_tensor_scan(flat(sv), flat(dA[:, dslot, :, :]), flat(sv), 0.0,
                                                                   ALU.mult, ALU.add))
                        dA_free[dslot] = sc
                        DVE.wait(sc)
                        pr = DVE.done(nc.vector.tensor_tensor(sv, sv, spread(1), ALU.mult))
                        c_free[n % 2] = pr
                        POOL.wait(pr, y_acc[half])
                        yv = y[:, half * HC:(half + 1) * HC, :]
                        y_acc[half] = POOL.done(nc.gpsimd.tensor_tensor(yv, yv, sv, ALU.add))
                        st_free[sslot] = y_acc[half]
                        step += 1
                DVE.wait(*y_acc, gate_ready)
                for c in range(KI):
                    yg = DVE.done(nc.vector.tensor_tensor(y[:, c, :], y[:, c, :], gate[:, c, :], ALU.mult))
                acc = wide[0]
                PE.wait(acc.free, yg)
                for t in range(TT):
                    for k in range(KI):
                        i = nc.tensor.matmul(acc.t[:, t * D:(t + 1) * D], y[:, k, t * P:(t + 1) * P], w_out[:, k, :],
                                             start=(k == 0), stop=(k == KI - 1))
                md = PE.done(i)
                DVE.wait(md, rows_got, parts[-1][0])
                a = DVE.done(nc.vector.tensor_tensor(xhat[:, :, :], acc.t[:, :].rearrange("p (t d) -> p t d", t=TT),
                                                     rows1[:, GA:GA + 1, :].broadcast_to([P, TT, D]), ALU.mult))
                acc.free = a
                DVE.wait(a)
                a = DVE.done(nc.vector.tensor_tensor(xres[:, :, :], xres[:, :, :], xhat[:, :, :], ALU.add))
                SP.wait(a)
                stores.start(SP, x_ssm_v[b], xres[:, :, :])

            wk2 = lambda parts, n, k, c: (parts[0][:, k * n + c:k * n + c + P], parts[1][:, k * n + c:k * n + c + P])
            with nc.Fori(0, B) as b:
                ssm(b)
                join()

        with ExitStack() as stack:
            sb = sb_in(stack)
            w1 = sb("w1", [P, KD, DH], F32R)
            w2 = sb("w2", [P, KD, DH], F32R)
            h1 = sb("h1", [P, KF, DH], F32R)
            h2 = sb("h2", [P, KF, DH], F32R)
            w3 = sb("w3", [P, KF, D])
            sc_in = sb("sc_in", [P, 4, KF])
            s3_row = sb("s3_row", [P, D])
            with ExitStack() as st2:
                stage_buf = sb_in(st2)("stage3", [P, 2, 1024])
                free = [None, None]
                j = 0
                for name, dst, nk in (("w1_T", w1, KD), ("w2_T", w2, KD), ("h1_T", h1, KF), ("h2_T", h2, KF)):
                    src = kt(ins[name])
                    for k in range(nk):
                        SP.wait(free[j % 2])
                        got = load(stage_buf[:, j % 2, :], src[:, k, :])
                        DVE.wait(got)
                        free[j % 2] = DVE.done(nc.vector.tensor_copy(dst[:, k, :], stage_buf[:, j % 2, :]))
                        j += 1
                load(w3[:, :, :], kt(ins["w3_T"]))
                for j, name in enumerate(("w1_s", "w2_s", "h1_s", "h2_s")):
                    load(sc_in[:, j, :], ins[f"L1_ffn_{name}"])
                load(s3_row[:, :], row(ins["L1_ffn_w3_s"]))
                join()
            xres = sb("xres3", [P, TT, D])
            xhat = sb("xhat3", [P, TT, D])
            hT = sb("hT3", [P, KD, S])
            hTH = sb("hTH3", [P, KD, S], F32R)
            hTL = sb("hTL3", [P, KD, S], F32R)
            rows2 = sb("rows2", [P, NMOD, D])
            f_act = sb("f_act", [P, KF, S])
            f_H = [sb(f"f_H{i}", [P, KF, S], F32R) for i in range(2)]
            f_L = [sb(f"f_L{i}", [P, KF, S], F32R) for i in range(2)]
            s_tmp = sb("s_tmp", [P, 2, S])

            def mlp(b):
                x_got = load(xres[:, :, :], x_ssm_v[b])
                rows_got = load(rows2[:, :, :], mod_dram[1, b].rearrange("(j d) -> j d", j=NMOD).partition_broadcast(P))
                cols = DVE.done(nc.vector.tensor_copy(cur_col[:, :], mod_col[1][:, :, b]))
                n1 = layernorm(xres, xhat, x_got)
                ACTE.wait(cols)
                parts = modulated_T(xhat, n1, lambda k: col(CB, k), lambda k: col(SB_, k), hT, hTH, hTL)

                def ternary(bank, w, m, hi, lo, nk, ready):
                    PE.wait(bank.free)
                    for k in range(nk):
                        PE.wait(*ready[k])
                        for n, a in enumerate((hi, lo)):
                            i = nc.tensor.matmul(bank.t[:, :], w[:, k, m * P:(m + 1) * P], a[:, k, :],
                                                 start=(k == 0 and n == 0), stop=(k == nk - 1 and n == 1))
                    return PE.done(i)

                free = [None, None]
                act1 = []
                for m in range(KF):
                    b1 = ring.take()
                    md = ternary(b1, w1, m, hTH, hTL, KD, parts)
                    ACTE.wait(md, free[m % 2])
                    a1 = ACTE.done(nc.scalar.activation(s_tmp[:, m % 2, :], b1.t[:, :], ACT.Silu, scale=sc_in[:, 0, m:m + 1]))
                    b1.free = a1
                    b2 = ring.take()
                    md = ternary(b2, w2, m, hTH, hTL, KD, parts)
                    DVE.wait(md, a1)
                    a2 = DVE.done(nc.vector.scalar_tensor_tensor(
                        out=f_act[:, m, :], in0=b2.t[:, :], scalar=sc_in[:, 1, m:m + 1], in1=s_tmp[:, m % 2, :],
                        op0=ALU.mult, op1=ALU.mult))
                    b2.free = a2
                    free[m % 2] = a2
                    act1.append((a2,) + split(f_act[:, m, :], f_H[0][:, m, :], f_L[0][:, m, :], a2))
                prev, hidden_last = act1, None
                for layer, w in ((0, h1), (1, h2)):
                    nxt = []
                    for m in range(KF):
                        bank = ring.take()
                        md = ternary(bank, w, m, f_H[layer], f_L[layer], KF, prev)
                        ACTE.wait(md, *prev[m])
                        a = ACTE.done(nc.scalar.activation(f_act[:, m, :], bank.t[:, :], ACT.Gelu,
                                                           scale=sc_in[:, 2 + layer, m:m + 1]))
                        bank.free = a
                        nxt.append((a,) + (split(f_act[:, m, :], f_H[1][:, m, :], f_L[1][:, m, :], a) if layer == 0 else ()))
                    prev = nxt
                acc = wide[0]
                PE.wait(acc.free)
                for t in range(TT):
                    for k in range(KF):
                        PE.wait(*prev[k])
                        i = nc.tensor.matmul(acc.t[:, t * D:(t + 1) * D], f_act[:, k, t * P:(t + 1) * P], w3[:, k, :],
                                             start=(k == 0), stop=(k == KF - 1))
                md = PE.done(i)
                DVE.wait(md, rows_got, parts[-1][0])
                a = DVE.done(nc.vector.tensor_tensor(xhat[:, :, :], acc.t[:, :].rearrange("p (t d) -> p t d", t=TT),
                                                     s3_row[:, None, :].broadcast_to([P, TT, D]), ALU.mult))
                acc.free = a
                DVE.wait(a)
                a = DVE.done(nc.vector.tensor_tensor(xhat[:, :, :], xhat[:, :, :],
                                                     rows2[:, GB:GB + 1, :].broadcast_to([P, TT, D]), ALU.mult))
                DVE.wait(a)
                a = DVE.done(nc.vector.tensor_tensor(xres[:, :, :], xres[:, :, :], xhat[:, :, :], ALU.add))
                SP.wait(a)
                stores.start(SP, out_v[b], xres[:, :, :])

            with nc.Fori(0, B) as b:
                mlp(b)
                join()


TURNED = {"router_T": "L0_ffn_router_w", "w1_T": "L1_ffn_w1_w", "w2_T": "L1_ffn_w2_w",
          "h1_T": "L1_ffn_h1_w", "h2_T": "L1_ffn_h2_w", "w3_T": "L1_ffn_w3_w"}


PER_FEATURE = ["L0_attn_ln_g", "L0_attn_ln_b", "L0_attn_b_hidden", "L1_attn_conv_w", "L1_attn_conv_b",
               "L1_attn_b_dt", "L1_attn_D", "L1_ffn_w1_s", "L1_ffn_w2_s", "L1_ffn_h1_s", "L1_ffn_h2_s"]


def kernel(**inputs):
    import numpy as np
    import concourse.bacc as bacc
    from concourse.bass_utils import run_bass_kernel_spmd

    nc = bacc.Bacc("TRN2", target_bir_lowering=False, num_devices=1)
    arrays = {}
    turned_names = set(TURNED.values())
    for name, a in inputs.items():
        if name not in turned_names:
            arrays[name] = np.ascontiguousarray(a)
    for short, name in TURNED.items():
        arrays[short] = np.ascontiguousarray(np.asarray(inputs[name]).T)
    for name in PER_FEATURE:
        a = np.asarray(inputs[name])
        tiles = a.reshape(*[n for n in a.shape[:-1] if n > 1], -1, P)
        arrays[name] = np.ascontiguousarray(np.moveaxis(tiles, -1, 0))
    aps = {}
    for name, a in arrays.items():
        aps[name] = nc.dram_tensor(name, a.shape, mybir.dt.from_np(a.dtype), kind="ExternalInput").ap()
    out = nc.dram_tensor("x_out", inputs["L0_attn_x"].shape, F32, kind="ExternalOutput").ap()
    adaln_kernel(nc, aps, out)
    result = run_bass_kernel_spmd(nc, [arrays], core_ids=[0])
    return result.results[0]["x_out"]
```

```python
from contextlib import ExitStack

import concourse.bass as bass
from concourse import mybir

F32 = mybir.dt.float32
F32R = mybir.dt.float32r
U32 = mybir.dt.uint32
ALU = mybir.AluOpType
ACT = mybir.ActivationFunctionType
AX = mybir.AxisListType

P = 128


class Counts:

    def __init__(self):
        self.per_turn, self.last, self.kinds = {}, {}, []


class Event:

    def __init__(self, sem, value, at=0.0):
        self.sem, self.value, self.at = sem, value, at


class Lane:

    def __init__(self, name, engine, sem, cost, loop):
        self.name, self.e, self.sem, self.cost, self.loop = name, engine, sem, cost, loop
        self.restart()

    def restart(self):
        self.count, self.seen, self.clock, self.table = 0, {}, 0.0, None

    def done(self, instruction, cost=None):
        instruction.then_inc(self.sem, 1)
        self.count += 1
        self.clock += self.cost if cost is None else cost
        return Event(self.sem, self.count, self.clock + SIGNAL_US)

    def wait(self, *events):
        for event in sorted((e for e in events if e is not None), key=lambda e: -e.value):
            if event.value <= self.seen.get(event.sem.name, NEVER):
                continue
            self.e.wait_ge(event.sem, self.loop.value(event))
            self.seen[event.sem.name] = event.value
            self.clock = max(self.clock, event.at)


NEVER = -1 << 30


class Loop:

    def __init__(self):
        self.turn, self.counts = None, None

    def value(self, event):
        if self.turn is None:
            return event.value
        per_turn = self.counts.per_turn.get(event.sem.name, 0)
        return (self.turn + 1) * per_turn + event.value

    def before(self, key):
        if self.turn is None or self.counts is None:
            return []
        return [Event(e.sem, e.value - self.counts.per_turn.get(e.sem.name, 0))
                for e in self.counts.last.get(key, [])]


class Load:

    def __init__(self, sem):
        self.sem = sem
        self.restart()

    def restart(self):
        self.count = 0

    def start(self, lane, out, in_):
        lane.e.dma_start(out, in_).then_inc(self.sem, 16)
        self.count += 16
        return Event(self.sem, self.count, lane.clock + 3.0)


class Bank:

    def __init__(self, tensor):
        self.t, self.free = tensor, None


class Ring:
    def __init__(self, banks):
        self.banks, self.at = banks, 0

    def take(self):
        bank = self.banks[self.at % len(self.banks)]
        self.at += 1
        return bank


TABLE_US = 1.3
SIGNAL_US = 0.13


def holds(lane, table):
    return table is None or lane.table == table or (table == ACT.Exp and lane.table == ACT.Ln)


def at(lane, *events, table=None, apart=False):
    yield lane, events, table
    lane.wait(*events)
    if apart:
        lane.e.nop(nofuse=True)
    if not holds(lane, table):
        lane.clock += TABLE_US
        lane.table = table


def interleave(*stages):
    heads = [[stage, next(stage, None)] for stage in stages]

    def start(head):
        lane, events, table = head[1]
        ready = max([lane.clock] + [e.at for e in events if e is not None])
        return ready + (0 if holds(lane, table) else TABLE_US)

    while live := [h for h in heads if h[1] is not None]:
        first = min(live, key=start)
        first[1] = next(first[0], None)


def adaln_kernel(nc, ins, out, counts):
    B, S, D = ins["L0_attn_x"].shape
    TT = S // P
    KD = D // P
    HID = ins["L0_attn_W_hidden"].shape[1] // 2
    KH = HID // P
    HS = ins["L0_ffn_sw1"].shape[1]
    KS = HS // P
    E, _, HR = ins["L0_ffn_ew1"].shape
    KR = HR // P
    INTER = ins["L1_attn_W_in"].shape[1] // 2
    KI = INTER // P
    NST = ins["L1_attn_A_log"].shape[1]
    DTR = ins["L1_attn_W_dt"].shape[0]
    KC = ins["L1_attn_conv_w"].shape[1]
    PAD = KC - 1
    DH = ins["w1_T"].shape[1]
    KF = DH // P
    HC = KI // 2
    EPS = 1e-5
    NMOD = 6
    SA, CA, GA, SB_, CB, GB = range(NMOD)
    POOL_EVERY = 2
    PASS = 0.215

    def scratch(name, shape):
        return nc.dram_tensor(name, shape, F32, kind="Internal").ap()

    mod_rows = scratch("mod_rows", (2, B, NMOD, D))
    mod_cols = scratch("mod_cols", (2, B, P, NMOD * KD))
    x_mid = scratch("x_after_layer0", (B, S, D))
    x_ssm = scratch("x_after_ssm", (B, S, D))

    def token_tiles(dram):
        return dram.rearrange("b (t p) d -> b p t d", p=P)

    def k_tiles(weights):
        return weights.rearrange("(k p) n -> p k n", p=P)

    def over_partitions(vector):
        return vector.partition_broadcast(P)

    x_in_v, x_mid_v, x_ssm_v, out_v = map(token_tiles, (ins["L0_attn_x"], x_mid, x_ssm, out))

    with ExitStack() as top:
        def sem(name):
            return top.enter_context(nc.semaphore(name))

        loop = Loop()
        PE = Lane("pe", nc.tensor, sem("pe_done"), 6 * PASS, loop)
        ACTE = Lane("act", nc.scalar, sem("act_done"), 0.62, loop)
        DVE = Lane("dve", nc.vector, sem("dve_done"), 0.68, loop)
        POOL = Lane("pool", nc.gpsimd, sem("pool_done"), 1.25, loop)
        SP = Lane("sp", nc.sync, sem("sp_done"), 0.1, loop)
        lanes = (PE, ACTE, DVE, POOL, SP)
        queues = {}

        def queue(kind):
            if kind not in queues:
                queues[kind] = Load(sem("dma_" + kind))
            return queues[kind]

        def dma(kind, out_, in_):
            return queue(kind).start(SP, out_, in_)

        banks = [Bank(top.enter_context(nc.psum_tensor(f"bank{i}", [P, 512], F32))) for i in range(8)]

        def restart():
            for x in (*lanes, *queues.values()):
                x.restart()
            for bank in banks:
                bank.free = None

        def all_sems():
            return [x.sem for x in (*lanes, *queues.values())]

        def join():
            for q in queues.values():
                if q.count:
                    SP.wait(Event(q.sem, q.count))
            nc.all_engine_barrier()
            for s in all_sems():
                nc.sync.sem_clear(s)
            nc.all_engine_barrier()
            restart()

        def turns(name, n, lay_out):
            known = counts.setdefault(name, Counts())
            for kind in known.kinds:
                queue(kind)
            join()
            for s in all_sems():
                if known.per_turn.get(s.name):
                    nc.sync.sem_inc(s, known.per_turn[s.name])
            nc.all_engine_barrier()
            with nc.Fori(0, n) as turn:
                loop.turn, loop.counts = turn, known
                for k, bank in enumerate(banks):
                    bank.free = (loop.before(f"bank{k}") or [None])[0]
                ended.clear()
                lay_out(turn)
                for k, bank in enumerate(banks):
                    if bank.free is not None:
                        ended[f"bank{k}"] = [bank.free]
            loop.turn = None
            known.per_turn = {x.sem.name: x.count for x in (*lanes, *queues.values())}
            known.last = dict(ended)
            ended.clear()
            known.kinds = [kind for kind, q in queues.items() if q.count]
            for q in queues.values():
                if q.count:
                    nc.sync.wait_ge(q.sem, (n + 1) * q.count)
            nc.all_engine_barrier()
            for s in all_sems():
                nc.sync.sem_clear(s)
            nc.all_engine_barrier()
            restart()

        ended = {}

        def sb_in(stack):
            return lambda name, shape, dt=F32: stack.enter_context(nc.sbuf_tensor(name, shape, dt))

        keep = sb_in(top)
        ident = keep("ident", [P, P])
        minus_half = keep("minus_half", [P, TT])

        class Norm:

            def __init__(self, name, sb):
                self.stat6 = sb(f"{name}_stat6", [P, TT, 6])
                self.stat = sb(f"{name}_stat", [P, TT, 2])
                self.veps = sb(f"{name}_veps", [P, TT])
                self.rstd = sb(f"{name}_rstd", [P, TT])

        def layernorm(norm, x, xhat, x_ready, xhat_free=None):
            yield from at(DVE, x_ready)
            for t in range(TT):
                s6 = DVE.done(nc.vector.bn_stats(norm.stat6[:, t, :], x[:, t, :]), 0.33)
            yield from at(DVE, s6, apart=True)
            for t in range(TT):
                s2 = DVE.done(nc.vector.bn_aggr(norm.stat[:, t, :], norm.stat6[:, t, :]), 0.08)
            yield from at(DVE, s2)
            v = DVE.done(nc.vector.tensor_scalar(norm.veps[:, :], norm.stat[:, :, 1], EPS, None, ALU.add), 0.08)
            yield from at(POOL, v)
            r = POOL.done(nc.gpsimd.tensor_tensor(norm.rstd[:, :], norm.veps[:, :], minus_half[:, :], ALU.pow), 1.0)
            yield from at(DVE, r, xhat_free)
            for t in range(TT):
                done = DVE.done(nc.vector.tensor_scalar(xhat[:, t, :], x[:, t, :], norm.stat[:, t, 0:1],
                                                        norm.rstd[:, t:t + 1], ALU.subtract, ALU.mult), 0.4)
            return done

        def split(full, hi, lo, *ready):
            yield from at(DVE, *ready)
            h = DVE.done(nc.vector.tensor_copy(hi, full), 0.34)
            yield from at(DVE, h)
            return h, DVE.done(nc.vector.tensor_tensor(lo, full, hi.bitcast(F32), ALU.subtract))

        def modulated_T(ring, src, src_ready, scale, bias, full, hi, lo, *free):
            parts = []
            for k in range(KD):
                bank = ring.take()
                yield from at(PE, src_ready, bank.free)
                for t in range(TT):
                    i = nc.tensor.transpose(bank.t[:, t * P:(t + 1) * P], src[:, t, k * P:(k + 1) * P], ident[:, :])
                turned = PE.done(i, 1.2)
                yield from at(ACTE, turned, *free)
                m = ACTE.done(nc.scalar.activation(full[:, k, :], bank.t[:, :], ACT.Identity,
                                                   bias=bias(k), scale=scale(k)))
                bank.free = m
                parts.append((m,) + (yield from split(full[:, k, :], hi[:, k, :], lo[:, k, :], m, *free)))
            return parts

        def split_product(out_, lhs, rhs, nk, parts):
            for k in range(nk):
                PE.wait(*parts[k])
                (lh, ll), (rh, rl) = lhs(k), rhs(k)
                for n, (a, b) in enumerate(((lh, rh), (lh, rl), (ll, rh))):
                    i = nc.tensor.matmul(out_, a, b, start=(k == 0 and n == 0), stop=(k == nk - 1 and n == 2))
            return PE.done(i, 3 * nk * PASS)

        def token_product(ring, lhs, rhs, nk, width, *ready):
            made = []
            for pair in range(0, TT, 2):
                bank = ring.take()
                yield from at(PE, bank.free, *ready)
                for j in range(2):
                    t = pair + j
                    for k in range(nk):
                        i = nc.tensor.matmul(bank.t[:, j * width:(j + 1) * width], lhs(k)[:, t * P:(t + 1) * P],
                                             rhs(k), start=(k == 0), stop=(k == nk - 1))
                made.append((bank, PE.done(i, 4 * nk * PASS)))
            return made

        def pair_of(tile, pair):
            return tile[:, 2 * pair:2 * pair + 2, :]

        def bank_pair(bank):
            return bank.t[:, :].rearrange("p (t d) -> p t d", t=2)

        def load_split(stage_buf, hi, lo, src, free):
            width, step = src.shape[1], stage_buf.shape[2]
            for c in range(0, width, step):
                w = min(step, width - c)
                n = free["turn"] % 2
                free["turn"] += 1
                slot = stage_buf[:, n, 0:w]
                yield from at(SP, free.get(n))
                got = dma(f"stage{n}", slot, src[:, c:c + w])
                _, free[n] = yield from split(slot, hi[:, c:c + w], lo[:, c:c + w], got)

        z = POOL.done(nc.gpsimd.memset(ident[:, :], 0.0))
        POOL.wait(z)
        ident_ready = POOL.done(nc.gpsimd.affine_select(
            out=ident[:, :], in_=ident[:, :], compare_op=ALU.not_equal, fill=1.0, base=0,
            pattern=[[-1, P]], channel_multiplier=1))
        POOL.done(nc.gpsimd.memset(minus_half[:, :], -0.5))

        ring = Ring(banks)
        with ExitStack() as stack:
            sb = sb_in(stack)
            c_tok = sb("c_tok", [B, 2, D])
            c_act = sb("c_act", [B, 2, D])
            cT = sb("cT", [P, 2, KD, B])
            wmod = sb("wmod", [P, 2, KD, NMOD * D])
            rows = sb("rows", [B, 2, NMOD * D])
            sgn = sb("sgn", [B, 2, D])
            mag = sb("mag", [B, 2, D])
            mod_T = sb("mod_T", [P, 2, B, NMOD * KD])
            c_got, wmod_got = [], []
            for l in range(2):
                c_got.append(dma(f"c{l}", c_tok[:, l, :], ins[f"L{l}_c"]))
                wmod_got.append(dma(f"wmod{l}", wmod[:, l, :, :], k_tiles(ins[f"L{l}_wmod"])))
            ACTE.wait(*c_got)
            silu_c = ACTE.done(nc.scalar.activation(c_act[:, :, :], c_tok[:, :, :], ACT.Silu))
            PE.wait(ident_ready, silu_c)
            bank = ring.take()
            for l in range(2):
                for k in range(KD):
                    o = (l * KD + k) * B
                    i = nc.tensor.transpose(bank.t[:, o:o + B], c_act[:, l, k * P:(k + 1) * P], ident[0:B, 0:B])
            turned = PE.done(i)
            DVE.wait(turned)
            cT_ready = DVE.done(nc.vector.tensor_copy(
                cT[:, :, :, :], bank.t[:, 0:2 * KD * B].rearrange("p (l k b) -> p l k b", l=2, k=KD)))
            bank.free = cT_ready
            PE.wait(cT_ready)
            for l in range(2):
                PE.wait(wmod_got[l])
                for c in range(0, NMOD * D, 512):
                    bank = ring.take()
                    PE.wait(bank.free)
                    for k in range(KD):
                        i = nc.tensor.matmul(bank.t[0:B, :], cT[:, l, k, :], wmod[:, l, k, c:c + 512],
                                             start=(k == 0), stop=(k == KD - 1))
                    made = PE.done(i)
                    DVE.wait(made)
                    copied = DVE.done(nc.vector.tensor_copy(rows[:, l, c:c + 512], bank.t[0:B, :]))
                    bank.free = copied
            DVE.wait(copied)
            for l in range(2):
                for which in (CA, CB):
                    r = rows[:, l, which * D:(which + 1) * D]
                    last = DVE.done(nc.vector.tensor_scalar(r, r, 1.0, None, ALU.add))
            for which in (GA, GB):
                r = rows[:, :, which * D:(which + 1) * D]
                DVE.wait(last)
                a = DVE.done(nc.vector.tensor_scalar(sgn[:, :, :], r, 0.0, 2.0, ALU.is_ge, ALU.mult))
                b = DVE.done(nc.vector.tensor_scalar(mag[:, :, :], r, -1.0, None, ALU.mult))
                DVE.wait(b)
                c = DVE.done(nc.vector.tensor_tensor(mag[:, :, :], mag[:, :, :], r, ALU.max))
                DVE.wait(c)
                d = DVE.done(nc.vector.tensor_scalar(mag[:, :, :], mag[:, :, :], 0.25, None, ALU.max))
                e = DVE.done(nc.vector.tensor_scalar(sgn[:, :, :], sgn[:, :, :], -1.0, None, ALU.add))
                DVE.wait(d, e)
                last = DVE.done(nc.vector.tensor_tensor(r, sgn[:, :, :], mag[:, :, :], ALU.mult))
            PE.wait(last)
            for l in range(2):
                bank = ring.take()
                PE.wait(bank.free)
                for j in range(NMOD * KD):
                    i = nc.tensor.transpose(bank.t[:, j * B:(j + 1) * B], rows[:, l, j * P:(j + 1) * P],
                                            ident[0:B, 0:B])
                turned = PE.done(i)
                DVE.wait(turned)
                bank.free = DVE.done(nc.vector.tensor_copy(
                    mod_T[:, l, :, :].rearrange("p b j -> p j b"),
                    bank.t[:, 0:NMOD * KD * B].rearrange("p (j b) -> p j b", b=B)))
            SP.wait(last, bank.free)
            for l in range(2):
                dma("mod", mod_rows[l].rearrange("b j d -> b (j d)"), rows[:, l, :])
                dma("mod", mod_cols[l].rearrange("b p j -> p b j"), mod_T[:, l, :, :])
            join()

        with ExitStack() as stack:
            sb = sb_in(stack)
            w_hid = [sb(f"w_hid{h}", [P, KD, 2 * HID], F32R) for h in "HL"]
            w_qk = [sb(f"w_qk{h}", [P, KD, HID], F32R) for h in "HL"]
            w_s1 = [sb(f"w_s1{h}", [P, KD, HS], F32R) for h in "HL"]
            w_s3 = [sb(f"w_s3{h}", [P, KD, HS], F32R) for h in "HL"]
            w_o = sb("w_o", [P, KH, D])
            w_s2 = sb("w_s2", [P, KS, D])
            w_router = sb("w_router", [P, KD, E])
            lnc = sb("lnc", [P, 2, KD])
            b_hid = sb("b_hid", [P, 2 * KH])
            bqk_row = sb("bqk_row", [P, HID])
            bout_row = sb("bout_row", [P, D])
            rbias_row = sb("rbias_row", [P, E])
            iota_e = sb("iota_e", [P, E])
            w_in = [sb(f"w_in{h}", [P, KD, 2 * INTER], F32R) for h in "HL"]
            w_x = sb("w_x", [P, KI, DTR])
            w_bc = sb("w_bc", [P, KI, 2, 2 * NST])
            w_dt = sb("w_dt", [DTR, INTER])
            w_out = sb("w_out", [P, KI, D])
            conv_w = sb("conv_w", [P, KC, KI])
            conv_b = sb("conv_b", [P, KI])
            b_dt = sb("b_dt", [P, KI])
            d_skip = sb("d_skip", [P, KI])
            a_neg = sb("a_neg", [P, KI, NST])
            pick = sb("pick", [4 * NST, 2 * NST], F32R)
            normA, normB = Norm("normA", sb), Norm("normB", sb)
            with ExitStack() as staging:
                stage_buf = sb_in(staging)("stage1", [P, 2, 2048])
                pick_f = sb_in(staging)("pick_f", [4 * NST, 2 * NST])

                def first_weights():
                    free = {"turn": 0}
                    for name, parts in (("L0_attn_W_hidden", w_hid), ("L0_attn_W_qk", w_qk), ("L0_ffn_sw1", w_s1),
                                        ("L0_ffn_sw3", w_s3), ("L1_attn_W_in", w_in)):
                        src = k_tiles(ins[name])
                        for k in range(KD):
                            yield from load_split(stage_buf, parts[0][:, k, :], parts[1][:, k, :], src[:, k, :], free)

                interleave(first_weights())
                dma("w", w_o[:, :, :], k_tiles(ins["L0_attn_W_out"]))
                dma("w", w_s2[:, :, :], k_tiles(ins["L0_ffn_sw2"]))
                dma("w", w_router[:, :, :], k_tiles(ins["router_T"]))
                dma("w", lnc[:, 0, :], ins["L0_attn_ln_g"])
                dma("w", lnc[:, 1, :], ins["L0_attn_ln_b"])
                dma("w", b_hid[:, :], ins["L0_attn_b_hidden"])
                dma("w", bqk_row[:, :], over_partitions(ins["L0_attn_b_qk"]))
                dma("w", bout_row[:, :], over_partitions(ins["L0_attn_b_out"]))
                dma("w", rbias_row[:, :], over_partitions(ins["L0_ffn_router_bias"]))
                wx = k_tiles(ins["L1_attn_W_x"])
                dma("w", w_x[:, :, :], wx[:, :, 0:DTR])
                for twice in range(2):
                    dma("w", w_bc[:, :, twice, :], wx[:, :, DTR:DTR + 2 * NST])
                dma("w", w_dt[:, :], ins["L1_attn_W_dt"])
                dma("w", w_out[:, :, :], k_tiles(ins["L1_attn_W_out"]))
                dma("w", conv_w[:, :, :], ins["L1_attn_conv_w"])
                dma("w", conv_b[:, :], ins["L1_attn_conv_b"])
                dma("w", b_dt[:, :], ins["L1_attn_b_dt"])
                dma("w", d_skip[:, :], ins["L1_attn_D"])
                al = dma("a_log", a_neg[:, :, :], ins["L1_attn_A_log"].rearrange("(k p) n -> p k n", p=P))
                ACTE.wait(al)
                ex = ACTE.done(nc.scalar.activation(a_neg[:, :, :], a_neg[:, :, :], ACT.Exp))
                DVE.wait(ex)
                DVE.done(nc.vector.tensor_scalar(a_neg[:, :, :], a_neg[:, :, :], -1.0, None, ALU.mult))
                POOL.done(nc.gpsimd.iota(iota_e[:, :], pattern=[[1, E]], base=0, channel_multiplier=0,
                                         allow_small_or_imprecise_dtypes=True))
                zz = POOL.done(nc.gpsimd.memset(pick_f[:, :], 0.0))
                for shift in (0, 2 * NST):
                    POOL.wait(zz)
                    zz = POOL.done(nc.gpsimd.affine_select(
                        out=pick_f[:, :], in_=pick_f[:, :], compare_op=ALU.not_equal, fill=1.0, base=-shift,
                        pattern=[[-1, 2 * NST]], channel_multiplier=1))
                DVE.wait(zz)
                DVE.done(nc.vector.tensor_copy(pick[:, :], pick_f[:, :]))
                join()

            xresA = sb("xresA", [P, TT, D])
            h_tok = sb("h_tok", [P, TT, D])
            nT = sb("nT", [P, KD, S])
            nTH = sb("nTH", [P, KD, S], F32R)
            nTL = sb("nTL", [P, KD, S], F32R)
            rowsA = sb("rowsA", [P, 4, D])
            colsA = sb("colsA", [P, NMOD * KD])
            q_tok = sb("q_tok", [P, TT, HID])
            v_T = q_tok
            s_act = q_tok
            k_tok = sb("k_tok", [P, TT, HID])
            g_T = k_tok
            e_act = k_tok
            tmpA = sb("tmpA", [P, 2, HID])
            xhatA = tmpA[:, :, :].rearrange("p a (t d) -> p (a t) d", d=D)
            w_e = sb("w_e", [P, 2, 2, KD * HR])
            os_rows = w_e
            smax = sb("smax", [P, KH])
            esum = sb("esum", [P, KH])
            rsum = sb("rsum", [P, KH])
            attn_sum = sb("attn_sum", [P, KH])
            rt = sb("rt", [P, 9, TT, E])
            rt_idx = sb("rt_idx", [P, TT, 8], U32)
            rt_small = sb("rt_small", [P, 4, TT])
            xresB = sb("xresB", [P, TT, D])
            hTH = sb("hTH", [P, KD, S], F32R)
            hTL = sb("hTL", [P, KD, S], F32R)
            gaB = sb("gaB", [P, D])
            colsB = sb("colsB", [P, NMOD * KD])
            RAW = KI * (PAD + S)
            work = sb("work", [P, max(RAW + 6 * S, 2 * HC * S + 3 * HC * S)])
            raw = work[:, 0:RAW].rearrange("p (c s) -> p c s", c=KI)
            cv = work[:, RAW:RAW + 2 * S].rearrange("p (c s) -> p c s", c=2)
            ts = cv[0:DTR, 0, :]
            bc_full = cv[0:4 * NST, 1, :]
            sp_t = work[:, RAW + 2 * S:RAW + 6 * S].rearrange("p (a b s) -> p a b s", a=2, b=2)
            dA = work[:, 0:2 * HC * S].rearrange("p (a j s) -> p a j s", a=2, j=HC)
            st = work[:, 2 * HC * S:5 * HC * S].rearrange("p (a j s) -> p a j s", a=3, j=HC)
            bc_parts = sb("bc_parts", [4 * NST, S], F32R)
            hcv = sb("hcv", [P, KI, S])
            y = hcv
            gate = sb("gate", [P, KI, S])
            dt = sb("dt", [P, KI, S])
            tokB = dt[:, 0:2, :].rearrange("p a (t d) -> p (a t) d", d=D)
            u = sb("u", [P, KI, S])
            xhatB = u[:, 0:2, :].rearrange("p a (t d) -> p (a t) d", d=D)
            hT = u[:, 2:4, :]
            bcb = sb("bcb", [P, 2, 2, S])

            ringA, ringB = Ring(banks[0:5]), Ring(banks[5:8])

            def w_cols(parts, k, c, w=P):
                return parts[0][:, k, c:c + w], parts[1][:, k, c:c + w]

            def layer0(b):
                stored = loop.before("A.stored")
                x_got = None
                yield from at(SP, *stored)
                x_got = dma("A_x", xresA[:, :, :], x_in_v[b])
                rows_got = [dma("A_rows", rowsA[:, 0:3, :], mod_rows[0, b, 0:3].partition_broadcast(P)),
                            dma("A_gb", rowsA[:, 3:4, :], mod_rows[0, b, 5:6].partition_broadcast(P))]
                cols = dma("A_cols", colsA[:, :], mod_cols[0, b])
                yield from at(SP, *loop.before("A.experts"))
                os_got = [dma(f"A_os{j}", os_rows[:, j, :, :], ins["os_rows"][j].partition_broadcast(P)) for j in range(2)]

                def rb(which):
                    return rowsA[:, which:which + 1, :].broadcast_to([P, TT, D])

                def col(which, k):
                    return colsA[:, which * KD + k:which * KD + k + 1]

                n1 = yield from layernorm(normA, xresA, xhatA, x_got)
                yield from at(DVE, n1, *rows_got)
                m1 = DVE.done(nc.vector.tensor_tensor(h_tok[:, :, :], xhatA, rb(1), ALU.mult), 1.2)
                yield from at(DVE, m1)
                h_ready = DVE.done(nc.vector.tensor_tensor(h_tok[:, :, :], h_tok[:, :, :], rb(0), ALU.add), 1.2)
                n2 = yield from layernorm(normA, h_tok, xhatA, h_ready, m1)
                parts = yield from modulated_T(ringA, xhatA, n2, lambda k: lnc[:, 0, k:k + 1],
                                               lambda k: lnc[:, 1, k:k + 1], nT, nTH, nTL, *loop.before("A.experts"))
                tmp_free = [[], []]
                qk_ready = []
                for t in range(TT):
                    bank = ringA.take()
                    yield from at(PE, bank.free)
                    made = split_product(bank.t[:, :], lambda k: (nTH[:, k, t * P:(t + 1) * P], nTL[:, k, t * P:(t + 1) * P]),
                                         lambda k: w_cols(w_qk, k, 0, HID), KD, parts)
                    tmp = tmpA[:, t % 2, :]
                    yield from at(DVE, made, *tmp_free[t % 2])
                    biased = DVE.done(nc.vector.tensor_tensor(tmp, bank.t[:, :], bqk_row[:, :], ALU.add))
                    bank.free = biased
                    yield from at(ACTE, biased, table=ACT.Silu)
                    act = ACTE.done(nc.scalar.activation(tmp, tmp, ACT.Silu))
                    yield from at(DVE, act, *os_got)
                    qm = DVE.done(nc.vector.tensor_tensor(q_tok[:, t, :], tmp, os_rows[:, 0, 0, :], ALU.mult))
                    yield from at(POOL, act, *os_got)
                    km = POOL.done(nc.gpsimd.tensor_tensor(k_tok[:, t, :], tmp, os_rows[:, 1, 0, :], ALU.mult))
                    yield from at(DVE, qm)
                    qa = DVE.done(nc.vector.tensor_tensor(q_tok[:, t, :], q_tok[:, t, :], os_rows[:, 0, 1, :], ALU.add))
                    yield from at(POOL, km)
                    ka = POOL.done(nc.gpsimd.tensor_tensor(k_tok[:, t, :], k_tok[:, t, :], os_rows[:, 1, 1, :], ALU.add))
                    tmp_free[t % 2] = [qm, km]
                    qk_ready.append([qa, ka])
                up_got, down_got = {}, {}

                def fetch(e, *free):
                    yield from at(SP, *free)
                    up_got[e] = dma(f"A_up{e % 2}", w_e[:, e % 2, 0, :].rearrange("p (k n) -> p k n", k=KD), k_tiles(ins["L0_ffn_ew1"][e]))
                    down_got[e] = dma(f"A_down{e % 2}", w_e[:, e % 2, 1, :].rearrange("p (k n) -> p k n", k=KR), k_tiles(ins["L0_ffn_ew2"][e]))

                yield from fetch(0, qa, ka)
                yield from fetch(1, qa, ka)
                for d in range(KH):
                    bank = ringA.take()
                    yield from at(PE, bank.free)
                    for t in range(TT):
                        PE.wait(*qk_ready[t])
                        i = nc.tensor.matmul(bank.t[:, :], q_tok[:, t, d * P:(d + 1) * P], k_tok[:, t, :],
                                             start=(t == 0), stop=(t == TT - 1))
                    sim_done = PE.done(i, 4 * TT * PASS)
                    yield from at(DVE, sim_done)
                    mx = DVE.done(nc.vector.tensor_reduce(smax[:, d:d + 1], bank.t[:, :], AX.X, ALU.max))
                    yield from at(DVE, mx)
                    neg = DVE.done(nc.vector.tensor_scalar(smax[:, d:d + 1], smax[:, d:d + 1], -1.0 / S, None, ALU.mult), 0.1)
                    yield from at(ACTE, neg, sim_done, table=ACT.Exp)
                    ex = ACTE.done(nc.scalar.activation(bank.t[:, :], bank.t[:, :], ACT.Exp, bias=smax[:, d:d + 1],
                                                        scale=1.0 / S, accum_out=esum[:, d:d + 1]))
                    bank.free = ex
                yield from at(DVE, ex)
                rc = DVE.done(nc.vector.reciprocal(rsum[:, :], esum[:, :]), 0.1)
                yield from at(DVE, rc)
                asum = DVE.done(nc.vector.tensor_tensor(attn_sum[:, :], esum[:, :], rsum[:, :], ALU.mult), 0.1)
                gated = []
                for d in range(KH):
                    evs = []
                    for half, dst in ((0, v_T), (1, g_T)):
                        bank = ringA.take()
                        yield from at(PE, bank.free)
                        made = split_product(bank.t[:, :], lambda k: w_cols(w_hid, k, half * HID + d * P),
                                             lambda k: (nTH[:, k, :], nTL[:, k, :]), KD, parts)
                        j = half * KH + d
                        yield from at(ACTE, made, sim_done, table=ACT.Silu)
                        ev = ACTE.done(nc.scalar.activation(dst[:, d, :], bank.t[:, :], ACT.Silu, bias=b_hid[:, j:j + 1]))
                        bank.free = ev
                        evs.append(ev)
                    yield from at(DVE, asum, *evs)
                    gated.append(DVE.done(nc.vector.scalar_tensor_tensor(
                        out=v_T[:, d, :], in0=v_T[:, d, :], scalar=attn_sum[:, d:d + 1], in1=g_T[:, d, :],
                        op0=ALU.mult, op1=ALU.mult)))
                yield from at(POOL, n2)
                i1 = POOL.done(nc.gpsimd.tensor_tensor(h_tok[:, :, :], h_tok[:, :, :],
                                                       bout_row[:, None, :].broadcast_to([P, TT, D]), ALU.add), 2.4)
                made = yield from token_product(ringA, lambda k: v_T[:, k, :], lambda k: w_o[:, k, :], KH, D, *gated)
                wo_done = made[-1][1]
                x1 = []
                for n, (bank, ev) in enumerate(made):
                    hp, xp = pair_of(h_tok, n), pair_of(xresA, n)
                    yield from at(DVE, ev, i1)
                    i2 = DVE.done(nc.vector.tensor_tensor(hp, hp, bank_pair(bank), ALU.add))
                    bank.free = i2
                    yield from at(DVE, i2)
                    i3 = DVE.done(nc.vector.tensor_tensor(hp, hp, rowsA[:, 2:3, :].broadcast_to([P, 2, D]), ALU.mult))
                    yield from at(DVE, i3)
                    x1 = DVE.done(nc.vector.tensor_tensor(xp, xp, hp, ALU.add))
                n3 = yield from layernorm(normA, xresA, xhatA, x1)
                yield from at(ACTE, cols)
                parts = yield from modulated_T(ringA, xhatA, n3, lambda k: col(CB, k), lambda k: col(SB_, k),
                                               nT, nTH, nTL, wo_done)
                rbank = ringA.take()
                yield from at(PE, rbank.free, parts[0][0], parts[1][0])
                for t in range(TT):
                    for k in range(KD):
                        i = nc.tensor.matmul(rbank.t[:, t * E:(t + 1) * E], nT[:, k, t * P:(t + 1) * P], w_router[:, k, :],
                                             start=(k == 0), stop=(k == KD - 1))
                routed = PE.done(i, 0.8)
                scores_sig = rt[:, 0, :, :]
                yield from at(ACTE, routed, table=ACT.Sigmoid)
                sig = ACTE.done(nc.scalar.activation(
                    scores_sig, rbank.t[:, 0:TT * E].rearrange("p (t e) -> p t e", t=TT), ACT.Sigmoid), 0.2)
                rbank.free = sig

                def route():
                    sg, sel, oh1, oh2, msk, scored, comb, ix = (rt[:, j, :, :] for j in (0, 1, 3, 4, 5, 6, 7, 8))
                    small = 0.1
                    yield from at(DVE, sig)
                    a = DVE.done(nc.vector.tensor_tensor(sel, sg, rbias_row[:, None, :].broadcast_to([P, TT, E]), ALU.add), small)
                    yield from at(DVE, a, apart=True)
                    for t in range(TT):
                        a = DVE.done(nc.vector.max(rt[:, 2, t, :], rt[:, 1, t, :]), small)
                    yield from at(DVE, a, apart=True)
                    for t in range(TT):
                        a = DVE.done(nc.vector.max_index(rt_idx[:, t, :], rt[:, 2, t, :], rt[:, 1, t, :]), small)
                    yield from at(DVE, a)
                    a = DVE.done(nc.vector.tensor_copy(ix, rt_idx[:, :, :]), small)
                    yield from at(DVE, a)
                    iob = iota_e[:, None, :].broadcast_to([P, TT, E])
                    DVE.done(nc.vector.tensor_tensor(oh1, rt[:, 8, :, 0:1].broadcast_to([P, TT, E]), iob, ALU.is_equal), small)
                    a = DVE.done(nc.vector.tensor_tensor(oh2, rt[:, 8, :, 1:2].broadcast_to([P, TT, E]), iob, ALU.is_equal), small)
                    yield from at(DVE, a)
                    a = DVE.done(nc.vector.tensor_tensor(msk, oh1, oh2, ALU.add), small)
                    yield from at(DVE, a)
                    a = DVE.done(nc.vector.tensor_tensor(scored, msk, sg, ALU.mult), small)
                    yield from at(DVE, a)
                    den, ok, rden, half_ = (rt_small[:, j, :] for j in range(4))
                    a = DVE.done(nc.vector.tensor_reduce(den, scored, AX.X, ALU.add), small)
                    yield from at(DVE, a)
                    DVE.done(nc.vector.tensor_scalar(ok, den, 1e-9, None, ALU.is_gt), small)
                    DVE.done(nc.vector.tensor_scalar(half_, den, 1e-9, 0.5, ALU.is_le, ALU.mult), small)
                    a = DVE.done(nc.vector.tensor_scalar(den, den, 1e-9, None, ALU.add), small)
                    yield from at(DVE, a)
                    a = DVE.done(nc.vector.reciprocal(rden, den), small)
                    yield from at(DVE, a)
                    a = DVE.done(nc.vector.tensor_tensor(rden, rden, ok, ALU.mult), small)
                    yield from at(DVE, a)
                    bc = lambda j: rt_small[:, j, :, None].broadcast_to([P, TT, E])
                    DVE.done(nc.vector.tensor_tensor(scored, scored, bc(2), ALU.mult), small)
                    a = DVE.done(nc.vector.tensor_tensor(msk, msk, bc(3), ALU.mult), small)
                    yield from at(DVE, a)
                    return DVE.done(nc.vector.tensor_tensor(comb, scored, msk, ALU.add), small)

                s_parts = []
                tmp_free = [None, None]
                for m in range(KS):
                    bank = ringA.take()
                    yield from at(PE, bank.free)
                    made = split_product(bank.t[:, :], lambda k: w_cols(w_s1, k, m * P),
                                         lambda k: (nTH[:, k, :], nTL[:, k, :]), KD, parts)
                    yield from at(ACTE, made, tmp_free[m % 2], table=ACT.Silu)
                    a1 = ACTE.done(nc.scalar.activation(tmpA[:, m % 2, :], bank.t[:, :], ACT.Silu))
                    bank.free = a1
                    bank = ringA.take()
                    yield from at(PE, bank.free)
                    made = split_product(bank.t[:, :], lambda k: w_cols(w_s3, k, m * P),
                                         lambda k: (nTH[:, k, :], nTL[:, k, :]), KD, parts)
                    yield from at(DVE, made, a1)
                    a3 = DVE.done(nc.vector.tensor_tensor(s_act[:, m, :], bank.t[:, :], tmpA[:, m % 2, :], ALU.mult))
                    bank.free = a3
                    tmp_free[m % 2] = a3
                    s_parts.append(a3)
                comb_ready = yield from route()
                acts, act_free = {}, [None, None]

                def expert_up(e):
                    acts[e] = []
                    for m in range(KR):
                        bank = ringA.take()
                        yield from at(PE, bank.free, up_got[e])
                        for k in range(KD):
                            c = k * HR + m * P
                            i = nc.tensor.matmul(bank.t[:, :], w_e[:, e % 2, 0, c:c + P], nT[:, k, :],
                                                 start=(k == 0), stop=(k == KD - 1))
                        made = PE.done(i, 4 * KD * PASS)
                        yield from at(ACTE, made, act_free[e % 2], table=ACT.Gelu)
                        ev = ACTE.done(nc.scalar.activation(e_act[:, (e % 2) * KR + m, :], bank.t[:, :], ACT.Gelu))
                        bank.free = ev
                        acts[e].append(ev)

                yield from expert_up(0)
                made = yield from token_product(ringA, lambda k: s_act[:, k, :], lambda k: w_s2[:, k, :], KS, D, *s_parts)
                summed = [None] * TT
                for n, (bank, ev) in enumerate(made):
                    yield from at(ACTE, ev, x1)
                    bank.free = ACTE.done(nc.scalar.activation(pair_of(h_tok, n), bank_pair(bank), ACT.Copy))
                    summed[2 * n] = summed[2 * n + 1] = bank.free
                for e in range(E):
                    if e + 1 < E:
                        yield from expert_up(e + 1)
                    made = yield from token_product(
                        ringA, lambda k: e_act[:, (e % 2) * KR + k, :], lambda k: w_e[:, e % 2, 1, k * D:(k + 1) * D],
                        KR, D, down_got[e], *acts[e])
                    act_free[e % 2] = made[-1][1]
                    if e + 2 < E:
                        yield from fetch(e + 2, made[-1][1])
                    for n, (bank, ev) in enumerate(made):
                        for j in range(2):
                            t = 2 * n + j
                            yield from at(DVE, ev, comb_ready, summed[t])
                            summed[t] = DVE.done(nc.vector.scalar_tensor_tensor(
                                out=h_tok[:, t, :], in0=bank.t[:, j * D:(j + 1) * D], scalar=rt[:, 7, t, e:e + 1],
                                in1=h_tok[:, t, :], op0=ALU.mult, op1=ALU.add), 0.4)
                        bank.free = summed[t]
                ended["A.experts"] = [made[-1][1]]
                yield from at(DVE, summed[-1])
                a = DVE.done(nc.vector.tensor_tensor(h_tok[:, :, :], h_tok[:, :, :], rb(3), ALU.mult), 1.2)
                yield from at(DVE, a)
                x2 = DVE.done(nc.vector.tensor_tensor(xresA[:, :, :], xresA[:, :, :], h_tok[:, :, :], ALU.add), 1.2)
                yield from at(SP, x2)
                ended["A.stored"] = [dma("A_store", x_mid_v[b], xresA[:, :, :])]

            def ssm(b):
                yield from at(SP, *loop.before("A.stored"), *loop.before("B.stored"))
                x_got = dma("B_x", xresB[:, :, :], x_mid_v[b])
                ga_got = dma("B_ga", gaB[:, :], mod_rows[1, b, GA].partition_broadcast(P))
                cols = dma("B_cols", colsB[:, :], mod_cols[1, b])

                def col(which, k):
                    return colsB[:, which * KD + k:which * KD + k + 1]

                y_last, out_read = loop.before("B.y"), loop.before("B.out")
                yield from at(POOL, *y_last, apart=True)
                pad_zero = POOL.done(nc.gpsimd.memset(raw[:, :, 0:PAD], 0.0), 0.1)
                n1 = yield from layernorm(normB, xresB, xhatB, x_got, *y_last[-1:])
                yield from at(ACTE, cols, *out_read, *y_last)
                parts = yield from modulated_T(ringB, xhatB, n1, lambda k: col(CA, k), lambda k: col(SA, k), hT, hTH, hTL)
                conv_done, cv_free = [], []
                for pair in range(0, KI, 2):
                    both = (pair, pair + 1)
                    taps = []
                    for c in both:
                        bank = ringB.take()
                        yield from at(PE, bank.free)
                        made = split_product(bank.t[:, :], lambda k: w_cols(w_in, k, c * P),
                                             lambda k: (hTH[:, k, :], hTL[:, k, :]), KD, parts)
                        yield from at(ACTE, made)
                        rw = ACTE.done(nc.scalar.activation(raw[:, c, PAD:], bank.t[:, :], ACT.Copy))
                        bank.free = rw
                    for tap in range(KC):
                        for c in both:
                            o = cv[:, c % 2, :]
                            if tap == 0:
                                yield from at(DVE, rw, pad_zero, *cv_free)
                                taps.append(DVE.done(nc.vector.tensor_scalar(o, raw[:, c, 0:S], conv_w[:, 0, c:c + 1],
                                                                             None, ALU.mult), 0.4))
                            else:
                                yield from at(DVE, taps[c % 2])
                                taps[c % 2] = DVE.done(nc.vector.scalar_tensor_tensor(
                                    out=o, in0=raw[:, c, tap:tap + S], scalar=conv_w[:, tap, c:c + 1], in1=o,
                                    op0=ALU.mult, op1=ALU.add))
                    cv_free = []
                    for c in both:
                        yield from at(ACTE, taps[c % 2], table=ACT.Silu)
                        hv = ACTE.done(nc.scalar.activation(hcv[:, c, :], cv[:, c % 2, :], ACT.Silu, bias=conv_b[:, c:c + 1]))
                        cv_free.append(hv)
                    conv_done += cv_free
                for c in range(KI):
                    bank = ringB.take()
                    yield from at(PE, bank.free)
                    made = split_product(bank.t[:, :], lambda k: w_cols(w_in, k, INTER + c * P),
                                         lambda k: (hTH[:, k, :], hTL[:, k, :]), KD, parts)
                    yield from at(ACTE, made, table=ACT.Silu)
                    gate_ready = ACTE.done(nc.scalar.activation(gate[:, c, :], bank.t[:, :], ACT.Silu))
                    bank.free = gate_ready
                bank = ringB.take()
                yield from at(PE, bank.free, *conv_done)
                for k in range(KI):
                    i = nc.tensor.matmul(bank.t[0:DTR, :], w_x[:, k, :], hcv[:, k, :], start=(k == 0), stop=(k == KI - 1))
                md = PE.done(i, 4 * KI * PASS)
                bank2 = ringB.take()
                yield from at(PE, bank2.free)
                for k in range(KI):
                    i = nc.tensor.matmul(bank2.t[0:4 * NST, :], w_bc[:, k, :, :].rearrange("p a n -> p (a n)"),
                                         hcv[:, k, :], start=(k == 0), stop=(k == KI - 1))
                md2 = PE.done(i, 4 * KI * PASS)
                yield from at(ACTE, md)
                ts_ready = ACTE.done(nc.scalar.activation(ts, bank.t[0:DTR, :], ACT.Copy))
                bank.free = ts_ready
                yield from at(ACTE, md2)
                f = ACTE.done(nc.scalar.activation(bc_full, bank2.t[0:4 * NST, :], ACT.Copy))
                bank2.free = f
                yield from at(DVE, f)
                p1 = DVE.done(nc.vector.tensor_copy(bc_parts[:, :], bc_full))
                yield from at(DVE, p1)
                low = slice(2 * NST, 4 * NST)
                bc_ready = DVE.done(nc.vector.tensor_tensor(bc_parts[low, :], cv[low, 1, :],
                                                            bc_parts[low, :].bitcast(F32), ALU.subtract))
                mags, maxs = [], []
                for pair in range(0, KI, 2):
                    for c in (pair, pair + 1):
                        bank = ringB.take()
                        yield from at(PE, bank.free, ts_ready)
                        md = PE.done(nc.tensor.matmul(bank.t[:, :], w_dt[:, c * P:(c + 1) * P], ts, start=True, stop=True), 4 * PASS)
                        ab, mx = sp_t[:, c % 2, 0, :], sp_t[:, c % 2, 1, :]
                        yield from at(ACTE, md, *(mags[-2:] if pair else []), *maxs[:])
                        s1 = ACTE.done(nc.scalar.activation(ab, bank.t[:, :], ACT.Abs, bias=b_dt[:, c:c + 1]))
                        s2 = ACTE.done(nc.scalar.activation(mx, bank.t[:, :], ACT.Relu, bias=b_dt[:, c:c + 1]))
                        bank.free = s2
                    both = sp_t[:, :, 0, :]
                    yield from at(ACTE, s1, table=ACT.Exp)
                    s3 = ACTE.done(nc.scalar.activation(both, both, ACT.Exp, scale=-1.0), 1.1)
                    yield from at(ACTE, s3, table=ACT.Ln)
                    s4 = ACTE.done(nc.scalar.activation(both, both, ACT.Ln, bias=1.0), 1.1)
                    yield from at(DVE, s4, s2)
                    s5 = DVE.done(nc.vector.tensor_tensor(dt[:, pair:pair + 2, :], both, sp_t[:, :, 1, :], ALU.add), 1.2)
                    maxs.append(s5)
                    yield from at(DVE, s5)
                    u_ready = DVE.done(nc.vector.tensor_tensor(u[:, pair:pair + 2, :], dt[:, pair:pair + 2, :],
                                                               hcv[:, pair:pair + 2, :], ALU.mult), 1.2)
                yield from at(POOL, u_ready, apart=True)
                zeroed = POOL.done(nc.gpsimd.memset(dA[:, :, :, 0:1], 0.0), 0.1)
                yield from at(ACTE, u_ready)
                for c in range(KI):
                    y_ready = ACTE.done(nc.scalar.activation(y[:, c, :], hcv[:, c, :], ACT.Copy, scale=d_skip[:, c:c + 1]))
                b_free, c_free = [None, None], [None, None]
                dA_free, st_free = [None, None], [None, None, None]
                y_acc = [y_ready] * (KI // HC)
                flat = lambda a: a.rearrange("p j s -> p (j s)")
                halves = KI // HC
                steps = NST * halves
                rows_ready, exp_ready, bu_ready = {}, {}, {}

                def spread_rows(n):
                    rows_ready[n] = []
                    for which, free in ((0, b_free), (1, c_free)):
                        bank = ringB.take()
                        yield from at(PE, bank.free, bc_ready)
                        r = which * NST + n
                        md = PE.done(nc.tensor.matmul(bank.t[:, :], pick[:, r:r + 1].broadcast_to([4 * NST, P]),
                                                      bc_parts[:, :], start=True, stop=True), PASS)
                        yield from at(ACTE, md, free[n % 2])
                        bank.free = ACTE.done(nc.scalar.activation(bcb[:, n % 2, which, :], bank.t[:, :], ACT.Copy))
                        rows_ready[n].append(bank.free)

                def prepare(step):
                    n, half = divmod(step, halves)
                    if half == 0:
                        yield from spread_rows(n)
                    yield from at(ACTE, dA_free[step % 2], u_ready, table=ACT.Exp)
                    for j in range(HC):
                        c = half * HC + j
                        exp_ready[step] = ACTE.done(nc.scalar.activation(
                            dA[:, step % 2, j, 1:], dt[:, c, 1:], ACT.Exp, scale=a_neg[:, c, n:n + 1]))
                    lane, cost = (POOL, 2.4) if step % POOL_EVERY == POOL_EVERY - 1 else (DVE, 1.2)
                    yield from at(lane, *rows_ready[n], st_free[step % 3], u_ready)
                    bu_ready[step] = lane.done(lane.e.tensor_tensor(
                        st[:, step % 3, :, :], u[:, half * HC:(half + 1) * HC, :],
                        bcb[:, n % 2, 0:1, :].broadcast_to([P, HC, S]), ALU.mult), cost)
                    b_free[n % 2] = bu_ready[step]

                yield from prepare(0)
                for step in range(steps):
                    if step + 1 < steps:
                        yield from prepare(step + 1)
                    n, half = divmod(step, halves)
                    sv = st[:, step % 3, :, :]
                    yield from at(DVE, bu_ready[step], exp_ready[step], zeroed)
                    sc = DVE.done(nc.vector.tensor_tensor_scan(flat(sv), flat(dA[:, step % 2, :, :]), flat(sv), 0.0,
                                                               ALU.mult, ALU.add), 1.2)
                    dA_free[step % 2] = sc
                    yield from at(DVE, sc)
                    pr = DVE.done(nc.vector.tensor_tensor(
                        sv, sv, bcb[:, n % 2, 1:2, :].broadcast_to([P, HC, S]), ALU.mult), 1.2)
                    c_free[n % 2] = pr
                    yield from at(POOL, pr, y_acc[half])
                    yv = y[:, half * HC:(half + 1) * HC, :]
                    y_acc[half] = POOL.done(nc.gpsimd.tensor_tensor(yv, yv, sv, ALU.add), 2.4)
                    st_free[step % 3] = y_acc[half]
                ended["B.y"] = list(y_acc)
                yield from at(DVE, *y_acc, gate_ready)
                for c in range(0, KI, 2):
                    yg = DVE.done(nc.vector.tensor_tensor(y[:, c:c + 2, :], y[:, c:c + 2, :], gate[:, c:c + 2, :], ALU.mult), 1.2)
                made = yield from token_product(ringB, lambda k: y[:, k, :], lambda k: w_out[:, k, :], KI, D, yg)
                ended["B.out"] = [made[-1][1]]
                for n, (bank, ev) in enumerate(made):
                    tp, xp = pair_of(tokB, n), pair_of(xresB, n)
                    yield from at(DVE, ev, ga_got)
                    a = DVE.done(nc.vector.tensor_tensor(tp, bank_pair(bank), gaB[:, None, :].broadcast_to([P, 2, D]), ALU.mult))
                    bank.free = a
                    yield from at(DVE, a)
                    a = DVE.done(nc.vector.tensor_tensor(xp, xp, tp, ALU.add))
                yield from at(SP, a)
                ended["B.stored"] = [dma("B_store", x_ssm_v[b], xresB[:, :, :])]

            interleave(layer0(0))
            turns("layer0_and_ssm", B - 1, lambda turn: interleave(ssm(turn), layer0(turn + 1)))
            interleave(ssm(B - 1))
            join()

        with ExitStack() as stack:
            sb = sb_in(stack)
            w1 = sb("w1", [P, KD, DH], F32R)
            w2 = sb("w2", [P, KD, DH], F32R)
            h1 = sb("h1", [P, KF, DH], F32R)
            h2 = sb("h2", [P, KF, DH], F32R)
            w3 = sb("w3", [P, KF, D])
            sc_in = sb("sc_in", [P, 4, KF])
            s3_row = sb("s3_row", [P, D])
            with ExitStack() as staging:
                stage_buf = sb_in(staging)("stage3", [P, 4, 1024])
                free = [None] * 4
                j = 0
                for name, dst, nk in (("w1_T", w1, KD), ("w2_T", w2, KD), ("h1_T", h1, KF), ("h2_T", h2, KF)):
                    src = k_tiles(ins[name])
                    for k in range(nk):
                        SP.wait(free[j % 4])
                        got = dma(f"stage{j % 4}", stage_buf[:, j % 4, :], src[:, k, :])
                        DVE.wait(got)
                        free[j % 4] = DVE.done(nc.vector.tensor_copy(dst[:, k, :], stage_buf[:, j % 4, :]))
                        j += 1
                dma("w", w3[:, :, :], k_tiles(ins["w3_T"]))
                for j, name in enumerate(("w1_s", "w2_s", "h1_s", "h2_s")):
                    dma("w", sc_in[:, j, :], ins[f"L1_ffn_{name}"])
                dma("w", s3_row[:, :], over_partitions(ins["L1_ffn_w3_s"]))
                join()
            xres = [sb(f"xresM{i}", [P, TT, D]) for i in range(2)]
            xhat = sb("xhatM", [P, TT, D])
            hTM = sb("hTM", [P, KD, S])
            hTH = [sb(f"hTHM{i}", [P, KD, S], F32R) for i in range(2)]
            hTL = [sb(f"hTLM{i}", [P, KD, S], F32R) for i in range(2)]
            gbM = [sb(f"gbM{i}", [P, D]) for i in range(2)]
            colsM = sb("colsM", [P, NMOD * KD])
            normM = Norm("normM", sb)
            FR = 4
            f_act = sb("f_act", [P, FR, S])
            f_H = [sb(f"f_H{i}", [P, KF, S], F32R) for i in range(2)]
            f_L = [sb(f"f_L{i}", [P, KF, S], F32R) for i in range(2)]
            s_tmp = sb("s_tmp", [P, 2, S])
            tokM = s_tmp[:, :, :].rearrange("p a (t d) -> p (a t) d", d=D)
            ringF, ringM, ringMid = Ring(banks[0:2]), Ring(banks[2:6]), Ring(banks[6:8])

            def mlp_front(b, slot):
                yield from at(SP, *(ended.get(f"M.stored{slot}") or loop.before(f"M.stored{slot}")))
                x_got = dma(f"M_x{slot}", xres[slot][:, :, :], x_ssm_v[b])
                gb_got = dma(f"M_gb{slot}", gbM[slot][:, :], mod_rows[1, b, GB].partition_broadcast(P))
                yield from at(SP, *(ended.get("M.front") or loop.before("M.front")))
                cols = dma("M_cols", colsM[:, :], mod_cols[1, b])

                def col(which, k):
                    return colsM[:, which * KD + k:which * KD + k + 1]

                n1 = yield from layernorm(normM, xres[slot], xhat, x_got)
                up_read = ended.get(f"M.up{slot}") or loop.before(f"M.up{slot}")
                yield from at(ACTE, cols, *up_read)
                yield from at(DVE, *up_read)
                parts = yield from modulated_T(ringF, xhat, n1, lambda k: col(CB, k), lambda k: col(SB_, k),
                                               hTM, hTH[slot], hTL[slot])
                ended[f"M.parts{slot}"] = [e for part in parts for e in part] + [gb_got]
                ended["M.front"] = [parts[-1][0]]

            def mlp_main(b, slot):
                *front, gb_got = ended.get(f"M.parts{slot}") or loop.before(f"M.parts{slot}") or [None] * (3 * KD + 1)
                parts = [front[3 * k:3 * k + 3] for k in range(KD)]
                def ternary(bank, w, m, hi, lo, nk, ready):
                    for k in range(nk):
                        PE.wait(*ready[k])
                        for n, a in enumerate((hi, lo)):
                            i = nc.tensor.matmul(bank.t[:, :], w[:, k, m * P:(m + 1) * P], a[:, k, :],
                                                 start=(k == 0 and n == 0), stop=(k == nk - 1 and n == 1))
                    return PE.done(i, 2 * nk * PASS)

                tmp_free, act_free = [None, None], list(ended.get("M.acts") or loop.before("M.acts") or [None] * FR)
                tok_read = ended.get("M.tok") or loop.before("M.tok")
                prev = []
                for m in range(KF):
                    bank = ringM.take()
                    yield from at(PE, bank.free)
                    md = ternary(bank, w1, m, hTH[slot], hTL[slot], KD, parts)
                    yield from at(ACTE, md, tmp_free[m % 2], *tok_read, table=ACT.Silu)
                    a1 = ACTE.done(nc.scalar.activation(s_tmp[:, m % 2, :], bank.t[:, :], ACT.Silu, scale=sc_in[:, 0, m:m + 1]))
                    bank.free = a1
                    bank = ringM.take()
                    yield from at(PE, bank.free)
                    md = ternary(bank, w2, m, hTH[slot], hTL[slot], KD, parts)
                    act = f_act[:, m % FR, :]
                    yield from at(DVE, md, a1, act_free[m % FR])
                    a2 = DVE.done(nc.vector.scalar_tensor_tensor(
                        out=act, in0=bank.t[:, :], scalar=sc_in[:, 1, m:m + 1], in1=s_tmp[:, m % 2, :],
                        op0=ALU.mult, op1=ALU.mult))
                    bank.free = a2
                    tmp_free[m % 2] = a2
                    halves = yield from split(act, f_H[0][:, m, :], f_L[0][:, m, :], a2)
                    act_free[m % FR] = halves[1]
                    prev.append(halves)
                ended[f"M.up{slot}"] = [md]
                nxt = []
                for m in range(KF):
                    bank = ringM.take()
                    yield from at(PE, bank.free)
                    md = ternary(bank, h1, m, f_H[0], f_L[0], KF, prev)
                    act = f_act[:, m % FR, :]
                    yield from at(ACTE, md, act_free[m % FR], table=ACT.Gelu)
                    a = ACTE.done(nc.scalar.activation(act, bank.t[:, :], ACT.Gelu, scale=sc_in[:, 2, m:m + 1]))
                    bank.free = a
                    halves = yield from split(act, f_H[1][:, m, :], f_L[1][:, m, :], a)
                    act_free[m % FR] = halves[1]
                    nxt.append(halves)
                sums = [ringM.take() for _ in range(TT // 2)]
                acts = []

                def add_tile(m):
                    yield from at(PE, acts[m], *[bank.free for bank in sums] if m == 0 else [])
                    for t in range(TT):
                        i = nc.tensor.matmul(sums[t // 2].t[:, (t % 2) * D:(t % 2 + 1) * D],
                                             f_act[:, m % FR, t * P:(t + 1) * P], w3[:, m, :],
                                             start=(m == 0 and t % 2 == 0), stop=(m == KF - 1), skip_group_check=True)
                    act_free[m % FR] = PE.done(i, 8 * PASS)

                for m in range(KF):
                    bank = ringMid.take()
                    yield from at(PE, bank.free)
                    md = ternary(bank, h2, m, f_H[1], f_L[1], KF, nxt)
                    if m:
                        yield from add_tile(m - 1)
                    yield from at(ACTE, md, act_free[m % FR], table=ACT.Gelu)
                    acts.append(ACTE.done(nc.scalar.activation(f_act[:, m % FR, :], bank.t[:, :], ACT.Gelu,
                                                               scale=sc_in[:, 3, m:m + 1])))
                    bank.free = acts[m]
                yield from add_tile(KF - 1)
                ended["M.acts"] = list(act_free)
                made = [(bank, act_free[(KF - 1) % FR]) for bank in sums]
                for n, (bank, ev) in enumerate(made):
                    tp, xp = pair_of(tokM, n), pair_of(xres[slot], n)
                    yield from at(DVE, ev, gb_got, md)
                    a = DVE.done(nc.vector.tensor_tensor(tp, bank_pair(bank), s3_row[:, None, :].broadcast_to([P, 2, D]), ALU.mult))
                    bank.free = a
                    yield from at(DVE, a)
                    a = DVE.done(nc.vector.tensor_tensor(tp, tp, gbM[slot][:, None, :].broadcast_to([P, 2, D]), ALU.mult))
                    yield from at(DVE, a)
                    a = DVE.done(nc.vector.tensor_tensor(xp, xp, tp, ALU.add))
                ended["M.tok"] = [a]
                yield from at(SP, a)
                ended[f"M.stored{slot}"] = [dma(f"M_store{slot}", out_v[b], xres[slot][:, :, :])]

            def two(turn):
                interleave(mlp_main(turn * 2, 0), mlp_front(turn * 2 + 1, 1))
                interleave(mlp_main(turn * 2 + 1, 1), mlp_front(turn * 2 + 2, 0))

            interleave(mlp_front(0, 0))
            turns("mlp", B // 2 - 1, two)
            interleave(mlp_main(B - 2, 0), mlp_front(B - 1, 1))
            interleave(mlp_main(B - 1, 1))
            join()


TURNED = {"router_T": "L0_ffn_router_w", "w1_T": "L1_ffn_w1_w", "w2_T": "L1_ffn_w2_w",
          "h1_T": "L1_ffn_h1_w", "h2_T": "L1_ffn_h2_w", "w3_T": "L1_ffn_w3_w"}


PER_FEATURE = ["L0_attn_ln_g", "L0_attn_ln_b", "L0_attn_b_hidden", "L1_attn_conv_w", "L1_attn_conv_b",
               "L1_attn_b_dt", "L1_attn_D", "L1_ffn_w1_s", "L1_ffn_w2_s", "L1_ffn_h1_s", "L1_ffn_h2_s"]


def kernel(**inputs):
    import numpy as np
    import concourse.bacc as bacc
    from concourse.bass_utils import run_bass_kernel_spmd

    arrays = {}
    turned_names = set(TURNED.values())
    for name, a in inputs.items():
        if name not in turned_names:
            arrays[name] = np.ascontiguousarray(a)
    for short, name in TURNED.items():
        arrays[short] = np.ascontiguousarray(np.asarray(inputs[name]).T)
    for name in PER_FEATURE:
        a = np.asarray(inputs[name])
        tiles = a.reshape(*[n for n in a.shape[:-1] if n > 1], -1, P)
        arrays[name] = np.ascontiguousarray(np.moveaxis(tiles, -1, 0))
    arrays["os_rows"] = np.ascontiguousarray(
        np.stack([inputs["L0_attn_os_gamma"], inputs["L0_attn_os_beta"]], axis=1))

    def program(counts):
        nc = bacc.Bacc("TRN2", target_bir_lowering=False, num_devices=1)
        aps = {name: nc.dram_tensor(name, a.shape, mybir.dt.from_np(a.dtype), kind="ExternalInput").ap()
               for name, a in arrays.items()}
        out = nc.dram_tensor("x_out", inputs["L0_attn_x"].shape, F32, kind="ExternalOutput").ap()
        adaln_kernel(nc, aps, out, counts)
        return nc

    counts = {}
    program(counts)
    nc = program(counts)
    result = run_bass_kernel_spmd(nc, [arrays], core_ids=[0])
    return result.results[0]["x_out"]
```

```python
from contextlib import ExitStack

import concourse.bass as bass
from concourse import mybir

F32 = mybir.dt.float32
F32R = mybir.dt.float32r
U32 = mybir.dt.uint32
ALU = mybir.AluOpType
ACT = mybir.ActivationFunctionType
AX = mybir.AxisListType

P = 128


class Counts:

    def __init__(self):
        self.per_turn, self.last, self.kinds = {}, {}, []


class Event:

    def __init__(self, sem=None, value=None, at=0.0):
        self.sem, self.value, self.at = sem, value, at

    @property
    def pending(self):
        return self.sem is None


def filled(event, sem, value, at):
    event = event or Event()
    event.sem, event.value, event.at = sem, value, at
    return event


def copy_event(event, into):
    return filled(into, event.sem, event.value, event.at)


class Lane:

    def __init__(self, name, engine, sem, cost, loop):
        self.name, self.e, self.sem, self.cost, self.loop = name, engine, sem, cost, loop
        self.restart()

    def restart(self):
        self.count, self.seen, self.clock, self.table = 0, {}, 0.0, None

    def done(self, instruction, cost=None, into=None):
        instruction.then_inc(self.sem, 1)
        self.count += 1
        self.clock += self.cost if cost is None else cost
        return filled(into, self.sem, self.count, self.clock + SIGNAL_US)

    def wait(self, *events):
        for event in sorted((e for e in events if e is not None), key=lambda e: -e.value):
            if event.value <= self.seen.get(event.sem.name, NEVER):
                continue
            self.e.wait_ge(event.sem, self.loop.value(event))
            self.seen[event.sem.name] = event.value
            self.clock = max(self.clock, event.at)


NEVER = -1 << 30


class Loop:

    def __init__(self):
        self.turn, self.counts = None, None

    def value(self, event):
        if self.turn is None:
            return event.value
        per_turn = self.counts.per_turn.get(event.sem.name, 0)
        return (self.turn + 1) * per_turn + event.value

    def before(self, key):
        if self.turn is None or self.counts is None:
            return []
        return [Event(e.sem, e.value - self.counts.per_turn.get(e.sem.name, 0))
                for e in self.counts.last.get(key, [])]


class Load:

    def __init__(self, sem):
        self.sem = sem
        self.restart()

    def restart(self):
        self.count = 0

    def start(self, lane, out, in_, into=None):
        lane.e.dma_start(out, in_).then_inc(self.sem, 16)
        self.count += 16
        return filled(into, self.sem, self.count, lane.clock + 3.0)


class Bank:

    def __init__(self, tensor):
        self.t, self.held, self.last_read = tensor, False, None

    @property
    def free(self):
        return self.last_read

    @free.setter
    def free(self, event):
        self.held, self.last_read = False, event


class Ring:

    def __init__(self, banks):
        self.banks = banks

    def best(self):
        left = [bank for bank in self.banks if not bank.held]
        return min(left, key=lambda bank: bank.free.at if bank.free else 0.0) if left else None


START_RANK = 1
TABLE_US = 1.0
SAME_US = 0.05
SIGNAL_US = 0.2


def holds(lane, table):
    return table is None or lane.table == table or (table == ACT.Exp and lane.table == ACT.Ln)


class Request:

    def __init__(self, lane, events, table, ring, laid=()):
        self.lane, self.events, self.table, self.ring = lane, [e for e in events if e is not None], table, ring
        self.laid = [e for e in laid if e is not None]

    def answer(self):
        bank = self.ring.best() if self.ring is not None else None
        if bank is not None:
            bank.held = True
        return bank

    def start(self):
        if any(e.pending for e in self.events + self.laid):
            return None
        ready = max([self.lane.clock] + [e.at for e in self.events])
        if self.ring is not None:
            bank = self.ring.best()
            if bank is None:
                return None
            if bank.free:
                ready = max(ready, bank.free.at)
        return ready + (0 if holds(self.lane, self.table) else TABLE_US)


class Choice:

    def __init__(self, choices, events):
        self.requests = [(Request(lane, events, None, None), cost) for lane, cost, _ in choices]
        self.handicaps = [handicap for *_, handicap in choices]

    def start(self):
        if self.requests[0][0].start() is None:
            return None
        return self.best()[0].start()

    def best(self):
        return min(zip(self.requests, self.handicaps), key=lambda r: r[0][0].start() + r[0][1] + r[1])[0]

    def answer(self):
        request, cost = self.best()
        return request.lane, cost


def at(lane, *events, table=None, apart=False, ring=None, laid=()):
    bank = yield Request(lane, events, table, ring, laid)
    lane.wait(*events, bank and bank.free)
    if apart:
        lane.e.nop(nofuse=True)
    if not holds(lane, table):
        lane.clock += TABLE_US
        lane.table = table
    return bank


def either(choices, *events):
    lane, cost = yield Choice(choices, events)
    lane.wait(*events)
    return lane, cost


def start(*stages):
    yield stages


def chain(*stages):
    for stage in stages:
        yield from stage


def urgency(rank):
    yield rank


def interleave(*stages):
    heads = []

    def advance(stage, answer, place, rank):
        started = []
        while True:
            try:
                asked = stage.send(answer)
            except StopIteration:
                break
            if isinstance(asked, (Request, Choice)):
                heads.insert(place, (stage, asked, rank))
                place += 1
                break
            if isinstance(asked, int):
                rank, answer = asked, None
                continue
            started += asked
            answer = None
        for other in started:
            place = advance(other, None, place, rank)
        return place

    for stage in stages:
        advance(stage, None, len(heads), START_RANK)
    while heads:
        ready = [(when // SAME_US, rank, when, n) for n, (_, asked, rank) in enumerate(heads) if (when := asked.start()) is not None]
        *_, n = min(ready)
        stage, asked, rank = heads.pop(n)
        advance(stage, asked.answer(), n, rank)


def adaln_kernel(nc, ins, out, counts):
    B, S, D = ins["L0_attn_x"].shape
    TT = S // P
    KD = D // P
    HID = ins["L0_attn_W_hidden"].shape[1] // 2
    KH = HID // P
    HS = ins["L0_ffn_sw1"].shape[1]
    KS = HS // P
    E, _, HR = ins["L0_ffn_ew1"].shape
    KR = HR // P
    INTER = ins["L1_attn_W_in"].shape[1] // 2
    KI = INTER // P
    NST = ins["L1_attn_A_log"].shape[1]
    DTR = ins["L1_attn_W_dt"].shape[0]
    KC = ins["L1_attn_conv_w"].shape[1]
    PAD = KC - 1
    DH = ins["w1_T"].shape[1]
    KF = DH // P
    HC = KI // 2
    EPS = 1e-5
    NMOD = 6
    SA, CA, GA, SB_, CB, GB = range(NMOD)
    FIRST, LAST = START_RANK - 1, START_RANK + 1
    PASS = 0.215

    def scratch(name, shape):
        return nc.dram_tensor(name, shape, F32, kind="Internal").ap()

    mod_rows = scratch("mod_rows", (2, B, NMOD, D))
    mod_cols = scratch("mod_cols", (2, B, P, NMOD * KD))
    x_ssm = scratch("x_after_ssm", (B, S, D))

    def token_tiles(dram):
        return dram.rearrange("b (t p) d -> b p t d", p=P)

    def k_tiles(weights):
        return weights.rearrange("(k p) n -> p k n", p=P)

    def over_partitions(vector):
        return vector.partition_broadcast(P)

    x_in_v, x_ssm_v, out_v = map(token_tiles, (ins["L0_attn_x"], x_ssm, out))

    with ExitStack() as top:
        def sem(name):
            return top.enter_context(nc.semaphore(name))

        loop = Loop()
        PE = Lane("pe", nc.tensor, sem("pe_done"), 6 * PASS, loop)
        ACTE = Lane("act", nc.scalar, sem("act_done"), 0.62, loop)
        DVE = Lane("dve", nc.vector, sem("dve_done"), 0.68, loop)
        POOL = Lane("pool", nc.gpsimd, sem("pool_done"), 1.25, loop)
        SP = Lane("sp", nc.sync, sem("sp_done"), 0.1, loop)
        lanes = (PE, ACTE, DVE, POOL, SP)
        queues = {}

        def queue(kind):
            if kind not in queues:
                queues[kind] = Load(sem("dma_" + kind))
            return queues[kind]

        def dma(kind, out_, in_, into=None):
            return queue(kind).start(SP, out_, in_, into)

        banks = [Bank(top.enter_context(nc.psum_tensor(f"bank{i}", [P, 512], F32))) for i in range(8)]

        ended = {}

        def carried(key):
            return ended.get(key) or loop.before(key)

        def restart():
            ended.clear()
            for x in (*lanes, *queues.values()):
                x.restart()
            for bank in banks:
                bank.free = None

        def all_sems():
            return [x.sem for x in (*lanes, *queues.values())]

        def join():
            for q in queues.values():
                if q.count:
                    SP.wait(Event(q.sem, q.count))
            nc.all_engine_barrier()
            for s in all_sems():
                nc.sync.sem_clear(s)
            nc.all_engine_barrier()
            restart()

        def turns(name, n, lay_out):
            known = counts.setdefault(name, Counts())
            for kind in known.kinds:
                queue(kind)
            join()
            for s in all_sems():
                if known.per_turn.get(s.name):
                    nc.sync.sem_inc(s, known.per_turn[s.name])
            nc.all_engine_barrier()
            with nc.Fori(0, n) as turn:
                loop.turn, loop.counts = turn, known
                for k, bank in enumerate(banks):
                    bank.free = (loop.before(f"bank{k}") or [None])[0]
                lay_out(turn)
                for k, bank in enumerate(banks):
                    if bank.free is not None:
                        ended[f"bank{k}"] = [bank.free]
            loop.turn = None
            known.per_turn = {x.sem.name: x.count for x in (*lanes, *queues.values())}
            known.last = dict(ended)
            known.kinds = [kind for kind, q in queues.items() if q.count]
            for q in queues.values():
                if q.count:
                    nc.sync.wait_ge(q.sem, (n + 1) * q.count)
            nc.all_engine_barrier()
            for s in all_sems():
                nc.sync.sem_clear(s)
            nc.all_engine_barrier()
            restart()

        def sb_in(stack):
            return lambda name, shape, dt=F32: stack.enter_context(nc.sbuf_tensor(name, shape, dt))

        keep = sb_in(top)
        ident = keep("ident", [P, P])
        minus_half = keep("minus_half", [P, TT])

        class Norm:

            def __init__(self, name, sb):
                self.stat6 = sb(f"{name}_stat6", [P, TT, 6])
                self.stat = sb(f"{name}_stat", [P, TT, 2])
                self.veps = sb(f"{name}_veps", [P, TT])
                self.rstd = sb(f"{name}_rstd", [P, TT])

        def layernorm(norm, x, xhat, x_ready, xhat_free=None):
            yield from at(DVE, x_ready)
            for t in range(TT):
                s6 = DVE.done(nc.vector.bn_stats(norm.stat6[:, t, :], x[:, t, :]), 0.33)
            yield from at(DVE, s6, apart=True)
            for t in range(TT):
                s2 = DVE.done(nc.vector.bn_aggr(norm.stat[:, t, :], norm.stat6[:, t, :]), 0.08)
            yield from at(DVE, s2)
            v = DVE.done(nc.vector.tensor_scalar(norm.veps[:, :], norm.stat[:, :, 1], EPS, None, ALU.add), 0.08)
            yield from at(POOL, v)
            r = POOL.done(nc.gpsimd.tensor_tensor(norm.rstd[:, :], norm.veps[:, :], minus_half[:, :], ALU.pow), 1.0)
            yield from at(DVE, r, xhat_free)
            for t in range(TT):
                done = DVE.done(nc.vector.tensor_scalar(xhat[:, t, :], x[:, t, :], norm.stat[:, t, 0:1],
                                                        norm.rstd[:, t:t + 1], ALU.subtract, ALU.mult), 0.4)
            return done

        def split(full, hi, lo, *ready, into=(None, None)):
            yield from at(DVE, *ready)
            h = DVE.done(nc.vector.tensor_copy(hi, full), 0.34, into=into[0])
            yield from at(DVE, h)
            return h, DVE.done(nc.vector.tensor_tensor(lo, full, hi.bitcast(F32), ALU.subtract), into=into[1])

        def modulated_T(ring, src, src_ready, scale, bias, full, hi, lo, *free):
            parts = [(Event(), Event(), Event()) for _ in range(KD)]

            def feature_tile(k):
                bank = yield from at(PE, src_ready, ring=ring)
                for t in range(TT):
                    i = nc.tensor.transpose(bank.t[:, t * P:(t + 1) * P], src[:, t, k * P:(k + 1) * P], ident[:, :])
                turned = PE.done(i, 1.2)
                yield from at(ACTE, turned, *free)
                m = ACTE.done(nc.scalar.activation(full[:, k, :], bank.t[:, :], ACT.Identity,
                                                   bias=bias(k), scale=scale(k)), into=parts[k][0])
                bank.free = m
                yield from split(full[:, k, :], hi[:, k, :], lo[:, k, :], m, *free, into=parts[k][1:])

            yield from start(*(feature_tile(k) for k in range(KD)))
            return parts

        def of_all(parts):
            return [event for part in parts for event in part]

        def split_product(out_, lhs, rhs, nk):
            for k in range(nk):
                (lh, ll), (rh, rl) = lhs(k), rhs(k)
                for n, (a, b) in enumerate(((lh, rh), (lh, rl), (ll, rh))):
                    i = nc.tensor.matmul(out_, a, b, start=(k == 0 and n == 0), stop=(k == nk - 1 and n == 2))
            return PE.done(i, 3 * nk * PASS)

        def token_product(ring, lhs, rhs, nk, width, *ready, made):
            banks_ = []
            for pair in range(0, TT, 2):
                bank = yield from at(PE, *ready, ring=ring)
                for j in range(2):
                    t = pair + j
                    for k in range(nk):
                        i = nc.tensor.matmul(bank.t[:, j * width:(j + 1) * width], lhs(k)[:, t * P:(t + 1) * P],
                                             rhs(k), start=(k == 0), stop=(k == nk - 1))
                PE.done(i, 4 * nk * PASS, into=made[pair // 2])
                banks_.append(bank)
            return banks_

        def pair_of(tile, pair):
            return tile[:, 2 * pair:2 * pair + 2, :]

        def bank_pair(bank):
            return bank.t[:, :].rearrange("p (t d) -> p t d", t=2)

        def load_split(stage_buf, hi, lo, src, free):
            width, step = src.shape[1], stage_buf.shape[2]
            for c in range(0, width, step):
                w = min(step, width - c)
                n = free["turn"] % 2
                free["turn"] += 1
                slot = stage_buf[:, n, 0:w]
                yield from at(SP, free.get(n))
                got = dma(f"stage{n}", slot, src[:, c:c + w])
                _, free[n] = yield from split(slot, hi[:, c:c + w], lo[:, c:c + w], got)

        def rounded(weights, places):
            free, events = [None] * len(places), []
            width = DH
            for name, dst in weights:
                tiles = width // dst.shape[2]
                for k in range(0, dst.shape[1], tiles):
                    n = len(events) % len(places)
                    place = places[n][:, :, :].rearrange("p a b -> p (a b)").rearrange("p (k n) -> p k n", k=tiles)
                    yield from at(SP, free[n])
                    got = dma(f"stage{n}", place, k_tiles(ins[name])[:, k:k + tiles, :])
                    lane, cost = yield from either([(ACTE, 1.1, 0.0), (DVE, 0.65, 0.0)], got)
                    part = dst[:, k:k + tiles, :]
                    free[n] = lane.done(nc.scalar.activation(part, place, ACT.Copy) if lane is ACTE
                                        else nc.vector.tensor_copy(part, place), cost)
                    events.append(free[n])
            return events

        z = POOL.done(nc.gpsimd.memset(ident[:, :], 0.0))
        POOL.wait(z)
        ident_ready = POOL.done(nc.gpsimd.affine_select(
            out=ident[:, :], in_=ident[:, :], compare_op=ALU.not_equal, fill=1.0, base=0,
            pattern=[[-1, P]], channel_multiplier=1))
        POOL.done(nc.gpsimd.memset(minus_half[:, :], -0.5))

        w1 = keep("w1", [P, KD, DH], F32R)
        h1 = keep("h1", [P, KF, DH], F32R)
        w3 = keep("w3", [P, KF, D], F32R)
        sc_in = keep("sc_in", [P, 4, KF])
        s3_row = keep("s3_row", [P, D])

        with ExitStack() as stack:
            sb = sb_in(stack)
            def rows_of(place, n):
                return place.rearrange("p (k n) -> p k n", k=n)

            w_hid = [h1[:, KD * i:KD * (i + 1), :] for i in range(2)]
            w_qk = [rows_of(h1[:, 2 * KD + i, :], KD) for i in range(2)]
            w_s1 = [rows_of(h1[:, 2 * KD + 2 + i, :], KD) for i in range(2)]
            w_s3 = [rows_of(w1[:, i, :], KD) for i in range(2)]
            w_o = sb("w_o", [P, KH, D])
            w_s2 = sb("w_s2", [P, KS, D])
            w_router = sb("w_router", [P, KD, E])
            lnc = sb("lnc", [P, 2, KD])
            b_hid = sb("b_hid", [P, 2 * KH])
            bqk_row = sb("bqk_row", [P, HID])
            bout_row = sb("bout_row", [P, D])
            rbias_row = sb("rbias_row", [P, E])
            iota_e = sb("iota_e", [P, E])
            w_in = [sb(f"w_in{h}", [P, KD, 2 * INTER], F32R) for h in "HL"]
            w_x = sb("w_x", [P, KI, DTR])
            w_bc = sb("w_bc", [P, KI, 2, 2 * NST])
            w_dt = sb("w_dt", [DTR, INTER])
            w_out = sb("w_out", [P, KI, D])
            conv_w = sb("conv_w", [P, KC, KI])
            conv_b = sb("conv_b", [P, KI])
            b_dt = sb("b_dt", [P, KI])
            d_skip = sb("d_skip", [P, KI])
            a_neg = sb("a_neg", [P, KI, NST])
            pick = sb("pick", [4 * NST, 2 * NST], F32R)
            normA, normB = Norm("normA", sb), Norm("normB", sb)
            with ExitStack() as staging:
                stage_buf = sb_in(staging)("stage1", [P, 2, 2048])
                pick_f = sb_in(staging)("pick_f", [4 * NST, 2 * NST])
                c_tok = sb_in(staging)("c_tok", [B, 2, D])
                c_act = sb_in(staging)("c_act", [B, 2, D])
                cT = sb_in(staging)("cT", [P, 2, KD, B])
                wmod = sb_in(staging)("wmod", [P, 2, KD, NMOD * D])
                rows = sb_in(staging)("rows", [B, 2, NMOD * D])
                sgn = sb_in(staging)("sgn", [B, 2, D])
                mag = sb_in(staging)("mag", [B, 2, D])
                mod_T = sb_in(staging)("mod_T", [P, 2, B, NMOD * KD])


                def first_weights():
                    free = {"turn": 0}
                    for name, parts in (("L0_attn_W_hidden", w_hid), ("L0_attn_W_qk", w_qk), ("L0_ffn_sw1", w_s1),
                                        ("L0_ffn_sw3", w_s3), ("L1_attn_W_in", w_in)):
                        src = k_tiles(ins[name])
                        for k in range(KD):
                            yield from load_split(stage_buf, parts[0][:, k, :], parts[1][:, k, :], src[:, k, :], free)

                def modulation():
                    ring = Ring(banks[0:4])
                    c_got, wmod_got = [], []
                    for l in range(2):
                        c_got.append(dma(f"c{l}", c_tok[:, l, :], ins[f"L{l}_c"]))
                        wmod_got.append(dma(f"wmod{l}", wmod[:, l, :, :], k_tiles(ins[f"L{l}_wmod"])))
                    yield from at(ACTE, *c_got)
                    silu_c = ACTE.done(nc.scalar.activation(c_act[:, :, :], c_tok[:, :, :], ACT.Silu))
                    yield from at(PE, ident_ready, silu_c)
                    bank = yield from at(PE, ring=ring)
                    for l in range(2):
                        for k in range(KD):
                            o = (l * KD + k) * B
                            i = nc.tensor.transpose(bank.t[:, o:o + B], c_act[:, l, k * P:(k + 1) * P], ident[0:B, 0:B])
                    turned = PE.done(i)
                    yield from at(DVE, turned)
                    cT_ready = DVE.done(nc.vector.tensor_copy(
                        cT[:, :, :, :], bank.t[:, 0:2 * KD * B].rearrange("p (l k b) -> p l k b", l=2, k=KD)))
                    bank.free = cT_ready
                    yield from at(PE, cT_ready)
                    for l in range(2):
                        yield from at(PE, wmod_got[l])
                        for c in range(0, NMOD * D, 512):
                            bank = yield from at(PE, ring=ring)
                            for k in range(KD):
                                i = nc.tensor.matmul(bank.t[0:B, :], cT[:, l, k, :], wmod[:, l, k, c:c + 512],
                                                     start=(k == 0), stop=(k == KD - 1))
                            made = PE.done(i)
                            yield from at(DVE, made)
                            copied = DVE.done(nc.vector.tensor_copy(rows[:, l, c:c + 512], bank.t[0:B, :]))
                            bank.free = copied
                    yield from at(DVE, copied)
                    for l in range(2):
                        for which in (CA, CB):
                            r = rows[:, l, which * D:(which + 1) * D]
                            last = DVE.done(nc.vector.tensor_scalar(r, r, 1.0, None, ALU.add))
                    for which in (GA, GB):
                        r = rows[:, :, which * D:(which + 1) * D]
                        yield from at(DVE, last)
                        a = DVE.done(nc.vector.tensor_scalar(sgn[:, :, :], r, 0.0, 2.0, ALU.is_ge, ALU.mult))
                        b = DVE.done(nc.vector.tensor_scalar(mag[:, :, :], r, -1.0, None, ALU.mult))
                        yield from at(DVE, b)
                        c = DVE.done(nc.vector.tensor_tensor(mag[:, :, :], mag[:, :, :], r, ALU.max))
                        yield from at(DVE, c)
                        d = DVE.done(nc.vector.tensor_scalar(mag[:, :, :], mag[:, :, :], 0.25, None, ALU.max))
                        e = DVE.done(nc.vector.tensor_scalar(sgn[:, :, :], sgn[:, :, :], -1.0, None, ALU.add))
                        yield from at(DVE, d, e)
                        last = DVE.done(nc.vector.tensor_tensor(r, sgn[:, :, :], mag[:, :, :], ALU.mult))
                    yield from at(PE, last)
                    for l in range(2):
                        bank = yield from at(PE, ring=ring)
                        for j in range(NMOD * KD):
                            i = nc.tensor.transpose(bank.t[:, j * B:(j + 1) * B], rows[:, l, j * P:(j + 1) * P],
                                                    ident[0:B, 0:B])
                        turned = PE.done(i)
                        yield from at(DVE, turned)
                        bank.free = DVE.done(nc.vector.tensor_copy(
                            mod_T[:, l, :, :].rearrange("p b j -> p j b"),
                            bank.t[:, 0:NMOD * KD * B].rearrange("p (j b) -> p j b", b=B)))
                    yield from at(SP, last, bank.free)
                    for l in range(2):
                        dma("mod", mod_rows[l].rearrange("b j d -> b (j d)"), rows[:, l, :])
                        dma("mod", mod_cols[l].rearrange("b p j -> p b j"), mod_T[:, l, :, :])

                dma("w", w_o[:, :, :], k_tiles(ins["L0_attn_W_out"]))
                dma("w", w_s2[:, :, :], k_tiles(ins["L0_ffn_sw2"]))
                dma("w", w_router[:, :, :], k_tiles(ins["router_T"]))
                dma("w", lnc[:, 0, :], ins["L0_attn_ln_g"])
                dma("w", lnc[:, 1, :], ins["L0_attn_ln_b"])
                dma("w", b_hid[:, :], ins["L0_attn_b_hidden"])
                dma("w", bqk_row[:, :], over_partitions(ins["L0_attn_b_qk"]))
                dma("w", bout_row[:, :], over_partitions(ins["L0_attn_b_out"]))
                dma("w", rbias_row[:, :], over_partitions(ins["L0_ffn_router_bias"]))
                wx = k_tiles(ins["L1_attn_W_x"])
                dma("w", w_x[:, :, :], wx[:, :, 0:DTR])
                for twice in range(2):
                    dma("w", w_bc[:, :, twice, :], wx[:, :, DTR:DTR + 2 * NST])
                dma("w", w_dt[:, :], ins["L1_attn_W_dt"])
                dma("w", w_out[:, :, :], k_tiles(ins["L1_attn_W_out"]))
                dma("w", conv_w[:, :, :], ins["L1_attn_conv_w"])
                dma("w", conv_b[:, :], ins["L1_attn_conv_b"])
                dma("w", b_dt[:, :], ins["L1_attn_b_dt"])
                dma("w", d_skip[:, :], ins["L1_attn_D"])
                al = dma("a_log", a_neg[:, :, :], ins["L1_attn_A_log"].rearrange("(k p) n -> p k n", p=P))
                interleave(modulation(), first_weights())
                ACTE.wait(al)
                ex = ACTE.done(nc.scalar.activation(a_neg[:, :, :], a_neg[:, :, :], ACT.Exp))
                DVE.wait(ex)
                DVE.done(nc.vector.tensor_scalar(a_neg[:, :, :], a_neg[:, :, :], -1.0, None, ALU.mult))
                POOL.done(nc.gpsimd.iota(iota_e[:, :], pattern=[[1, E]], base=0, channel_multiplier=0,
                                         allow_small_or_imprecise_dtypes=True))
                zz = POOL.done(nc.gpsimd.memset(pick_f[:, :], 0.0))
                for shift in (0, 2 * NST):
                    POOL.wait(zz)
                    zz = POOL.done(nc.gpsimd.affine_select(
                        out=pick_f[:, :], in_=pick_f[:, :], compare_op=ALU.not_equal, fill=1.0, base=-shift,
                        pattern=[[-1, 2 * NST]], channel_multiplier=1))
                DVE.wait(zz)
                DVE.done(nc.vector.tensor_copy(pick[:, :], pick_f[:, :]))
                join()

            xresA = sb("xresA", [P, TT, D])
            h_tok = sb("h_tok", [P, TT, D])
            nT = sb("nT", [P, KD, S])
            nTH, nTL = (w3[:, i * KF // 2:(i + 1) * KF // 2, :].rearrange("p (k a) n -> p k (a n)", k=KD) for i in range(2))
            rowsA = sb("rowsA", [P, 4, D])
            colsA = sb("colsA", [P, NMOD * KD])
            q_tok = sb("q_tok", [P, TT, HID])
            v_T = q_tok
            s_act = q_tok
            k_tok = sb("k_tok", [P, TT, HID])
            g_T = k_tok
            e_act = k_tok
            tmpA = sb("tmpA", [P, 2, HID])
            xhatA = tmpA[:, :, :].rearrange("p a (t d) -> p (a t) d", d=D)
            w_e = sb("w_e", [P, 2, 2, KD * HR])
            os_rows = w_e
            smax = sb("smax", [P, KH])
            esum = sb("esum", [P, KH])
            rsum = sb("rsum", [P, KH])
            attn_sum = sb("attn_sum", [P, KH])
            rt = sb("rt", [P, 9, TT, E])
            rt_idx = sb("rt_idx", [P, TT, 8], U32)
            rt_small = sb("rt_small", [P, 4, TT])
            xresB = sb("xresB", [P, TT, D])
            hTH = sb("hTH", [P, KD, S], F32R)
            hTL = sb("hTL", [P, KD, S], F32R)
            gaB = sb("gaB", [P, D])
            colsB = sb("colsB", [P, NMOD * KD])
            RAW = KI * (PAD + S)
            work = sb("work", [P, max(RAW + 6 * S, 2 * HC * S + 3 * HC * S)])
            raw = work[:, 0:RAW].rearrange("p (c s) -> p c s", c=KI)
            cv = work[:, RAW:RAW + 2 * S].rearrange("p (c s) -> p c s", c=2)
            ts = cv[0:DTR, 0, :]
            bc_full = cv[0:4 * NST, 1, :]
            sp_t = work[:, RAW + 2 * S:RAW + 6 * S].rearrange("p (a b s) -> p a b s", a=2, b=2)
            dA = work[:, 0:2 * HC * S].rearrange("p (a j s) -> p a j s", a=2, j=HC)
            st = work[:, 2 * HC * S:5 * HC * S].rearrange("p (a j s) -> p a j s", a=3, j=HC)
            bc_parts = sb("bc_parts", [4 * NST, S], F32R)
            hcv = sb("hcv", [P, KI, S])
            y = hcv
            gate = sb("gate", [P, KI, S])
            dt = sb("dt", [P, KI, S])
            tokB = dt[:, 0:2, :].rearrange("p a (t d) -> p (a t) d", d=D)
            u = sb("u", [P, KI, S])
            xhatB = u[:, 0:2, :].rearrange("p a (t d) -> p (a t) d", d=D)
            hT = u[:, 2:4, :]
            bcb = sb("bcb", [P, 2, 2, S])

            ringA, ringB = Ring(banks[0:4]), Ring(banks[4:8])

            def w_cols(parts, k, c, w=P):
                return parts[0][:, k, c:c + w], parts[1][:, k, c:c + w]

            def rb(which):
                return rowsA[:, which:which + 1, :].broadcast_to([P, TT, D])

            def col(which, k):
                return colsA[:, which * KD + k:which * KD + k + 1]

            up_got, down_got = {}, {}

            def fetch(e, *free):
                yield from at(SP, *free)
                for kind, which, got, name in (("up", 0, up_got, "L0_ffn_ew1"), ("down", 1, down_got, "L0_ffn_ew2")):
                    dma(f"A_{kind}{e % 2}", w_e[:, e % 2, which, :].rearrange("p (k n) -> p k n", n=HR if which == 0 else D),
                        k_tiles(ins[name][e]), into=got[e])

            def attention(b):
                yield from at(SP, *carried("A.x2"))
                x_got = dma("A_x", xresA[:, :, :], x_in_v[b])
                rows_got = [dma("A_rows", rowsA[:, 0:3, :], mod_rows[0, b, 0:3].partition_broadcast(P)),
                            dma("A_gb", rowsA[:, 3:4, :], mod_rows[0, b, 5:6].partition_broadcast(P))]
                cols = dma("A_cols", colsA[:, :], mod_cols[0, b])
                yield from at(SP, x_got, *carried("A.experts"))
                os_got = [dma(f"A_os{j}", os_rows[:, j, :, :], ins["os_rows"][j].partition_broadcast(P)) for j in range(2)]

                n1 = yield from layernorm(normA, xresA, xhatA, x_got)
                yield from at(DVE, n1, *rows_got)
                m1 = DVE.done(nc.vector.tensor_tensor(h_tok[:, :, :], xhatA, rb(1), ALU.mult), 1.2)
                yield from at(DVE, m1)
                h_ready = DVE.done(nc.vector.tensor_tensor(h_tok[:, :, :], h_tok[:, :, :], rb(0), ALU.add), 1.2)
                n2 = yield from layernorm(normA, h_tok, xhatA, h_ready, m1)
                parts = yield from modulated_T(ringA, xhatA, n2, lambda k: lnc[:, 0, k:k + 1],
                                               lambda k: lnc[:, 1, k:k + 1], nT, nTH, nTL, *carried("A.experts"))
                qk_ready = [(Event(), Event()) for _ in range(TT)]
                scaled = [(Event(), Event()) for _ in range(TT)]

                def qk_tile(t):
                    bank = yield from at(PE, *of_all(parts), ring=ringA)
                    made = split_product(bank.t[:, :], lambda k: (nTH[:, k, t * P:(t + 1) * P], nTL[:, k, t * P:(t + 1) * P]),
                                         lambda k: w_cols(w_qk, k, 0, HID), KD)
                    tmp = tmpA[:, t % 2, :]
                    yield from at(DVE, made, *(scaled[t - 2] if t >= 2 else []))
                    biased = DVE.done(nc.vector.tensor_tensor(tmp, bank.t[:, :], bqk_row[:, :], ALU.add))
                    bank.free = biased
                    yield from at(ACTE, biased, table=ACT.Silu)
                    act = ACTE.done(nc.scalar.activation(tmp, tmp, ACT.Silu))
                    for which, lane, dst in ((0, DVE, q_tok), (1, POOL, k_tok)):
                        yield from start(scale_tile(t, act, which, lane, dst[:, t, :], tmp))

                def scale_tile(t, act, which, lane, dst, tmp):
                    yield from at(lane, act, *os_got)
                    m = lane.done(lane.e.tensor_tensor(dst, tmp, os_rows[:, which, 0, :], ALU.mult), into=scaled[t][which])
                    yield from at(lane, m)
                    lane.done(lane.e.tensor_tensor(dst, dst, os_rows[:, which, 1, :], ALU.add), into=qk_ready[t][which])

                yield from start(*(qk_tile(t) for t in range(TT)))
                for e in range(2):
                    up_got[e], down_got[e] = Event(), Event()
                    yield from fetch(e, *of_all(qk_ready))
                sims, exps = [Event() for _ in range(KH)], [Event() for _ in range(KH)]

                def sim_tile(d):
                    bank = yield from at(PE, *of_all(qk_ready), ring=ringA)
                    for t in range(TT):
                        i = nc.tensor.matmul(bank.t[:, :], q_tok[:, t, d * P:(d + 1) * P], k_tok[:, t, :],
                                             start=(t == 0), stop=(t == TT - 1))
                    PE.done(i, 4 * TT * PASS, into=sims[d])
                    yield from at(DVE, sims[d])
                    mx = DVE.done(nc.vector.tensor_reduce(smax[:, d:d + 1], bank.t[:, :], AX.X, ALU.max))
                    yield from at(DVE, mx)
                    neg = DVE.done(nc.vector.tensor_scalar(smax[:, d:d + 1], smax[:, d:d + 1], -1.0 / S, None, ALU.mult), 0.1)
                    yield from at(ACTE, neg, sims[d], table=ACT.Exp)
                    bank.free = ACTE.done(nc.scalar.activation(bank.t[:, :], bank.t[:, :], ACT.Exp, bias=smax[:, d:d + 1],
                                                               scale=1.0 / S, accum_out=esum[:, d:d + 1]), into=exps[d])

                hidden = [(Event(), Event()) for _ in range(KH)]

                def hidden_tile(d, half, dst):
                    bank = yield from at(PE, *of_all(parts), ring=ringA)
                    made = split_product(bank.t[:, :], lambda k: w_cols(w_hid, k, half * HID + d * P),
                                         lambda k: (nTH[:, k, :], nTL[:, k, :]), KD)
                    j = half * KH + d
                    yield from at(ACTE, made, *sims, table=ACT.Silu)
                    bank.free = ACTE.done(nc.scalar.activation(dst[:, d, :], bank.t[:, :], ACT.Silu, bias=b_hid[:, j:j + 1]),
                                          into=hidden[d][half])

                def hidden_tiles():
                    for d in range(KH):
                        for half, dst in ((0, v_T), (1, g_T)):
                            yield from hidden_tile(d, half, dst)

                yield from start(*(sim_tile(d) for d in range(KH)), hidden_tiles())
                yield from at(DVE, *exps)
                rc = DVE.done(nc.vector.reciprocal(rsum[:, :], esum[:, :]), 0.1)
                yield from at(DVE, rc)
                asum = DVE.done(nc.vector.tensor_tensor(attn_sum[:, :], esum[:, :], rsum[:, :], ALU.mult), 0.1)
                gated = []
                for d in range(KH):
                    yield from at(DVE, asum, *hidden[d])
                    gated.append(DVE.done(nc.vector.scalar_tensor_tensor(
                        out=v_T[:, d, :], in0=v_T[:, d, :], scalar=attn_sum[:, d:d + 1], in1=g_T[:, d, :],
                        op0=ALU.mult, op1=ALU.mult)))
                yield from at(POOL, n2)
                i1 = POOL.done(nc.gpsimd.tensor_tensor(h_tok[:, :, :], h_tok[:, :, :],
                                                       bout_row[:, None, :].broadcast_to([P, TT, D]), ALU.add), 2.4)
                made = [Event() for _ in range(TT // 2)]
                outs = yield from token_product(ringA, lambda k: v_T[:, k, :], lambda k: w_o[:, k, :], KH, D, *gated, made=made)
                wo_done = made[-1]
                for n, (bank, ev) in enumerate(zip(outs, made)):
                    hp, xp = pair_of(h_tok, n), pair_of(xresA, n)
                    yield from at(DVE, ev, i1)
                    i2 = DVE.done(nc.vector.tensor_tensor(hp, hp, bank_pair(bank), ALU.add))
                    bank.free = i2
                    yield from at(DVE, i2)
                    i3 = DVE.done(nc.vector.tensor_tensor(hp, hp, rowsA[:, 2:3, :].broadcast_to([P, 2, D]), ALU.mult))
                    yield from at(DVE, i3)
                    x1 = DVE.done(nc.vector.tensor_tensor(xp, xp, hp, ALU.add))
                ended["A.x1"] = [x1]
                ended["A.wo"] = [wo_done]
                ended["A.cols"] = [cols]
                ended["A.gb"] = rows_got[1:]
                ended["A.weights"] = [up_got[0], down_got[0], up_got[1], down_got[1]]

            def feed_forward(b, xresB_free=None):
                (x1,), (wo_done,), (cols,), (gb_got,) = (carried(f"A.{key}") or [None] for key in ("x1", "wo", "cols", "gb"))
                up_got[0], down_got[0], up_got[1], down_got[1] = carried("A.weights") or [None] * 4
                n3 = yield from layernorm(normA, xresA, xhatA, x1)
                yield from at(ACTE, cols)
                parts = yield from modulated_T(ringA, xhatA, n3, lambda k: col(CB, k), lambda k: col(SB_, k),
                                               nT, nTH, nTL, wo_done)
                rbank = yield from at(PE, *(part[0] for part in parts), ring=ringA)
                for t in range(TT):
                    for k in range(KD):
                        i = nc.tensor.matmul(rbank.t[:, t * E:(t + 1) * E], nT[:, k, t * P:(t + 1) * P], w_router[:, k, :],
                                             start=(k == 0), stop=(k == KD - 1))
                routed = PE.done(i, 0.8)
                scores_sig = rt[:, 0, :, :]
                yield from at(ACTE, routed, table=ACT.Sigmoid)
                sig = ACTE.done(nc.scalar.activation(
                    scores_sig, rbank.t[:, 0:TT * E].rearrange("p (t e) -> p t e", t=TT), ACT.Sigmoid), 0.2)
                rbank.free = sig

                def route():
                    sg, sel, oh1, oh2, msk, scored, comb, ix = (rt[:, j, :, :] for j in (0, 1, 3, 4, 5, 6, 7, 8))
                    small = 0.1
                    yield from at(DVE, sig)
                    a = DVE.done(nc.vector.tensor_tensor(sel, sg, rbias_row[:, None, :].broadcast_to([P, TT, E]), ALU.add), small)
                    yield from at(DVE, a, apart=True)
                    for t in range(TT):
                        a = DVE.done(nc.vector.max(rt[:, 2, t, :], rt[:, 1, t, :]), small)
                    yield from at(DVE, a, apart=True)
                    for t in range(TT):
                        a = DVE.done(nc.vector.max_index(rt_idx[:, t, :], rt[:, 2, t, :], rt[:, 1, t, :]), small)
                    yield from at(DVE, a)
                    a = DVE.done(nc.vector.tensor_copy(ix, rt_idx[:, :, :]), small)
                    yield from at(DVE, a)
                    iob = iota_e[:, None, :].broadcast_to([P, TT, E])
                    DVE.done(nc.vector.tensor_tensor(oh1, rt[:, 8, :, 0:1].broadcast_to([P, TT, E]), iob, ALU.is_equal), small)
                    a = DVE.done(nc.vector.tensor_tensor(oh2, rt[:, 8, :, 1:2].broadcast_to([P, TT, E]), iob, ALU.is_equal), small)
                    yield from at(DVE, a)
                    a = DVE.done(nc.vector.tensor_tensor(msk, oh1, oh2, ALU.add), small)
                    yield from at(DVE, a)
                    a = DVE.done(nc.vector.tensor_tensor(scored, msk, sg, ALU.mult), small)
                    yield from at(DVE, a)
                    den, ok, rden, half_ = (rt_small[:, j, :] for j in range(4))
                    a = DVE.done(nc.vector.tensor_reduce(den, scored, AX.X, ALU.add), small)
                    yield from at(DVE, a)
                    DVE.done(nc.vector.tensor_scalar(ok, den, 1e-9, None, ALU.is_gt), small)
                    DVE.done(nc.vector.tensor_scalar(half_, den, 1e-9, 0.5, ALU.is_le, ALU.mult), small)
                    a = DVE.done(nc.vector.tensor_scalar(den, den, 1e-9, None, ALU.add), small)
                    yield from at(DVE, a)
                    a = DVE.done(nc.vector.reciprocal(rden, den), small)
                    yield from at(DVE, a)
                    a = DVE.done(nc.vector.tensor_tensor(rden, rden, ok, ALU.mult), small)
                    yield from at(DVE, a)
                    bc = lambda j: rt_small[:, j, :, None].broadcast_to([P, TT, E])
                    DVE.done(nc.vector.tensor_tensor(scored, scored, bc(2), ALU.mult), small)
                    a = DVE.done(nc.vector.tensor_tensor(msk, msk, bc(3), ALU.mult), small)
                    yield from at(DVE, a)
                    DVE.done(nc.vector.tensor_tensor(comb, scored, msk, ALU.add), small, into=comb_ready)

                s_parts = [Event() for _ in range(KS)]

                def shared_tile(m):
                    bank = yield from at(PE, *of_all(parts), ring=ringA)
                    made = split_product(bank.t[:, :], lambda k: w_cols(w_s1, k, m * P),
                                         lambda k: (nTH[:, k, :], nTL[:, k, :]), KD)
                    yield from at(ACTE, made, s_parts[m - 2] if m >= 2 else None, table=ACT.Silu)
                    a1 = ACTE.done(nc.scalar.activation(tmpA[:, m % 2, :], bank.t[:, :], ACT.Silu))
                    bank.free = a1
                    bank = yield from at(PE, *of_all(parts), ring=ringA)
                    made = split_product(bank.t[:, :], lambda k: w_cols(w_s3, k, m * P),
                                         lambda k: (nTH[:, k, :], nTL[:, k, :]), KD)
                    yield from at(DVE, made, a1)
                    bank.free = DVE.done(nc.vector.tensor_tensor(s_act[:, m, :], bank.t[:, :], tmpA[:, m % 2, :], ALU.mult),
                                         into=s_parts[m])

                comb_ready = Event()
                summed = [[Event() for _ in range(TT)] for _ in range(E + 1)]

                def shared():
                    yield from start(*(shared_tile(m) for m in range(KS)))
                    made = [Event() for _ in range(TT // 2)]
                    outs = yield from token_product(ringA, lambda k: s_act[:, k, :], lambda k: w_s2[:, k, :], KS, D,
                                                    *s_parts, made=made)
                    for n, (bank, ev) in enumerate(zip(outs, made)):
                        yield from at(ACTE, ev, x1)
                        bank.free = ACTE.done(nc.scalar.activation(pair_of(h_tok, n), bank_pair(bank), ACT.Copy),
                                              into=summed[0][2 * n])
                        copy_event(summed[0][2 * n], summed[0][2 * n + 1])

                acts = [[Event() for _ in range(KR)] for _ in range(E)]
                downs = [[Event() for _ in range(TT // 2)] for _ in range(E)]

                def experts_up():
                    for e in range(E):
                        for m in range(KR):
                            bank = yield from at(PE, *(part[0] for part in parts), up_got[e], ring=ringA)
                            for k in range(KD):
                                c = k * HR + m * P
                                i = nc.tensor.matmul(bank.t[:, :], w_e[:, e % 2, 0, c:c + P], nT[:, k, :],
                                                     start=(k == 0), stop=(k == KD - 1))
                            made = PE.done(i, 4 * KD * PASS)
                            yield from at(ACTE, made, *(downs[e - 2] if e >= 2 else []), table=ACT.Gelu)
                            bank.free = ACTE.done(nc.scalar.activation(e_act[:, (e % 2) * KR + m, :], bank.t[:, :], ACT.Gelu),
                                                  into=acts[e][m])

                def experts_down():
                    for e in range(E):
                        outs = yield from token_product(
                            ringA, lambda k: e_act[:, (e % 2) * KR + k, :], lambda k: w_e[:, e % 2, 1, k * D:(k + 1) * D],
                            KR, D, down_got[e], *acts[e], made=downs[e])
                        yield from start(weighted(e, outs))
                        if e + 2 < E:
                            yield from start(fetch(e + 2, downs[e][-1]))

                def weighted(e, outs):
                    for n, (bank, ev) in enumerate(zip(outs, downs[e])):
                        for j in range(2):
                            t = 2 * n + j
                            yield from at(DVE, ev, comb_ready, summed[e][t], summed[0][t])
                            DVE.done(nc.vector.scalar_tensor_tensor(
                                out=h_tok[:, t, :], in0=bank.t[:, j * D:(j + 1) * D], scalar=rt[:, 7, t, e:e + 1],
                                in1=h_tok[:, t, :], op0=ALU.mult, op1=ALU.add), 0.4, into=summed[e + 1][t])
                        bank.free = summed[e + 1][t]

                for e in range(2, E):
                    up_got[e], down_got[e] = Event(), Event()
                yield from start(shared(), route(), experts_up(), experts_down())
                yield from at(DVE, *summed[E])
                ended["A.experts"] = downs[-1]
                yield from at(DVE, gb_got)
                a = DVE.done(nc.vector.tensor_tensor(h_tok[:, :, :], h_tok[:, :, :], rb(3), ALU.mult), 1.2)
                yield from at(DVE, a, xresB_free)
                x2 = DVE.done(nc.vector.tensor_tensor(xresB[:, :, :], xresA[:, :, :], h_tok[:, :, :], ALU.add), 1.2)
                ended["A.x2"] = [x2]

            input_lanes = [(POOL, 2.35, 0.0), (DVE, 1.15, 1.0)]
            sum_lanes = [(POOL, 2.35, 0.0), (DVE, 1.15, 3.0)]

            def ssm(b, x_read):
                yield from urgency(FIRST)
                ga_got = dma("B_ga", gaB[:, :], mod_rows[1, b, GA].partition_broadcast(P))
                cols = dma("B_cols", colsB[:, :], mod_cols[1, b])

                def col(which, k):
                    return colsB[:, which * KD + k:which * KD + k + 1]

                y_last, out_read, stored_before = carried("B.y"), carried("B.out"), carried("B.stored")
                yield from at(POOL, *y_last, apart=True)
                pad_zero = POOL.done(nc.gpsimd.memset(raw[:, :, 0:PAD], 0.0), 0.1)
                yield from at(DVE, *y_last)
                n1 = yield from layernorm(normB, xresB, xhatB, *carried("A.x2") or [None])
                yield from at(ACTE, cols, *out_read, *y_last)
                parts = yield from modulated_T(ringB, xhatB, n1, lambda k: col(CA, k), lambda k: col(SA, k), hT, hTH, hTL)
                hs = [Event() for _ in range(KI)]
                gates = [Event() for _ in range(KI)]

                def conv_tile(c):
                    bank = yield from at(PE, *of_all(parts), ring=ringB)
                    made = split_product(bank.t[:, :], lambda k: w_cols(w_in, k, c * P),
                                         lambda k: (hTH[:, k, :], hTL[:, k, :]), KD)
                    yield from at(ACTE, made)
                    bank.free = rw = ACTE.done(nc.scalar.activation(raw[:, c, PAD:], bank.t[:, :], ACT.Copy))
                    o = cv[:, c % 2, :]
                    yield from at(DVE, rw, pad_zero, hs[c - 2] if c >= 2 else None)
                    a = DVE.done(nc.vector.tensor_scalar(o, raw[:, c, 0:S], conv_w[:, 0, c:c + 1], None, ALU.mult), 0.4)
                    for tap in range(1, KC):
                        yield from at(DVE, a)
                        a = DVE.done(nc.vector.scalar_tensor_tensor(
                            out=o, in0=raw[:, c, tap:tap + S], scalar=conv_w[:, tap, c:c + 1], in1=o,
                            op0=ALU.mult, op1=ALU.add))
                    yield from at(ACTE, a, table=ACT.Silu)
                    ACTE.done(nc.scalar.activation(hcv[:, c, :], cv[:, c % 2, :], ACT.Silu, bias=conv_b[:, c:c + 1]), into=hs[c])

                def gate_tile(c):
                    bank = yield from at(PE, *of_all(parts), ring=ringB)
                    made = split_product(bank.t[:, :], lambda k: w_cols(w_in, k, INTER + c * P),
                                         lambda k: (hTH[:, k, :], hTL[:, k, :]), KD)
                    yield from at(ACTE, made, table=ACT.Silu)
                    bank.free = ACTE.done(nc.scalar.activation(gate[:, c, :], bank.t[:, :], ACT.Silu), into=gates[c])

                yield from start(*(conv_tile(c) for c in range(KI)), chain(*(gate_tile(c) for c in range(KI))))
                ts_ready, bc_ready = Event(), Event()

                def dt_inputs():
                    bank = yield from at(PE, *hs, ring=ringB)
                    for k in range(KI):
                        i = nc.tensor.matmul(bank.t[0:DTR, :], w_x[:, k, :], hcv[:, k, :], start=(k == 0), stop=(k == KI - 1))
                    md = PE.done(i, 4 * KI * PASS)
                    yield from at(ACTE, md)
                    bank.free = ACTE.done(nc.scalar.activation(ts, bank.t[0:DTR, :], ACT.Copy), into=ts_ready)

                def b_and_c():
                    bank = yield from at(PE, *hs, ring=ringB)
                    for k in range(KI):
                        i = nc.tensor.matmul(bank.t[0:4 * NST, :], w_bc[:, k, :, :].rearrange("p a n -> p (a n)"),
                                             hcv[:, k, :], start=(k == 0), stop=(k == KI - 1))
                    md = PE.done(i, 4 * KI * PASS)
                    yield from at(ACTE, md)
                    f = ACTE.done(nc.scalar.activation(bc_full, bank.t[0:4 * NST, :], ACT.Copy))
                    bank.free = f
                    yield from at(DVE, f)
                    p1 = DVE.done(nc.vector.tensor_copy(bc_parts[:, :], bc_full))
                    yield from at(DVE, p1)
                    low = slice(2 * NST, 4 * NST)
                    DVE.done(nc.vector.tensor_tensor(bc_parts[low, :], cv[low, 1, :], bc_parts[low, :].bitcast(F32), ALU.subtract),
                             into=bc_ready)

                u_pair = [Event() for _ in range(KI // 2)]
                dt_pair = [Event() for _ in range(KI // 2)]

                def softplus_pair(n):
                    pair = 2 * n
                    for c in (pair, pair + 1):
                        bank = yield from at(PE, ts_ready, ring=ringB)
                        md = PE.done(nc.tensor.matmul(bank.t[:, :], w_dt[:, c * P:(c + 1) * P], ts, start=True, stop=True), 4 * PASS)
                        ab, mx = sp_t[:, c % 2, 0, :], sp_t[:, c % 2, 1, :]
                        yield from at(ACTE, md, dt_pair[n - 1] if n else None)
                        s1 = ACTE.done(nc.scalar.activation(ab, bank.t[:, :], ACT.Abs, bias=b_dt[:, c:c + 1]))
                        s2 = ACTE.done(nc.scalar.activation(mx, bank.t[:, :], ACT.Relu, bias=b_dt[:, c:c + 1]))
                        bank.free = s2
                    both = sp_t[:, :, 0, :]
                    yield from at(ACTE, s1, table=ACT.Exp)
                    s3 = ACTE.done(nc.scalar.activation(both, both, ACT.Exp, scale=-1.0), 1.1)
                    yield from at(ACTE, s3, table=ACT.Ln)
                    s4 = ACTE.done(nc.scalar.activation(both, both, ACT.Ln, bias=1.0), 1.1)
                    yield from at(DVE, s4, s2)
                    yield from at(DVE, *stored_before)
                    s5 = DVE.done(nc.vector.tensor_tensor(dt[:, pair:pair + 2, :], both, sp_t[:, :, 1, :], ALU.add), 1.2,
                                  into=dt_pair[n])
                    yield from at(DVE, s5)
                    DVE.done(nc.vector.tensor_tensor(u[:, pair:pair + 2, :], dt[:, pair:pair + 2, :], hcv[:, pair:pair + 2, :],
                                                     ALU.mult), 1.2, into=u_pair[n])

                yield from start(dt_inputs(), b_and_c(), chain(*(softplus_pair(n) for n in range(KI // 2))))
                yield from at(POOL, *u_pair, bc_ready, apart=True)
                zeroed = POOL.done(nc.gpsimd.memset(dA[:, :, :, 0:1], 0.0), 0.1)
                yield from at(ACTE, *u_pair)
                for c in range(KI):
                    y_ready = ACTE.done(nc.scalar.activation(y[:, c, :], hcv[:, c, :], ACT.Copy, scale=d_skip[:, c:c + 1]))
                yield from urgency(LAST)
                flat = lambda a: a.rearrange("p j s -> p (j s)")
                halves = KI // HC
                steps = NST * halves
                b_rows, c_rows = [Event() for _ in range(NST)], [Event() for _ in range(NST)]
                exped, input_made, scanned, weighed, summed = ([Event() for _ in range(steps)] for _ in range(5))

                def of_step(events, step):
                    return events[step] if step >= 0 else None

                def spread(rows, which, readers):
                    for n in range(NST):
                        bank = yield from at(PE, bc_ready, ring=ringB)
                        r = which * NST + n
                        md = PE.done(nc.tensor.matmul(bank.t[:, :], pick[:, r:r + 1].broadcast_to([4 * NST, P]),
                                                      bc_parts[:, :], start=True, stop=True), PASS)
                        yield from at(ACTE, md, *(of_step(readers, (n - 2) * halves + h) for h in range(halves)))
                        bank.free = ACTE.done(nc.scalar.activation(bcb[:, n % 2, which, :], bank.t[:, :], ACT.Copy), into=rows[n])

                def decays():
                    for step in range(steps):
                        n, half = divmod(step, halves)
                        yield from at(ACTE, of_step(scanned, step - 2), *u_pair, table=ACT.Exp)
                        for j in range(HC):
                            c = half * HC + j
                            ACTE.done(nc.scalar.activation(dA[:, step % 2, j, 1:], dt[:, c, 1:], ACT.Exp,
                                                           scale=a_neg[:, c, n:n + 1]), into=exped[step])

                def inputs():
                    for step in range(steps):
                        n, half = divmod(step, halves)
                        lane, cost = yield from either(input_lanes, b_rows[n], of_step(summed, step - 3), *u_pair, bc_ready)
                        lane.done(lane.e.tensor_tensor(
                            st[:, step % 3, :, :], u[:, half * HC:(half + 1) * HC, :],
                            bcb[:, n % 2, 0:1, :].broadcast_to([P, HC, S]), ALU.mult), cost, into=input_made[step])

                def scans():
                    for step in range(steps):
                        sv = st[:, step % 3, :, :]
                        yield from at(DVE, input_made[step], exped[step], zeroed)
                        DVE.done(nc.vector.tensor_tensor_scan(flat(sv), flat(dA[:, step % 2, :, :]), flat(sv), 0.0,
                                                              ALU.mult, ALU.add), 1.1, into=scanned[step])

                def weighings():
                    for step in range(steps):
                        sv = st[:, step % 3, :, :]
                        yield from at(DVE, scanned[step], c_rows[step // halves])
                        DVE.done(nc.vector.tensor_tensor(sv, sv, bcb[:, step // halves % 2, 1:2, :].broadcast_to([P, HC, S]),
                                                         ALU.mult), 1.15, into=weighed[step])

                def sums():
                    for step in range(steps):
                        half = step % halves
                        yv = y[:, half * HC:(half + 1) * HC, :]
                        lane, cost = yield from either(sum_lanes, weighed[step], of_step(summed, step - halves), y_ready)
                        lane.done(lane.e.tensor_tensor(yv, yv, st[:, step % 3, :, :], ALU.add), cost, into=summed[step])

                yield from start(spread(b_rows, 0, input_made), spread(c_rows, 1, weighed), decays(), scans(), weighings(),
                                 inputs(), sums())
                yield from at(DVE, *summed[-halves:], *gates)
                ended["B.y"] = summed[-halves:]
                yield from urgency(FIRST)
                for c in range(0, KI, 2):
                    yg = DVE.done(nc.vector.tensor_tensor(y[:, c:c + 2, :], y[:, c:c + 2, :], gate[:, c:c + 2, :], ALU.mult), 1.2)
                made = [Event() for _ in range(TT // 2)]
                outs = yield from token_product(ringB, lambda k: y[:, k, :], lambda k: w_out[:, k, :], KI, D, yg, made=made)
                ended["B.out"] = made[-1:]
                for n, (bank, ev) in enumerate(zip(outs, made)):
                    tp, xp = pair_of(tokB, n), pair_of(xresB, n)
                    yield from at(DVE, ev, ga_got)
                    a = DVE.done(nc.vector.tensor_tensor(tp, bank_pair(bank), gaB[:, None, :].broadcast_to([P, 2, D]), ALU.mult))
                    bank.free = a
                    yield from at(DVE, a)
                    a = DVE.done(nc.vector.tensor_tensor(tp, tp, xp, ALU.add), into=x_read if n else None)
                yield from at(SP, a)
                ended["B.stored"] = [dma("B_store", x_ssm_v[b], tokB)]

            interleave(chain(attention(0), feed_forward(0)))

            def layer0_and_ssm(turn):
                x_read = Event()
                interleave(chain(attention(turn + 1), feed_forward(turn + 1, x_read)), ssm(turn, x_read))

            turns("layer0_and_ssm", B - 1, layer0_and_ssm)

            def first_mlp_weights():
                yield from urgency(LAST + 1)
                for j, name in enumerate(("w1_s", "w2_s", "h1_s", "h2_s")):
                    dma("w", sc_in[:, j, :], ins[f"L1_ffn_{name}"])
                dma("w", s3_row[:, :], over_partitions(ins["L1_ffn_w3_s"]))
                yield from rounded((("w1_T", w1), ("h1_T", h1), ("w3_T", w3)), [nT, rowsA, tmpA])

            interleave(ssm(B - 1, Event()), first_mlp_weights())
            join()

        with ExitStack() as stack:
            sb = sb_in(stack)
            w2 = sb("w2", [P, KD, DH], F32R)
            h2 = sb("h2", [P, KF, DH], F32R)
            xres = [sb(f"xresM{i}", [P, TT, D]) for i in range(2)]
            gbM = [sb(f"gbM{i}", [P, D]) for i in range(2)]
            xhat = sb("xhatM", [P, TT, D])
            hTM = sb("hTM", [P, KD, S])
            hTH = sb("hTHM", [P, KD, S], F32R)
            hTL = sb("hTLM", [P, KD, S], F32R)
            colsM = sb("colsM", [P, NMOD * KD])
            normM = Norm("normM", sb)
            silu_w1 = sb("silu_w1", [P, 2, S])
            up_full = sb("up_full", [P, 2, S])
            mid_full = sb("mid_full", [P, 2, S])
            f_H = [sb(f"f_H{i}", [P, KF, S], F32R) for i in range(2)]
            f_L = [sb(f"f_L{i}", [P, KF, S], F32R) for i in range(2)]
            last_H = sb("last_H", [P, 2, S], F32R)
            last_L = sb("last_L", [P, 2, S], F32R)
            tokM = sb("tokM", [P, TT, D])
            ring_up, ring_mid, ring_sums = Ring(banks[0:3]), Ring(banks[3:6]), Ring(banks[6:8])

            def ternary(bank, w, m, hi, lo, nk, ready, into=None):
                for k in range(nk):
                    PE.wait(*ready[k])
                    for n, a in enumerate((hi, lo)):
                        i = nc.tensor.matmul(bank.t[:, :], w[:, k, m * P:(m + 1) * P], a[:, k, :],
                                             start=(k == 0 and n == 0), stop=(k == nk - 1 and n == 1))
                return PE.done(i, 2 * nk * PASS, into=into)

            def two_before(tiles, m, before):
                return (tiles if m >= 2 else before)[m - 2]

            def mlp_up(b, slot, stored, front_before, halves_before, up_before, f_read, front, got, halves, up_read, w2_got):
                yield from at(SP, stored)
                x_got = dma(f"M_x{slot}", xres[slot][:, :, :], x_ssm_v[b])
                dma(f"M_gb{slot}", gbM[slot][:, :], mod_rows[1, b, GB].partition_broadcast(P), into=got)
                yield from at(SP, *front_before)
                cols = dma("M_cols", colsM[:, :], mod_cols[1, b])

                def col(which, k):
                    return colsM[:, which * KD + k:which * KD + k + 1]

                yield from at(DVE, *front_before, up_before)
                n1 = yield from layernorm(normM, xres[slot], xhat, x_got)
                yield from at(ACTE, cols, *front_before)
                parts = yield from modulated_T(ring_up, xhat, n1, lambda k: col(CB, k), lambda k: col(SB_, k),
                                               hTM, hTH, hTL)
                yield from at(PE, *of_all(parts))
                for part, event in zip(of_all(parts), front):
                    copy_event(part, event)
                for m in range(KF):
                    bank = yield from at(PE, ring=ring_up)
                    md = ternary(bank, w1, m, hTH, hTL, KD, parts)
                    yield from at(ACTE, md, *two_before(halves, m, halves_before), table=ACT.Silu)
                    a1 = ACTE.done(nc.scalar.activation(silu_w1[:, m % 2, :], bank.t[:, :], ACT.Silu, scale=sc_in[:, 0, m:m + 1]))
                    bank.free = a1
                    bank = yield from at(PE, *w2_got, ring=ring_up)
                    md = ternary(bank, w2, m, hTH, hTL, KD, parts, into=up_read if m == KF - 1 else None)
                    yield from start(gate_and_split(m, bank, md, a1, f_read, halves, halves_before))

            def gate_and_split(m, bank, md, a1, f_read, halves, halves_before):
                full = up_full[:, m % 2, :]
                yield from at(DVE, md, a1, *two_before(halves, m, halves_before))
                a2 = DVE.done(nc.vector.scalar_tensor_tensor(
                    out=full, in0=bank.t[:, :], scalar=sc_in[:, 1, m:m + 1], in1=silu_w1[:, m % 2, :],
                    op0=ALU.mult, op1=ALU.mult))
                bank.free = a2
                yield from split(full, f_H[0][:, m, :], f_L[0][:, m, :], a2, f_read, into=halves[m])

            def mlp_down(b, slot, halves, got, h2_before, lasts_before, summed_before, stored_before,
                         h1_read, h2_read, lasts, summed, stored):
                mids = [(Event(), Event()) for _ in range(KF)]

                def gelu_split(m, bank, md, s_row, hi, lo, full_free, parts_free, into):
                    full = mid_full[:, m % 2, :]
                    yield from at(ACTE, md, *full_free, table=ACT.Gelu)
                    a = ACTE.done(nc.scalar.activation(full, bank.t[:, :], ACT.Gelu, scale=sc_in[:, s_row, m:m + 1]))
                    bank.free = a
                    yield from split(full, hi, lo, a, parts_free, into=into)

                for m in range(KF):
                    bank = yield from at(PE, ring=ring_mid, laid=of_all(halves))
                    md = ternary(bank, h1, m, f_H[0], f_L[0], KF, halves, into=h1_read if m == KF - 1 else None)
                    yield from start(gelu_split(m, bank, md, 2, f_H[1][:, m, :], f_L[1][:, m, :],
                                                two_before(mids, m, lasts_before), h2_before, mids[m]))

                def sum_tiles():
                    outs = []
                    while len(outs) < TT // 2:
                        outs.append((yield from at(PE, *lasts[0], ring=ring_sums)))
                    for m in range(KF):
                        yield from at(PE, *lasts[m])
                        for t in range(TT):
                            for n, a in enumerate((last_H, last_L)):
                                i = nc.tensor.matmul(outs[t // 2].t[:, (t % 2) * D:(t % 2 + 1) * D],
                                                     a[:, m % 2, t * P:(t + 1) * P], w3[:, m, :],
                                                     start=(m == 0 and t % 2 == 0 and n == 0),
                                                     stop=(m == KF - 1 and n == 1), skip_group_check=True)
                        PE.done(i, 4 * PASS, into=summed[m])
                    for n, bank in enumerate(outs):
                        tp, xp = pair_of(tokM, n), pair_of(xres[slot], n)
                        yield from at(DVE, summed[-1], got, stored_before)
                        a = DVE.done(nc.vector.tensor_tensor(tp, bank_pair(bank), s3_row[:, None, :].broadcast_to([P, 2, D]), ALU.mult))
                        bank.free = a
                        yield from at(DVE, a)
                        a = DVE.done(nc.vector.tensor_tensor(tp, tp, gbM[slot][:, None, :].broadcast_to([P, 2, D]), ALU.mult))
                        yield from at(DVE, a)
                        a = DVE.done(nc.vector.tensor_tensor(xp, xp, tp, ALU.add))
                    yield from at(SP, a)
                    dma(f"M_store{slot}", out_v[b], xres[slot][:, :, :], into=stored)

                yield from start(sum_tiles())
                for m in range(KF):
                    bank = yield from at(PE, ring=ring_mid, laid=of_all(mids))
                    md = ternary(bank, h2, m, f_H[1], f_L[1], KF, mids, into=h2_read if m == KF - 1 else None)
                    yield from start(gelu_split(m, bank, md, 3, last_H[:, m % 2, :], last_L[:, m % 2, :],
                                                two_before(lasts, m, mids), two_before(summed, m, summed_before), lasts[m]))

            def mlp(downs, ups, *beside, w2_got=()):
                state = {key: [carried("M." + key) or [None] * size] for key, size in LEFT.items()}

                def new(*keys):
                    for key in keys:
                        state[key].append([Event() for _ in range(LEFT[key])])

                def now(key):
                    return state[key][-1]

                def before(key):
                    return state[key][-2]

                stages = []
                for n in range(max(len(downs), len(ups))):
                    if n < len(downs):
                        new("h1_read", "h2_read", "lasts", "summed", "stored")
                        stages.append(mlp_down(*downs[n], pairs(now("halves")), *now("got"), *before("h2_read"),
                                               pairs(before("lasts")), before("summed"), *before("stored"),
                                               *now("h1_read"), *now("h2_read"), pairs(now("lasts")), now("summed"), *now("stored")))
                    if n < len(ups):
                        new("front", "halves", "got", "up_read")
                        stages.append(mlp_up(*ups[n], before("stored")[0] if downs else None, before("front"),
                                             pairs(before("halves")), *before("up_read"), *now("h1_read"),
                                             now("front"), *now("got"), pairs(now("halves")), *now("up_read"), w2_got))
                interleave(*stages, *beside)
                for key in LEFT:
                    if now(key)[0] is not None:
                        ended["M." + key] = now(key)

            LEFT = {"front": 3 * KD, "halves": 2 * KF, "got": 1, "up_read": 1, "h1_read": 1, "h2_read": 1,
                    "lasts": 2 * KF, "summed": KF, "stored": 1}

            def pairs(events):
                return list(zip(events[::2], events[1::2]))

            w2_got = [Event() for _ in range(KD)]

            def last_mlp_weights():
                for got, event in zip((yield from rounded([("w2_T", w2)], [mid_full, tokM])), w2_got):
                    copy_event(got, event)
                yield from at(DVE, *w2_got)
                yield from at(ACTE, *w2_got)
                yield from at(SP, *w2_got)
                yield from rounded([("h2_T", h2)], [mid_full, tokM, xres[1]])

            mlp([], [(0, 0)], last_mlp_weights(), w2_got=w2_got)
            turns("mlp", B // 2 - 1, lambda turn: mlp([(turn * 2, 0), (turn * 2 + 1, 1)], [(turn * 2 + 1, 1), (turn * 2 + 2, 0)]))
            mlp([(B - 2, 0), (B - 1, 1)], [(B - 1, 1)])
            join()


TURNED = {"router_T": "L0_ffn_router_w", "w1_T": "L1_ffn_w1_w", "w2_T": "L1_ffn_w2_w",
          "h1_T": "L1_ffn_h1_w", "h2_T": "L1_ffn_h2_w", "w3_T": "L1_ffn_w3_w"}


PER_FEATURE = ["L0_attn_ln_g", "L0_attn_ln_b", "L0_attn_b_hidden", "L1_attn_conv_w", "L1_attn_conv_b",
               "L1_attn_b_dt", "L1_attn_D", "L1_ffn_w1_s", "L1_ffn_w2_s", "L1_ffn_h1_s", "L1_ffn_h2_s"]


def kernel(**inputs):
    import numpy as np
    import concourse.bacc as bacc
    from concourse.bass_utils import run_bass_kernel_spmd

    arrays = {}
    turned_names = set(TURNED.values())
    for name, a in inputs.items():
        if name not in turned_names:
            arrays[name] = np.ascontiguousarray(a)
    for short, name in TURNED.items():
        arrays[short] = np.ascontiguousarray(np.asarray(inputs[name]).T)
    for name in PER_FEATURE:
        a = np.asarray(inputs[name])
        tiles = a.reshape(*[n for n in a.shape[:-1] if n > 1], -1, P)
        arrays[name] = np.ascontiguousarray(np.moveaxis(tiles, -1, 0))
    arrays["os_rows"] = np.ascontiguousarray(
        np.stack([inputs["L0_attn_os_gamma"], inputs["L0_attn_os_beta"]], axis=1))

    def program(counts):
        nc = bacc.Bacc("TRN2", target_bir_lowering=False, num_devices=1)
        aps = {name: nc.dram_tensor(name, a.shape, mybir.dt.from_np(a.dtype), kind="ExternalInput").ap()
               for name, a in arrays.items()}
        out = nc.dram_tensor("x_out", inputs["L0_attn_x"].shape, F32, kind="ExternalOutput").ap()
        adaln_kernel(nc, aps, out, counts)
        return nc

    counts = {}
    program(counts)
    nc = program(counts)
    result = run_bass_kernel_spmd(nc, [arrays], core_ids=[0])
    return result.results[0]["x_out"]
```
